# Optimizing a Trainium2 kernel written in Bass

```python
import numpy as np
import jax
import jax.numpy as jnp

def _softmax(x, axis=-1):
    return jax.nn.softmax(x, axis=axis)

def _gelu(x):
    return jax.nn.gelu(x, approximate=True)

def _silu(x):
    return jax.nn.silu(x)

def _sigmoid(x):
    return jax.nn.sigmoid(x)

def _layernorm(x, axis=-1, eps=1e-05):
    m = jnp.mean(x, axis=axis, keepdims=True)
    v = jnp.var(x, axis=axis, keepdims=True)
    return (x - m) / jnp.sqrt(v + eps)

def _scatter_add(tgt, idx, src, axis=0):
    return tgt.at[idx].add(src)

def _segment_sum(src, seg, n):
    return jax.ops.segment_sum(src, seg, n)
kernel_name = 'mk_hybrid_d2_jaxref_r8_658dff'

def setup_inputs(seed: int=0):
    np.random.seed(seed)
    _w = jnp.asarray

    def _L0_attn_a_setup():
        import jax, jax.numpy as jnp
        import numpy as np
        RMS_EPS = 1e-05

        def _l2norm(t):
            return t / jnp.linalg.norm(t, axis=-1, keepdims=True)

        def _delta_rule(q, k, v, beta):
            B, H, N, Dk = q.shape
            Dv = v.shape[-1]
            qT = jnp.moveaxis(q, 2, 0)
            kT = jnp.moveaxis(k, 2, 0)
            vT = jnp.moveaxis(v, 2, 0)
            bT = jnp.moveaxis(beta, 2, 0)

            def step(S, inp):
                q_t, k_t, v_t, b_t = inp
                pred = jnp.einsum('bhk,bhkv->bhv', k_t, S)
                err = (v_t - pred) * b_t[..., None]
                S = S + jnp.einsum('bhk,bhv->bhkv', k_t, err)
                o_t = jnp.einsum('bhk,bhkv->bhv', q_t, S)
                return (S, o_t)
            S0 = jnp.zeros((B, H, Dk, Dv), q.dtype)
            _, oT = jax.lax.scan(step, S0, (qT, kT, vT, bT))
            return jnp.moveaxis(oT, 0, 2)
        key = jax.random.key(seed)
        ks = jax.random.split(key, 7)
        B, N, D, H = (8, 128, 128, 4)
        Dv = D // H
        s = lambda k, shp, fan: jax.random.normal(k, shp, jnp.float32) * (1.0 / np.sqrt(fan))
        return {'x': jax.random.normal(ks[0], (B, N, D), jnp.float32), 'Wq': s(ks[1], (D, D), D), 'Wk': s(ks[2], (D, D), D), 'Wv': s(ks[3], (D, D), D), 'Wbeta': s(ks[4], (D, H), D), 'Wo': s(ks[5], (D, D), D), 'g_norm': jnp.ones((Dv,), jnp.float32)}
    _L0_attn_a_in = _L0_attn_a_setup()

    def _L0_attn_b_setup():
        import math
        import jax, jax.numpy as jnp
        import numpy as np
        D_MODEL = 128
        D_STATE = 64
        BATCH = 8
        SEQLEN = 256

        def _reference_tuple_inner(x, log_Lam_real, Lam_imag, B_real, B_imag, C_real, C_imag, D, log_dt, W_out, b_out):
            B, L, H = x.shape
            N = log_Lam_real.shape[0]
            dt = jnp.exp(log_dt)
            Lam_r = -jnp.exp(log_Lam_real)
            mag = jnp.exp(Lam_r * dt)
            Lbar_r = mag * jnp.cos(Lam_imag * dt)
            Lbar_i = mag * jnp.sin(Lam_imag * dt)
            Bu_r = jnp.einsum('blh,nh->bln', x, dt * B_real)
            Bu_i = jnp.einsum('blh,nh->bln', x, dt * B_imag)

            def step(carry, bu):
                sr, si = carry
                bur, bui = bu
                nr = Lbar_r * sr - Lbar_i * si + bur
                ni = Lbar_r * si + Lbar_i * sr + bui
                return ((nr, ni), (nr, ni))
            sr0 = jnp.zeros((B, N), dtype=x.dtype)
            si0 = jnp.zeros((B, N), dtype=x.dtype)
            (sr, si), (SR, SI) = jax.lax.scan(step, (sr0, si0), (jnp.swapaxes(Bu_r, 0, 1), jnp.swapaxes(Bu_i, 0, 1)))
            y = jnp.einsum('lbn,hn->blh', SR, C_real) - jnp.einsum('lbn,hn->blh', SI, C_imag) + D * x
            out = y @ W_out.T + b_out
            return (out, (sr, si))
        key = jax.random.key(seed)
        ks = jax.random.split(key, 8)
        x = jax.random.normal(ks[0], (BATCH, SEQLEN, D_MODEL), dtype=jnp.float32)
        log_Lam_real = jnp.log(0.5 * jnp.ones((D_STATE,), dtype=jnp.float32))
        Lam_imag = math.pi * jnp.arange(D_STATE, dtype=jnp.float32)
        B_real = 0.02 * jax.random.normal(ks[1], (D_STATE, D_MODEL), dtype=jnp.float32)
        B_imag = 0.02 * jax.random.normal(ks[2], (D_STATE, D_MODEL), dtype=jnp.float32)
        C_real = 0.02 * jax.random.normal(ks[3], (D_MODEL, D_STATE), dtype=jnp.float32)
        C_imag = 0.02 * jax.random.normal(ks[4], (D_MODEL, D_STATE), dtype=jnp.float32)
        Dp = jnp.ones((D_MODEL,), dtype=jnp.float32)
        log_dt = jnp.zeros((1,), dtype=jnp.float32)
        W_out = 0.02 * jax.random.normal(ks[5], (D_MODEL, D_MODEL), dtype=jnp.float32)
        b_out = jnp.zeros((D_MODEL,), dtype=jnp.float32)
        return {'x': x, 'log_Lam_real': log_Lam_real, 'Lam_imag': Lam_imag, 'B_real': B_real, 'B_imag': B_imag, 'C_real': C_real, 'C_imag': C_imag, 'D': Dp, 'log_dt': log_dt, 'W_out': W_out, 'b_out': b_out}
    _L0_attn_b_in = _L0_attn_b_setup()

    def _L0_ffn_setup():
        import jax, jax.numpy as jnp
        import numpy as np
        DIM = 128
        DEPTH = 2
        HEADS = 8
        DIM_HEAD = 64
        WINDOW = 64
        INNER = HEADS * DIM_HEAD
        HID = int(DIM * 4 * 2 / 3)
        B, N = (2, 1024)
        QK_SCALE = 8.0

        def shift_token(t):
            t1, t2 = jnp.split(t, 2, axis=-1)
            t2 = jnp.pad(t2, ((0, 0), (1, 0), (0, 0)))[:, :-1]
            return jnp.concatenate([t1, t2], axis=-1)

        def l2norm(t):
            return t / jnp.clip(jnp.linalg.norm(t, axis=-1, keepdims=True), 1e-12)

        def rotate_half(x):
            x1, x2 = jnp.split(x, 2, axis=-1)
            return jnp.concatenate([-x2, x1], axis=-1)

        def rotary_xpos(q, k):
            n = q.shape[-2]
            half_idx = jnp.arange(0, DIM_HEAD, 2, dtype=jnp.float32)
            inv_freq = 1.0 / 10000.0 ** (half_idx / DIM_HEAD)
            t = jnp.arange(n, dtype=jnp.float32)
            freqs = t[:, None] * inv_freq[None, :]
            freqs = jnp.concatenate([freqs, freqs], axis=-1)
            base = (half_idx + 0.4 * DIM_HEAD) / (1.4 * DIM_HEAD)
            power = (t - n // 2) / float(WINDOW // 2)
            scale = base[None, :] ** power[:, None]
            scale = jnp.concatenate([scale, scale], axis=-1)
            cos, sin = (jnp.cos(freqs), jnp.sin(freqs))
            q = q * cos * scale + rotate_half(q) * sin * scale
            k = k * cos / scale + rotate_half(k) * sin / scale
            return (q, k)

        def local_attention(q, k, v):
            b, h, n, d = q.shape
            w = n // WINDOW
            bq = q.reshape(b, h, w, WINDOW, d) * QK_SCALE
            bk = k.reshape(b, h, w, WINDOW, d)
            bv = v.reshape(b, h, w, WINDOW, d)

            def look_around(t):
                p = jnp.pad(t, ((0, 0), (0, 0), (1, 0), (0, 0), (0, 0)))
                return jnp.concatenate([p[:, :, :w], p[:, :, 1:]], axis=3)
            bk, bv = (look_around(bk), look_around(bv))
            bt = jnp.arange(n).reshape(w, WINDOW)
            btp = jnp.pad(bt, ((1, 0), (0, 0)), constant_values=-1)
            btk = jnp.concatenate([btp[:w], btp[1:]], axis=1)
            sim = jnp.einsum('bhwid,bhwjd->bhwij', bq, bk)
            i = bt[:, :, None]
            j = btk[:, None, :]
            mask = (i < j) | (i > j + WINDOW) | (j == -1)
            sim = jnp.where(mask, -jnp.finfo(sim.dtype).max, sim)
            attn = jax.nn.softmax(sim, axis=-1)
            out = jnp.einsum('bhwij,bhwjd->bhwid', attn, bv)
            return out.reshape(b, h, n, d)

        def _layer(x, wqkv, qs, ksc, wo, lg, lb, w1, b1, w2, b2):
            b, n, _ = x.shape
            h = shift_token(x)
            qkv = h @ wqkv
            q, k, v = jnp.split(qkv, 3, axis=-1)
            to_heads = lambda t: t.reshape(b, n, HEADS, DIM_HEAD).transpose(0, 2, 1, 3)
            q, k, v = (to_heads(q), to_heads(k), to_heads(v))
            q = l2norm(q) * qs
            k = l2norm(k) * ksc
            q, k = rotary_xpos(q, k)
            o = local_attention(q, k, v)
            o = o.transpose(0, 2, 1, 3).reshape(b, n, INNER)
            x = x + o @ wo
            h = shift_token(x)
            mu = h.mean(-1, keepdims=True)
            var = h.var(-1, keepdims=True)
            h = (h - mu) / jnp.sqrt(var + 1e-05) * lg + lb
            h = h @ w1 + b1
            a, g = jnp.split(h, 2, axis=-1)
            h = a * jax.nn.gelu(g, approximate=False)
            x = x + h @ w2 + b2
            return x
        key = jax.random.key(seed)
        ks = jax.random.split(key, 6)
        return {'x': jax.random.normal(ks[0], (B, N, DIM), jnp.float32), 'wqkv': jax.random.normal(ks[1], (DEPTH, DIM, 3 * INNER), jnp.float32) * 0.02, 'q_scale': jnp.ones((DEPTH, DIM_HEAD), jnp.float32), 'k_scale': jnp.ones((DEPTH, DIM_HEAD), jnp.float32), 'wo': jax.random.normal(ks[2], (DEPTH, INNER, DIM), jnp.float32) * 0.02, 'ln_g': jnp.ones((DEPTH, DIM), jnp.float32), 'ln_b': jnp.zeros((DEPTH, DIM), jnp.float32), 'w1': jax.random.normal(ks[3], (DEPTH, DIM, 2 * HID), jnp.float32) * 0.02, 'b1': jnp.zeros((DEPTH, 2 * HID), jnp.float32), 'w2': jax.random.normal(ks[4], (DEPTH, HID, DIM), jnp.float32) * 0.02, 'b2': jnp.zeros((DEPTH, DIM), jnp.float32)}
    _L0_ffn_in = _L0_ffn_setup()

    def _L1_attn_a_setup():
        import jax, jax.numpy as jnp
        import numpy as np
        from math import sqrt
        EMBED_DIM = 128
        NUM_HEADS = 16
        HEAD_DIM = EMBED_DIM // NUM_HEADS
        CAUSAL = True
        key = jax.random.key(seed)
        ks = jax.random.split(key, 5)
        B, S, E = (2, 256, EMBED_DIM)
        x = jax.random.normal(ks[0], (B, S, E), dtype=jnp.float32)
        scale = 1.0 / sqrt(E)
        Wq = jax.random.normal(ks[1], (E, E), dtype=jnp.float32) * scale
        Wk = jax.random.normal(ks[2], (E, E), dtype=jnp.float32) * scale
        Wv = jax.random.normal(ks[3], (E, E), dtype=jnp.float32) * scale
        Wo = jax.random.normal(ks[4], (E, E), dtype=jnp.float32) * scale
        return {'x': x, 'Wq': Wq, 'Wk': Wk, 'Wv': Wv, 'Wo': Wo}
    _L1_attn_a_in = _L1_attn_a_setup()

    def _L1_attn_b_setup():
        import jax, jax.numpy as jnp
        import numpy as np
        D = 128
        M = 16
        H = D // M
        EPS = 1e-05

        def _rmsnorm(x, w, eps=EPS):
            var = jnp.mean(jnp.square(x), axis=-1, keepdims=True)
            return x * jax.lax.rsqrt(var + eps) * w
        key = jax.random.key(seed)
        ks = jax.random.split(key, 5)
        B, T = (4, 128)
        x = jax.random.normal(ks[0], (B, T, D), dtype=jnp.float32)
        norm_w = jnp.ones((D,), dtype=jnp.float32)
        s = 1.0 / np.sqrt(D)
        W_v = jax.random.uniform(ks[1], (D, D), dtype=jnp.float32, minval=-s, maxval=s)
        W_a = jax.random.uniform(ks[2], (H * M * (M + 1), D), dtype=jnp.float32, minval=-s, maxval=s)
        W_out = jax.random.uniform(ks[3], (D, D), dtype=jnp.float32, minval=-s, maxval=s)
        return {'x': x, 'norm_w': norm_w, 'W_v': W_v, 'W_a': W_a, 'W_out': W_out}
    _L1_attn_b_in = _L1_attn_b_setup()

    def _L1_ffn_setup():
        import jax, jax.numpy as jnp
        import numpy as np
        NUM_HEAVY = 128
        N_ITERS = 50
        FETCH_K_RATIO = 9.0 / 8.0
        EPS = 1.0

        def rmsnorm(x, gamma):
            scale = gamma.shape[0] ** 0.5
            normed = x / jnp.maximum(jnp.linalg.norm(x, axis=-1, keepdims=True), 1e-12)
            return normed * scale * gamma

        def feedforward(x, gamma, w1, b1, w2, b2):
            h = rmsnorm(x, gamma)
            h = jax.nn.gelu(h @ w1.T + b1, approximate=False)
            return h @ w2.T + b2

        def coor_descent(s, n_iters, k, eps):
            logk = jnp.log(jnp.asarray(k, s.dtype))
            a0 = jnp.zeros_like(s[..., :1])
            b0 = -s

            def body(carry, _):
                a, b = carry
                a = eps * (logk - jax.nn.logsumexp((s + b) / eps, axis=-1, keepdims=True))
                b = -jax.nn.relu(s + a)
                return ((a, b), None)
            (a, b), _ = jax.lax.scan(body, (a0, b0), None, length=n_iters)
            return jnp.exp((s + a + b) / eps)
        key = jax.random.key(seed)
        ks = jax.random.split(key, 12)
        b, n, dim = (8, 1024, 128)
        d_light, d_heavy = (int(dim * 0.5), dim * 4)

        def lin(k, dout, din):
            bound = 1.0 / np.sqrt(din)
            k1, k2 = jax.random.split(k)
            w = jax.random.uniform(k1, (dout, din), jnp.float32, -bound, bound)
            bb = jax.random.uniform(k2, (dout,), jnp.float32, -bound, bound)
            return (w, bb)
        x = jax.random.normal(ks[0], (b, n, dim), jnp.float32)
        routing_token = jax.random.normal(ks[1], (dim,), jnp.float32)
        w1_l, b1_l = lin(ks[2], d_light, dim)
        w2_l, b2_l = lin(ks[3], dim, d_light)
        w1_h, b1_h = lin(ks[4], d_heavy, dim)
        w2_h, b2_h = lin(ks[5], dim, d_heavy)
        return dict(x=x, routing_token=routing_token, gamma_l=jnp.ones((dim,), jnp.float32), w1_l=w1_l, b1_l=b1_l, w2_l=w2_l, b2_l=b2_l, gamma_h=jnp.ones((dim,), jnp.float32), w1_h=w1_h, b1_h=b1_h, w2_h=w2_h, b2_h=b2_h)
    _L1_ffn_in = _L1_ffn_setup()
    _d = {'L0_attn_a_x': _L0_attn_a_in['x'], 'L0_attn_a_Wq': _L0_attn_a_in['Wq'], 'L0_attn_a_Wk': _L0_attn_a_in['Wk'], 'L0_attn_a_Wv': _L0_attn_a_in['Wv'], 'L0_attn_a_Wbeta': _L0_attn_a_in['Wbeta'], 'L0_attn_a_Wo': _L0_attn_a_in['Wo'], 'L0_attn_a_g_norm': _L0_attn_a_in['g_norm'], 'L0_attn_b_log_Lam_real': _L0_attn_b_in['log_Lam_real'], 'L0_attn_b_Lam_imag': _L0_attn_b_in['Lam_imag'], 'L0_attn_b_B_real': _L0_attn_b_in['B_real'], 'L0_attn_b_B_imag': _L0_attn_b_in['B_imag'], 'L0_attn_b_C_real': _L0_attn_b_in['C_real'], 'L0_attn_b_C_imag': _L0_attn_b_in['C_imag'], 'L0_attn_b_D': _L0_attn_b_in['D'], 'L0_attn_b_log_dt': _L0_attn_b_in['log_dt'], 'L0_attn_b_W_out': _L0_attn_b_in['W_out'], 'L0_attn_b_b_out': _L0_attn_b_in['b_out'], 'L0_ffn_wqkv': _L0_ffn_in['wqkv'], 'L0_ffn_q_scale': _L0_ffn_in['q_scale'], 'L0_ffn_k_scale': _L0_ffn_in['k_scale'], 'L0_ffn_wo': _L0_ffn_in['wo'], 'L0_ffn_ln_g': _L0_ffn_in['ln_g'], 'L0_ffn_ln_b': _L0_ffn_in['ln_b'], 'L0_ffn_w1': _L0_ffn_in['w1'], 'L0_ffn_b1': _L0_ffn_in['b1'], 'L0_ffn_w2': _L0_ffn_in['w2'], 'L0_ffn_b2': _L0_ffn_in['b2'], 'L1_attn_a_Wq': _L1_attn_a_in['Wq'], 'L1_attn_a_Wk': _L1_attn_a_in['Wk'], 'L1_attn_a_Wv': _L1_attn_a_in['Wv'], 'L1_attn_a_Wo': _L1_attn_a_in['Wo'], 'L1_attn_b_norm_w': _L1_attn_b_in['norm_w'], 'L1_attn_b_W_v': _L1_attn_b_in['W_v'], 'L1_attn_b_W_a': _L1_attn_b_in['W_a'], 'L1_attn_b_W_out': _L1_attn_b_in['W_out'], 'L1_ffn_routing_token': _L1_ffn_in['routing_token'], 'L1_ffn_gamma_l': _L1_ffn_in['gamma_l'], 'L1_ffn_w1_l': _L1_ffn_in['w1_l'], 'L1_ffn_b1_l': _L1_ffn_in['b1_l'], 'L1_ffn_w2_l': _L1_ffn_in['w2_l'], 'L1_ffn_b2_l': _L1_ffn_in['b2_l'], 'L1_ffn_gamma_h': _L1_ffn_in['gamma_h'], 'L1_ffn_w1_h': _L1_ffn_in['w1_h'], 'L1_ffn_b1_h': _L1_ffn_in['b1_h'], 'L1_ffn_w2_h': _L1_ffn_in['w2_h'], 'L1_ffn_b2_h': _L1_ffn_in['b2_h']}
    _x0 = _d['L0_attn_a_x']
    _d['L0_attn_a_x'] = jax.random.normal(jax.random.fold_in(jax.random.key(seed), 1), (8, 512, 128), dtype=_x0.dtype)
    del _x0
    return _d

def reference(L0_attn_a_x, L0_attn_a_Wq, L0_attn_a_Wk, L0_attn_a_Wv, L0_attn_a_Wbeta, L0_attn_a_Wo, L0_attn_a_g_norm, L0_attn_b_log_Lam_real, L0_attn_b_Lam_imag, L0_attn_b_B_real, L0_attn_b_B_imag, L0_attn_b_C_real, L0_attn_b_C_imag, L0_attn_b_D, L0_attn_b_log_dt, L0_attn_b_W_out, L0_attn_b_b_out, L0_ffn_wqkv, L0_ffn_q_scale, L0_ffn_k_scale, L0_ffn_wo, L0_ffn_ln_g, L0_ffn_ln_b, L0_ffn_w1, L0_ffn_b1, L0_ffn_w2, L0_ffn_b2, L1_attn_a_Wq, L1_attn_a_Wk, L1_attn_a_Wv, L1_attn_a_Wo, L1_attn_b_norm_w, L1_attn_b_W_v, L1_attn_b_W_a, L1_attn_b_W_out, L1_ffn_routing_token, L1_ffn_gamma_l, L1_ffn_w1_l, L1_ffn_b1_l, L1_ffn_w2_l, L1_ffn_b2_l, L1_ffn_gamma_h, L1_ffn_w1_h, L1_ffn_b1_h, L1_ffn_w2_h, L1_ffn_b2_h):

    def _L0_attn_a_ref(x, Wq, Wk, Wv, Wbeta, Wo, g_norm):
        import jax, jax.numpy as jnp
        import numpy as np
        RMS_EPS = 1e-05

        def _l2norm(t):
            return t / jnp.linalg.norm(t, axis=-1, keepdims=True)

        def _delta_rule(q, k, v, beta):
            B, H, N, Dk = q.shape
            Dv = v.shape[-1]
            qT = jnp.moveaxis(q, 2, 0)
            kT = jnp.moveaxis(k, 2, 0)
            vT = jnp.moveaxis(v, 2, 0)
            bT = jnp.moveaxis(beta, 2, 0)

            def step(S, inp):
                q_t, k_t, v_t, b_t = inp
                pred = jnp.einsum('bhk,bhkv->bhv', k_t, S)
                err = (v_t - pred) * b_t[..., None]
                S = S + jnp.einsum('bhk,bhv->bhkv', k_t, err)
                o_t = jnp.einsum('bhk,bhkv->bhv', q_t, S)
                return (S, o_t)
            S0 = jnp.zeros((B, H, Dk, Dv), q.dtype)
            _, oT = jax.lax.scan(step, S0, (qT, kT, vT, bT))
            return jnp.moveaxis(oT, 0, 2)
        B, N, D = x.shape
        H = Wbeta.shape[1]
        Dk = Wq.shape[1] // H
        Dv = Wv.shape[1] // H
        split = lambda t, d: t.reshape(B, N, H, d).transpose(0, 2, 1, 3)
        q = _l2norm(split(x @ Wq, Dk))
        k = _l2norm(split(x @ Wk, Dk))
        v = split(x @ Wv, Dv)
        beta = jax.nn.sigmoid(x @ Wbeta).transpose(0, 2, 1)
        o = _delta_rule(q, k, v, beta)
        o = o * jax.lax.rsqrt(jnp.mean(o * o, axis=-1, keepdims=True) + RMS_EPS) * g_norm
        o = o.transpose(0, 2, 1, 3).reshape(B, N, H * Dv)
        return o @ Wo

    def _L0_attn_b_ref(x, log_Lam_real, Lam_imag, B_real, B_imag, C_real, C_imag, D, log_dt, W_out, b_out):
        import math
        import jax, jax.numpy as jnp
        import numpy as np
        D_MODEL = 128
        D_STATE = 64
        BATCH = 8
        SEQLEN = 256

        def _reference_tuple_inner(x, log_Lam_real, Lam_imag, B_real, B_imag, C_real, C_imag, D, log_dt, W_out, b_out):
            B, L, H = x.shape
            N = log_Lam_real.shape[0]
            dt = jnp.exp(log_dt)
            Lam_r = -jnp.exp(log_Lam_real)
            mag = jnp.exp(Lam_r * dt)
            Lbar_r = mag * jnp.cos(Lam_imag * dt)
            Lbar_i = mag * jnp.sin(Lam_imag * dt)
            Bu_r = jnp.einsum('blh,nh->bln', x, dt * B_real)
            Bu_i = jnp.einsum('blh,nh->bln', x, dt * B_imag)

            def step(carry, bu):
                sr, si = carry
                bur, bui = bu
                nr = Lbar_r * sr - Lbar_i * si + bur
                ni = Lbar_r * si + Lbar_i * sr + bui
                return ((nr, ni), (nr, ni))
            sr0 = jnp.zeros((B, N), dtype=x.dtype)
            si0 = jnp.zeros((B, N), dtype=x.dtype)
            (sr, si), (SR, SI) = jax.lax.scan(step, (sr0, si0), (jnp.swapaxes(Bu_r, 0, 1), jnp.swapaxes(Bu_i, 0, 1)))
            y = jnp.einsum('lbn,hn->blh', SR, C_real) - jnp.einsum('lbn,hn->blh', SI, C_imag) + D * x
            out = y @ W_out.T + b_out
            return (out, (sr, si))
        return _reference_tuple_inner(x, log_Lam_real, Lam_imag, B_real, B_imag, C_real, C_imag, D, log_dt, W_out, b_out)[0]

    def _L0_ffn_ref(x, wqkv, q_scale, k_scale, wo, ln_g, ln_b, w1, b1, w2, b2):
        import jax, jax.numpy as jnp
        import numpy as np
        DIM = 128
        DEPTH = 2
        HEADS = 8
        DIM_HEAD = 64
        WINDOW = 64
        INNER = HEADS * DIM_HEAD
        HID = int(DIM * 4 * 2 / 3)
        B, N = (2, 1024)
        QK_SCALE = 8.0

        def shift_token(t):
            t1, t2 = jnp.split(t, 2, axis=-1)
            t2 = jnp.pad(t2, ((0, 0), (1, 0), (0, 0)))[:, :-1]
            return jnp.concatenate([t1, t2], axis=-1)

        def l2norm(t):
            return t / jnp.clip(jnp.linalg.norm(t, axis=-1, keepdims=True), 1e-12)

        def rotate_half(x):
            x1, x2 = jnp.split(x, 2, axis=-1)
            return jnp.concatenate([-x2, x1], axis=-1)

        def rotary_xpos(q, k):
            n = q.shape[-2]
            half_idx = jnp.arange(0, DIM_HEAD, 2, dtype=jnp.float32)
            inv_freq = 1.0 / 10000.0 ** (half_idx / DIM_HEAD)
            t = jnp.arange(n, dtype=jnp.float32)
            freqs = t[:, None] * inv_freq[None, :]
            freqs = jnp.concatenate([freqs, freqs], axis=-1)
            base = (half_idx + 0.4 * DIM_HEAD) / (1.4 * DIM_HEAD)
            power = (t - n // 2) / float(WINDOW // 2)
            scale = base[None, :] ** power[:, None]
            scale = jnp.concatenate([scale, scale], axis=-1)
            cos, sin = (jnp.cos(freqs), jnp.sin(freqs))
            q = q * cos * scale + rotate_half(q) * sin * scale
            k = k * cos / scale + rotate_half(k) * sin / scale
            return (q, k)

        def local_attention(q, k, v):
            b, h, n, d = q.shape
            w = n // WINDOW
            bq = q.reshape(b, h, w, WINDOW, d) * QK_SCALE
            bk = k.reshape(b, h, w, WINDOW, d)
            bv = v.reshape(b, h, w, WINDOW, d)

            def look_around(t):
                p = jnp.pad(t, ((0, 0), (0, 0), (1, 0), (0, 0), (0, 0)))
                return jnp.concatenate([p[:, :, :w], p[:, :, 1:]], axis=3)
            bk, bv = (look_around(bk), look_around(bv))
            bt = jnp.arange(n).reshape(w, WINDOW)
            btp = jnp.pad(bt, ((1, 0), (0, 0)), constant_values=-1)
            btk = jnp.concatenate([btp[:w], btp[1:]], axis=1)
            sim = jnp.einsum('bhwid,bhwjd->bhwij', bq, bk)
            i = bt[:, :, None]
            j = btk[:, None, :]
            mask = (i < j) | (i > j + WINDOW) | (j == -1)
            sim = jnp.where(mask, -jnp.finfo(sim.dtype).max, sim)
            attn = jax.nn.softmax(sim, axis=-1)
            out = jnp.einsum('bhwij,bhwjd->bhwid', attn, bv)
            return out.reshape(b, h, n, d)

        def _layer(x, wqkv, qs, ksc, wo, lg, lb, w1, b1, w2, b2):
            b, n, _ = x.shape
            h = shift_token(x)
            qkv = h @ wqkv
            q, k, v = jnp.split(qkv, 3, axis=-1)
            to_heads = lambda t: t.reshape(b, n, HEADS, DIM_HEAD).transpose(0, 2, 1, 3)
            q, k, v = (to_heads(q), to_heads(k), to_heads(v))
            q = l2norm(q) * qs
            k = l2norm(k) * ksc
            q, k = rotary_xpos(q, k)
            o = local_attention(q, k, v)
            o = o.transpose(0, 2, 1, 3).reshape(b, n, INNER)
            x = x + o @ wo
            h = shift_token(x)
            mu = h.mean(-1, keepdims=True)
            var = h.var(-1, keepdims=True)
            h = (h - mu) / jnp.sqrt(var + 1e-05) * lg + lb
            h = h @ w1 + b1
            a, g = jnp.split(h, 2, axis=-1)
            h = a * jax.nn.gelu(g, approximate=False)
            x = x + h @ w2 + b2
            return x
        for l in range(DEPTH):
            x = _layer(x, wqkv[l], q_scale[l], k_scale[l], wo[l], ln_g[l], ln_b[l], w1[l], b1[l], w2[l], b2[l])
        return x

    def _L1_attn_a_ref(x, Wq, Wk, Wv, Wo):
        import jax, jax.numpy as jnp
        import numpy as np
        from math import sqrt
        EMBED_DIM = 128
        NUM_HEADS = 16
        HEAD_DIM = EMBED_DIM // NUM_HEADS
        CAUSAL = True
        B, S, E = x.shape
        H, D = (NUM_HEADS, HEAD_DIM)

        def proj(W):
            y = jnp.einsum('bse,fe->bsf', x, W)
            return y.reshape(B, S, H, D).transpose(0, 2, 1, 3)
        q, k, v = (proj(Wq), proj(Wk), proj(Wv))
        scores = jnp.einsum('bhsd,bhtd->bhst', q, k)
        if CAUSAL:
            mask = jnp.triu(jnp.ones((S, S), dtype=bool), k=1)
            scores = jnp.where(mask, -jnp.inf, scores)
        attn = jax.nn.softmax(scores / sqrt(D), axis=-1)
        out = jnp.einsum('bhst,bhtd->bhsd', attn, v)
        out = out.transpose(0, 2, 1, 3).reshape(B, S, E)
        return jnp.einsum('bse,fe->bsf', out, Wo)

    def _L1_attn_b_ref(x, norm_w, W_v, W_a, W_out):
        import jax, jax.numpy as jnp
        import numpy as np
        D = 128
        M = 16
        H = D // M
        EPS = 1e-05

        def _rmsnorm(x, w, eps=EPS):
            var = jnp.mean(jnp.square(x), axis=-1, keepdims=True)
            return x * jax.lax.rsqrt(var + eps) * w
        B, T, _ = x.shape
        h = _rmsnorm(x, norm_w)
        v = (h @ W_v.T).reshape(B, T, H, M)
        gate_logits = (h @ W_a.T).reshape(B, T, H, M, M + 1)
        gates = jax.nn.softmax(gate_logits, axis=-1)
        a0 = gates[..., 0]
        A = gates[..., 1:]
        A_t = jnp.moveaxis(A, 1, 0)
        u_t = jnp.moveaxis(a0 * v, 1, 0)

        def step(state, inp):
            At, ut = inp
            new = jnp.einsum('bhij,bhj->bhi', At, state) + ut
            return (new, new)
        init = jnp.zeros((B, H, M), dtype=x.dtype)
        _, ys = jax.lax.scan(step, init, (A_t, u_t))
        h_out = jnp.moveaxis(ys, 0, 1).reshape(B, T, D)
        return x + h_out @ W_out.T

    def _L1_ffn_ref(x, routing_token, gamma_l, w1_l, b1_l, w2_l, b2_l, gamma_h, w1_h, b1_h, w2_h, b2_h):
        import jax, jax.numpy as jnp
        import numpy as np
        NUM_HEAVY = 128
        N_ITERS = 50
        FETCH_K_RATIO = 9.0 / 8.0
        EPS = 1.0

        def rmsnorm(x, gamma):
            scale = gamma.shape[0] ** 0.5
            normed = x / jnp.maximum(jnp.linalg.norm(x, axis=-1, keepdims=True), 1e-12)
            return normed * scale * gamma

        def feedforward(x, gamma, w1, b1, w2, b2):
            h = rmsnorm(x, gamma)
            h = jax.nn.gelu(h @ w1.T + b1, approximate=False)
            return h @ w2.T + b2

        def coor_descent(s, n_iters, k, eps):
            logk = jnp.log(jnp.asarray(k, s.dtype))
            a0 = jnp.zeros_like(s[..., :1])
            b0 = -s

            def body(carry, _):
                a, b = carry
                a = eps * (logk - jax.nn.logsumexp((s + b) / eps, axis=-1, keepdims=True))
                b = -jax.nn.relu(s + a)
                return ((a, b), None)
            (a, b), _ = jax.lax.scan(body, (a0, b0), None, length=n_iters)
            return jnp.exp((s + a + b) / eps)
        b, n, dim = x.shape
        light_out = feedforward(x, gamma_l, w1_l, b1_l, w2_l, b2_l)
        s = jnp.einsum('bnd,d->bn', x, routing_token)
        effective_k = min(NUM_HEAVY * FETCH_K_RATIO, n)
        scores = coor_descent(s, N_ITERS, effective_k, EPS)
        selected_scores, selected_indices = jax.lax.top_k(scores, NUM_HEAVY)
        selected_scores = selected_scores + jax.lax.stop_gradient(1.0 - selected_scores)
        routed = jnp.take_along_axis(x, selected_indices[..., None], axis=1)
        routed_out = feedforward(routed, gamma_h, w1_h, b1_h, w2_h, b2_h)
        routed_out = routed_out * selected_scores[..., None]
        batch_range = jnp.arange(b)[:, None]
        heavy_out = jnp.zeros_like(x).at[batch_range, selected_indices].set(routed_out)
        return light_out + heavy_out
    x = L0_attn_a_x
    x = x + _L0_attn_a_ref(_layernorm(x, axis=-1), L0_attn_a_Wq, L0_attn_a_Wk, L0_attn_a_Wv, L0_attn_a_Wbeta, L0_attn_a_Wo, L0_attn_a_g_norm)
    x = x + _L0_ffn_ref(_layernorm(x, axis=-1), L0_ffn_wqkv, L0_ffn_q_scale, L0_ffn_k_scale, L0_ffn_wo, L0_ffn_ln_g, L0_ffn_ln_b, L0_ffn_w1, L0_ffn_b1, L0_ffn_w2, L0_ffn_b2)
    x = x + _L0_attn_b_ref(_layernorm(x, axis=-1), L0_attn_b_log_Lam_real, L0_attn_b_Lam_imag, L0_attn_b_B_real, L0_attn_b_B_imag, L0_attn_b_C_real, L0_attn_b_C_imag, L0_attn_b_D, L0_attn_b_log_dt, L0_attn_b_W_out, L0_attn_b_b_out)
    x = x + _L0_ffn_ref(_layernorm(x, axis=-1), L0_ffn_wqkv, L0_ffn_q_scale, L0_ffn_k_scale, L0_ffn_wo, L0_ffn_ln_g, L0_ffn_ln_b, L0_ffn_w1, L0_ffn_b1, L0_ffn_w2, L0_ffn_b2)
    x = x + _L1_attn_a_ref(_layernorm(x, axis=-1), L1_attn_a_Wq, L1_attn_a_Wk, L1_attn_a_Wv, L1_attn_a_Wo)
    x = x + _L1_ffn_ref(_layernorm(x, axis=-1), L1_ffn_routing_token, L1_ffn_gamma_l, L1_ffn_w1_l, L1_ffn_b1_l, L1_ffn_w2_l, L1_ffn_b2_l, L1_ffn_gamma_h, L1_ffn_w1_h, L1_ffn_b1_h, L1_ffn_w2_h, L1_ffn_b2_h)
    x = x + _L1_attn_b_ref(_layernorm(x, axis=-1), L1_attn_b_norm_w, L1_attn_b_W_v, L1_attn_b_W_a, L1_attn_b_W_out)
    x = x + _L1_ffn_ref(_layernorm(x, axis=-1), L1_ffn_routing_token, L1_ffn_gamma_l, L1_ffn_w1_l, L1_ffn_b1_l, L1_ffn_w2_l, L1_ffn_b2_l, L1_ffn_gamma_h, L1_ffn_w1_h, L1_ffn_b1_h, L1_ffn_w2_h, L1_ffn_b2_h)
    return x

_drawn_inputs = setup_inputs


def setup_inputs(seed=0):
    import zlib

    import numpy as np

    out = dict(_drawn_inputs(seed))
    spreads = {'L0_attn_a_g_norm': (1.0, 0.2),
     'L0_attn_b_log_Lam_real': (-0.6931471824645996, 0.6),
     'L0_attn_b_D': (1.0, 0.6),
     'L0_attn_b_b_out': (0.0, 0.1),
     'L0_ffn_q_scale': (1.0, 0.6),
     'L0_ffn_k_scale': (1.0, 0.6),
     'L0_ffn_ln_g': (1.0, 0.6),
     'L0_ffn_ln_b': (0.0, 0.8),
     'L0_ffn_b1': (0.0, 0.8),
     'L0_ffn_b2': (0.0, 0.1),
     'L1_attn_b_norm_w': (1.0, 0.6),
     'L1_ffn_gamma_l': (1.0, 0.6),
     'L1_ffn_gamma_h': (1.0, 0.6)}
    factors = {'L0_attn_b_Lam_imag': 8.0,
     'L0_attn_b_B_real': 8.0,
     'L0_attn_b_B_imag': 8.0,
     'L0_attn_b_C_real': 8.0,
     'L0_attn_b_C_imag': 8.0,
     'L0_ffn_w1': 4.217,
     'L0_ffn_w2': 4.064,
     'L1_attn_b_W_v': 7.293,
     'L1_attn_b_W_a': 8.0,
     'L1_attn_b_W_out': 7.144,
     'L1_ffn_b1_l': 6.344,
     'L1_ffn_b1_h': 8.0,
     'L1_ffn_b2_h': 8.0}
    for name, (base, spread) in spreads.items():
        noise = np.random.default_rng([zlib.crc32(name.encode()), seed]).standard_normal(out[name].shape)
        drawn = base * np.exp(spread * noise) if base else spread * noise
        out[name] = jnp.asarray(drawn.astype(out[name].dtype))
    for name, factor in factors.items():
        out[name] = (out[name] * factor).astype(out[name].dtype)
    return out
```

```python
from contextlib import ExitStack

import numpy as np

import concourse.bass as bass
from concourse import mybir

F32 = mybir.dt.float32
BF16 = mybir.dt.bfloat16
I32 = mybir.dt.int32
ALU = mybir.AluOpType
ACT = mybir.ActivationFunctionType
AX = mybir.AxisListType

B = 8
N = 512
T = 128
TILES = N // T
D = 128
SLOTS = 2
PAIRS = B // SLOTS
BANKS = 8 // SLOTS

DELTA_H, DELTA_D = 4, 32
WIN_H, WIN_D, WINDOW, DEPTH = 8, 64, 64, 2
HID = 341
STATES = 64
KEEP = 128
FETCH = 144
ITERS = 50
CAUSAL_H, CAUSAL_D = 16, 8
LIGHT, HEAVY = 64, 512
SCAN_H, SCAN_M = 8, 16
CELL = SCAN_M + 1
ROWS = SCAN_H * SCAN_M
GATES = ROWS * CELL
CHUNK = 16
CHUNKS = N // CHUNK
BANK_ROWS = 30

LN_EPS = 1e-5
MASKED = -1e30
RS_IN = 2.0 ** 16
RS_OUT = 2.0 ** 8



class Steps:

    def __init__(self, sem, names, turns=PAIRS * TILES, slots=SLOTS):
        self.sem, self.names, self.turns, self.slots = sem, names, turns, slots
        self.at = 0

    def value(self, run, i, name, s):
        i = i.n if isinstance(i, Turn) else i
        per = len(self.names) * self.slots
        return i * per + (run * self.turns * per + self.names.index(name) * self.slots + s + 1)

    def tick(self, name, s):
        assert (self.names[self.at // self.slots], self.at % self.slots) == (name, s), (name, s, self.names[self.at // self.slots])
        self.at = (self.at + 1) % (len(self.names) * self.slots)
        return self.sem


class Turn:

    def __init__(self, pair, j):
        self.pair, self.j, self.n = pair, j, pair * TILES + j

    def tile(self, s):
        return self.pair * (SLOTS * TILES) + self.j + s * TILES


NORM = ["stats", "mean", "var", "nr1", "nr2", "nr3", "xn"]


def constants():
    p, f = np.arange(128)[:, None], np.arange(128)[None, :]
    same = lambda n: p // n == f // n
    masks = [p == f, p < f, p <= f, -(same(2) & (p < f)).astype(np.float32), -(same(2) & (p > f)).astype(np.float32)]
    for n in (2, 4, 8, 16):
        masks.append(same(2 * n) & (p // n < f // n))
    masks.append(p // 32 < f // 32)
    masks.append(p + 1 == f)
    masks.append((p == 127) & (f == 0))
    masks.append(same(32))
    masks = np.stack([m.astype(np.float32) for m in masks], axis=1)
    k = np.arange(WINDOW + T)[None, :] - WINDOW
    seen = (k <= p) & (p - k <= WINDOW)
    window = np.stack([np.tile(np.where(seen & ((k >= 0) | (j > 0)), 0.0, MASKED), (1, 2)) for j in range(TILES)], axis=1)
    causal = np.where(f <= p, 0.0, MASKED)
    bf16 = mybir.dt.np(BF16)
    before = (np.arange(N + 384)[None, :] < 384 + p).astype(np.float32)
    half = np.arange(0, WIN_D, 2, dtype=np.float32)
    inv_freq = (1.0 / np.float32(10000.0) ** (half / np.float32(WIN_D))).astype(np.float32)
    t = np.arange(N, dtype=np.float32)
    freqs = (t[:, None] * inv_freq[None, :]).astype(np.float32)
    base = ((half + np.float32(0.4 * WIN_D)) / np.float32(1.4 * WIN_D)).astype(np.float32)
    power = ((t - N // 2) / np.float32(WINDOW // 2)).astype(np.float32)
    scale = (base[None, :] ** power[:, None]).astype(np.float32)
    cos, sin = np.cos(freqs), np.sin(freqs)
    both = lambda lo, hi: np.concatenate([lo, hi], axis=1)
    rope = np.stack([both(8 * cos * scale, 8 * cos * scale), both(-8 * sin * scale, 8 * sin * scale),
                     both(cos / scale, cos / scale), both(-sin / scale, sin / scale)], axis=1).astype(np.float32)
    rope = rope.reshape(TILES, T, 4, WIN_D).transpose(1, 0, 2, 3)
    pick = np.zeros((B, B, 128), np.float32)
    pick[np.arange(B), np.arange(B), :] = 1.0
    keep = np.tile((np.arange(TILES) < TILES - 1).astype(np.float32), (128, 1))
    return {"masks": masks, "window_mask": window.astype(bf16), "causal_mask": causal.astype(bf16), "eye_bf16": np.eye(128).astype(bf16),
            "before": before.astype(bf16), "rope": rope, "pick": pick, "keep": keep}


M_EYE, M_STRICT, M_UPPER, M_PAIR_U, M_PAIR_L, M_OFF, M_FAR, M_SHIFT, M_LAST, M_HEADS = 0, 1, 2, 3, 4, 5, 9, 10, 11, 12


def hybrid_layers(nc, t, out):
    ctx = ExitStack()
    with ctx:
        ctx.enter_context(nc.allow_non_contiguous_dma(reason="biases and scales, a column of values each"))

        def sb(name, shape, dt=F32):
            return ctx.enter_context(nc.sbuf_tensor(name, shape, dt))

        def sem(name):
            return ctx.enter_context(nc.semaphore(name))

        x = sb("x", [128, B * TILES, D])
        hs = sb("hs", [128, B * TILES, D])
        feedT = sb("feedT", [128, B, N])
        masks = sb("masks", [128, 13, 128])
        window_mask = sb("window_mask", [128, TILES, 2 * (WINDOW + T)], BF16)
        causal_mask = sb("causal_mask", [128, 128], BF16)
        eye_bf16 = sb("eye_bf16", [128, 128], BF16)
        before = sb("before", [128, N + 384], BF16)
        pick = sb("pick", [B, B, 128])
        keep = sb("keep", [128, TILES])
        began = sb("began", [128, TILES])
        ones_row = sb("ones_row", [1, 128])
        dw = sb("dw", [128, 3 * D + DELTA_H])
        dwo = sb("dwo", [128, D])
        dg = sb("dg", [128, 1])
        wqkv = sb("wqkv", [128, DEPTH, 3 * WIN_H * WIN_D])
        wwo = sb("wwo", [128, DEPTH, 4, D])
        qk_scale = sb("qk_scale", [128, DEPTH, 4, WIN_D])
        turnt = sb("turnt", [128, DEPTH, TILES, 4, WIN_D])
        lgb = sb("lgb", [128, DEPTH, 2])
        w1 = sb("w1", [128, DEPTH, 2 * HID])
        w1b = sb("w1b", [128, DEPTH, 6])
        w2 = sb("w2", [128, DEPTH, 3, D])
        sB = sb("sB", [128, 2, 2 * STATES])
        sC = sb("sC", [128, 2, D])
        sD = sb("sD", [128, 1])
        sWo = sb("sWo", [128, D])
        sbo = sb("sbo", [1, D])
        sp_ = sb("sp_", [128, 3])
        turns = sb("turns", [128, 2, N + 1])
        cqk = sb("cqk", [128, 2, 4, 128])
        cv = sb("cv", [128, D])
        cwo = sb("cwo", [128, D])
        fw1 = sb("fw1", [128, HEAVY + 128])
        fgam = sb("fgam", [128, 2])
        fb2 = sb("fb2", [1, D])
        token = sb("token", [128, D])
        scores = sb("scores", [128, B * TILES])
        weight = sb("weight", [128, B * TILES])
        fb1 = sb("fb1", [128, 5])
        fw2 = sb("fw2", [128, 5, D])
        gwn = sb("gwn", [128, 1])
        gwv = sb("gwv", [128, D])
        gwa = sb("gwa", [128, GATES])
        gwo = sb("gwo", [128, D])
        ARENA = 8960
        delta_state = sb("delta_state", [128, SLOTS, 128])
        upper_before = sb("upper_before", [128, SLOTS, 64])
        arena = sb("arena", [128, SLOTS, ARENA])
        small = sb("small", [128, SLOTS, 256])
        P = ctx.enter_context(nc.psum_tensor("P", [128, 8, 512], F32))

        def carve(sizes):
            at, views = 0, {}
            for name, size in sizes:
                views[name] = at, size
                at += size
            assert at <= ARENA, at
            return lambda s, name: arena[:, s, views[name][0]:views[name][0] + views[name][1]]

        def bank(s, k):
            return P[:, BANKS * s + k, :]

        def heads(ap, n):
            return ap.rearrange("p (h d) -> p h d", h=n)

        def over(ap, n, size):
            return ap.unsqueeze(2).broadcast_to([128, n, size])

        def each(ap, n):
            return ap.unsqueeze(1).broadcast_to([ap.shape[0], n, ap.shape[-1]])

        eye = masks[:, M_EYE, :]
        eyeb = eye_bf16[:, :]

        loaded = {k: sem(f"loaded_{k}") for k in ("x", "tables", "delta", "window", "state", "causal", "ffn", "gates")}
        prep = sem("weights_prepared")
        tables = sem("state_tables_step")
        tables_act = sem("state_tables_sine")
        theta_ready = sem("theta_ready")
        cleared = sem("carries_cleared")
        slot_free = sem("slot_free")
        y_moved = sem("scan_output_moved")
        stored = sem("stored")

        ln_act = ["ln", "rs"]
        SV = {}
        def steps(key, names, **kw):
            SV[key] = Steps(sem(key), names, **kw)
            return SV[key]

        done_before = [0]

        def stat(s, a, n=1):
            return small[:, s, a:a + n]

        BN, MV, VAR, RS, TMP, RSTD = 0, 12, 14, 16, 18, 20
        def wait_slots(eng, base, i):
            eng.wait_ge(slot_free, (i.n if isinstance(i, Turn) else i) * SLOTS + (base + SLOTS))

        def settle(eng):
            eng.wait_ge(slot_free, 1)

        def newton(eng, v, run, i, names, get, ready):
            a, b_, c = names
            for s in range(SLOTS):
                var, guess, tmp, res = get(s)
                ready(s)
                eng.tensor_tensor(tmp, guess, guess, ALU.mult).then_inc(v.tick(a, s), 1)
            for s in range(SLOTS):
                var, guess, tmp, res = get(s)
                eng.wait_ge(v.sem, v.value(run, i, a, s))
                eng.scalar_tensor_tensor(out=tmp, in0=tmp, scalar=-0.5 * RS_IN * RS_OUT, in1=var, op0=ALU.mult,
                                         op1=ALU.mult).then_inc(v.tick(b_, s), 1)
            for s in range(SLOTS):
                var, guess, tmp, res = get(s)
                eng.wait_ge(v.sem, v.value(run, i, b_, s))
                eng.scalar_tensor_tensor(out=res, in0=tmp, scalar=1.5 * RS_OUT, in1=guess, op0=ALU.add,
                                         op1=ALU.mult).then_inc(v.tick(c, s), 1)

        def guess_scalar(eng, v, a, run, i, var_step, names, get):
            for s in range(SLOTS):
                var, guess, tmp, res = get(s)
                eng.wait_ge(v.sem, v.value(run, i, var_step, s))
                eng.activation(guess, var, ACT.Ln, scale=RS_IN).then_inc(a.tick(names[0], s), 1)
            for s in range(SLOTS):
                var, guess, tmp, res = get(s)
                eng.wait_ge(a.sem, a.value(run, i, names[0], s))
                eng.activation(guess, guess, ACT.Exp, scale=-0.5).then_inc(a.tick(names[1], s), 1)

        def norm_place(s):
            return stat(s, VAR), stat(s, RS), stat(s, TMP), stat(s, RSTD)

        def norm_vector(eng, v, a, run, i, src, dst, first=None, names=NORM, acts=("ln", "rs")):
            for s in range(SLOTS):
                if first:
                    first(s)
                parts = src(s)
                for n, part in enumerate(parts):
                    ins = eng.bn_stats(stat(s, BN + 6 * n, 6), part)
                ins.then_inc(v.tick(names[0], s), 1)
            for s in range(SLOTS):
                eng.wait_ge(v.sem, v.value(run, i, names[0], s))
                eng.memset(stat(s, 22), 0.0)
                eng.bn_aggr(stat(s, MV, 2), stat(s, BN, 6 * len(src(s)))).then_inc(v.tick(names[1], s), 1)
            for s in range(SLOTS):
                eng.wait_ge(v.sem, v.value(run, i, names[1], s))
                eng.tensor_scalar(stat(s, VAR), stat(s, MV + 1), LN_EPS, None, ALU.add).then_inc(v.tick(names[2], s), 1)
            newton(eng, v, run, i, names[3:6], norm_place,
                   lambda s: eng.wait_ge(a.sem, a.value(run, i, acts[1], s)))
            for s in range(SLOTS):
                eng.wait_ge(v.sem, v.value(run, i, names[5], s))
                for o, part in zip(dst(s), src(s)):
                    ins = eng.tensor_scalar(o, part, stat(s, MV), stat(s, RSTD), ALU.subtract, ALU.mult)
                ins.then_inc(v.tick(names[6], s), 1)

        def xb(i, s):
            return x[:, bass.ds(i.tile(s), 1), :]

        def batch(ap, i, s):
            return ap[:, bass.ds(i * SLOTS + s, 1), :]

        def turn_loop(eng, body):
            with eng.Fori(0, PAIRS) as pair:
                with eng.Fori(0, TILES) as j:
                    body(Turn(pair, j))

        def tileT(i, s):
            return feedT[:, :, :].rearrange("p b (j t) -> p (b j) t", j=TILES)[:, bass.ds(i.tile(s), 1), :]

        def pair_loop(eng, body):
            with eng.Fori(0, PAIRS) as i:
                body(i)

        stages = []
        dv = steps("delta_vector", NORM + ["ss", "one_e", "nd1", "nd2", "nd3", "beta", "qkn", "kb", "vS", "A", "pair", "X2",
                                           "X4", "X8", "X16", "X32", "R1", "R2", "R3", "oss", "ovar", "no1", "no2", "no3", "on", "S1", "S2", "S3"])
        da = steps("delta_scalar", ["ln", "rs", "xT", "sq", "lnq", "rsq", "tT", "M2", "M4", "M8", "M16", "U0", "U1", "U2", "U3", "osq",
                                    "lno", "rso", "oT"])
        dp = steps("delta_pool", ["off"])
        dt_ = steps("delta_tensor", ["xT", "proj", "tT", "kS", "grams", "AX2", "XAX2", "AX4", "XAX4", "AX8", "XAX8", "AX16", "XAX16", "U0",
                                     "AU1", "U1", "AU2", "U2", "AU3", "U3", "O", "KU", "oT", "y"])
        dcv = carve([("xn", 128), ("xT", 128), ("sq", 256), ("qk", 384), ("v", 128), ("tT", 384), ("AT", 512), ("W", 512),
                     ("X", 512), ("XT", 512), ("M", 512), ("off", 2560), ("U", 128), ("R", 128), ("osq", 128), ("on", 128), ("oT", 128)])
        Q8 = (lambda s: (stat(s, 32, 8), stat(s, 40, 8), stat(s, 48, 8), stat(s, 56, 8)))
        O4 = (lambda s: (stat(s, 72, 4), stat(s, 76, 4), stat(s, 80, 4), stat(s, 84, 4)))
        BETA = 64

        def gram(s, n):
            return P[:, BANKS * s:BANKS * s + 4, 128 * n:128 * n + 128]

        class Delta:
            loads = ("x", "tables", "delta")

            def vector(self, eng, run, base):
                def body(i):
                    wait_slots(eng, base, i)
                    norm_vector(eng, dv, da, run, i, lambda s: [xb(i, s)], lambda s: [dcv(s, "xn")])
                    for s in range(SLOTS):
                        eng.wait_ge(da.sem, da.value(run, i, "sq", s))
                        eng.tensor_reduce(Q8(s)[0], heads(dcv(s, "sq"), 8), AX.X, ALU.add).then_inc(dv.tick("ss", s), 1)
                    for s in range(SLOTS):
                        eng.tensor_scalar(stat(s, BETA, 4), stat(s, BETA, 4), 1.0, None, ALU.add).then_inc(dv.tick("one_e", s), 1)
                    newton(eng, dv, run, i, ["nd1", "nd2", "nd3"], Q8,
                           lambda s: eng.wait_ge(da.sem, da.value(run, i, "rsq", s)))
                    for s in range(SLOTS):
                        eng.wait_ge(dv.sem, dv.value(run, i, "one_e", s))
                        eng.reciprocal(stat(s, BETA, 4), stat(s, BETA, 4)).then_inc(dv.tick("beta", s), 1)
                    for s in range(SLOTS):
                        eng.wait_ge(dv.sem, dv.value(run, i, "nd3", s))
                        eng.tensor_tensor(heads(dcv(s, "qk")[:, 0:256], 8), heads(bank(s, 1)[:, 0:256], 8),
                                          over(Q8(s)[3], 8, DELTA_D), ALU.mult).then_inc(dv.tick("qkn", s), 1)
                    for s in range(SLOTS):
                        eng.wait_ge(dv.sem, dv.value(run, i, "qkn", s))
                        eng.tensor_tensor(heads(dcv(s, "v"), 4), heads(bank(s, 1)[:, 256:384], 4),
                                          over(stat(s, BETA, 4), 4, DELTA_D), ALU.mult)
                        eng.tensor_tensor(heads(dcv(s, "qk")[:, 256:384], 4), heads(dcv(s, "qk")[:, 128:256], 4),
                                          over(stat(s, BETA, 4), 4, DELTA_D), ALU.mult).then_inc(dv.tick("kb", s), 1)
                    for s in range(SLOTS):
                        eng.wait_ge(dt_.sem, dt_.value(run, i, "kS", s))
                        eng.tensor_tensor(dcv(s, "v"), dcv(s, "v"), bank(s, 0)[:, 384:512], ALU.subtract).then_inc(dv.tick("vS", s), 1)
                    for s in range(SLOTS):
                        eng.wait_ge(dt_.sem, dt_.value(run, i, "grams", s))
                        eng.tensor_tensor(heads(dcv(s, "AT"), 4), gram(s, 0), each(masks[:, M_STRICT, :], 4), ALU.mult)\
                            .then_inc(dv.tick("A", s), 1)
                    for s in range(SLOTS):
                        eng.wait_ge(dv.sem, dv.value(run, i, "A", s))
                        eng.tensor_tensor(heads(dcv(s, "W"), 4), gram(s, 1), each(masks[:, M_UPPER, :], 4), ALU.mult)
                        eng.tensor_tensor(heads(dcv(s, "X"), 4), gram(s, 2), each(masks[:, M_PAIR_L, :], 4), ALU.mult)
                        eng.tensor_tensor(heads(dcv(s, "XT"), 4), heads(dcv(s, "AT"), 4), each(masks[:, M_PAIR_U, :], 4), ALU.mult)\
                            .then_inc(dv.tick("pair", s), 1)
                    for s in range(SLOTS):
                        eng.wait_ge(dv.sem, dv.value(run, i, "pair", s))
                        eng.tensor_tensor(heads(dcv(s, "X"), 4), heads(dcv(s, "X"), 4), each(eye, 4), ALU.add)
                        eng.tensor_tensor(heads(dcv(s, "XT"), 4), heads(dcv(s, "XT"), 4), each(eye, 4), ALU.add)\
                            .then_inc(dv.tick("X2", s), 1)
                    for n, nn in ((2, 4), (4, 8), (8, 16), (16, 32)):
                        for s in range(SLOTS):
                            eng.wait_ge(dt_.sem, dt_.value(run, i, f"XAX{n}", s))
                            if nn < 32:
                                eng.tensor_tensor(dcv(s, "X"), dcv(s, "X"), bank(s, 1), ALU.subtract)
                            eng.tensor_tensor(dcv(s, "XT"), dcv(s, "XT"), bank(s, 2), ALU.subtract).then_inc(dv.tick(f"X{nn}", s), 1)
                    for n in (1, 2, 3):
                        for s in range(SLOTS):
                            eng.wait_ge(dt_.sem, dt_.value(run, i, f"AU{n}", s))
                            eng.tensor_tensor(dcv(s, "R"), dcv(s, "v"), bank(s, 3)[:, 128:256], ALU.subtract).then_inc(dv.tick(f"R{n}", s), 1)
                    for s in range(SLOTS):
                        eng.wait_ge(da.sem, da.value(run, i, "osq", s))
                        eng.tensor_reduce(O4(s)[0], heads(dcv(s, "osq"), 4), AX.X, ALU.add).then_inc(dv.tick("oss", s), 1)
                    for s in range(SLOTS):
                        eng.wait_ge(dv.sem, dv.value(run, i, "oss", s))
                        eng.tensor_scalar(O4(s)[0], O4(s)[0], 1.0 / DELTA_D, LN_EPS, ALU.mult, ALU.add).then_inc(dv.tick("ovar", s), 1)
                    newton(eng, dv, run, i, ["no1", "no2", "no3"], O4,
                           lambda s: eng.wait_ge(da.sem, da.value(run, i, "rso", s)))
                    for s in range(SLOTS):
                        eng.wait_ge(dv.sem, dv.value(run, i, "no3", s))
                        eng.tensor_tensor(heads(dcv(s, "on"), 4), heads(bank(s, 0)[:, 0:128], 4),
                                          over(O4(s)[3], 4, DELTA_D), ALU.mult).then_inc(dv.tick("on", s), 1)
                    for s in range(SLOTS):
                        eng.wait_ge(dt_.sem, dt_.value(run, i, "KU", s))
                        eng.tensor_tensor(dcv(s, "R"), bank(s, 3)[:, 256:384], masks[:, M_HEADS, :], ALU.mult).then_inc(dv.tick("S1", s), 1)
                    for s in range(SLOTS):
                        eng.wait_ge(dv.sem, dv.value(run, i, "S1", s))
                        eng.tensor_tensor(dcv(s, "R"), dcv(s, "R"), delta_state[:, s, :], ALU.add).then_inc(dv.tick("S2", s), 1)
                    for s in range(SLOTS):
                        eng.wait_ge(dv.sem, dv.value(run, i, "S2", s))
                        eng.tensor_scalar(delta_state[:, s, :], dcv(s, "R"), keep[:, bass.ds(i.j, 1)], None, ALU.mult).then_inc(dv.tick("S3", s), 1)
                    for s in range(SLOTS):
                        eng.wait_ge(dt_.sem, dt_.value(run, i, "y", s))
                        eng.tensor_tensor(xb(i, s), xb(i, s), bank(s, 2)[:, 0:128], ALU.add).then_inc(slot_free, 1)
                turn_loop(eng, body)

            def scalar(self, eng, run, base):
                def body(i):
                    wait_slots(eng, base, i)
                    guess_scalar(eng, dv, da, run, i, "var", ["ln", "rs"], norm_place)
                    for s in range(SLOTS):
                        eng.wait_ge(dt_.sem, dt_.value(run, i, "xT", s))
                        eng.activation(dcv(s, "xT"), bank(s, 0)[:, 0:128], ACT.Copy).then_inc(da.tick("xT", s), 1)
                    for s in range(SLOTS):
                        eng.wait_ge(dt_.sem, dt_.value(run, i, "proj", s))
                        eng.activation(stat(s, BETA, 4), bank(s, 1)[:, 384:388], ACT.Exp, scale=-1.0)
                        eng.activation(dcv(s, "sq"), bank(s, 1)[:, 0:256], ACT.Square).then_inc(da.tick("sq", s), 1)
                    guess_scalar(eng, dv, da, run, i, "ss", ["lnq", "rsq"], Q8)
                    for s in range(SLOTS):
                        eng.wait_ge(dt_.sem, dt_.value(run, i, "tT", s))
                        eng.activation(dcv(s, "tT"), bank(s, 0)[:, 0:384], ACT.Copy).then_inc(da.tick("tT", s), 1)
                    for n in (2, 4, 8, 16):
                        for s in range(SLOTS):
                            eng.wait_ge(dt_.sem, dt_.value(run, i, f"AX{n}", s))
                            eng.activation(dcv(s, "M"), bank(s, 0), ACT.Copy).then_inc(da.tick(f"M{n}", s), 1)
                    for n in (0, 1, 2, 3):
                        for s in range(SLOTS):
                            eng.wait_ge(dt_.sem, dt_.value(run, i, f"U{n}", s))
                            eng.activation(dcv(s, "U"), bank(s, 3)[:, 0:128], ACT.Copy).then_inc(da.tick(f"U{n}", s), 1)
                    for s in range(SLOTS):
                        eng.wait_ge(dt_.sem, dt_.value(run, i, "O", s))
                        eng.activation(dcv(s, "osq"), bank(s, 0)[:, 0:128], ACT.Square).then_inc(da.tick("osq", s), 1)
                    guess_scalar(eng, dv, da, run, i, "ovar", ["lno", "rso"], O4)
                    for s in range(SLOTS):
                        eng.wait_ge(dt_.sem, dt_.value(run, i, "oT", s))
                        eng.activation(dcv(s, "oT"), bank(s, 1)[:, 0:128], ACT.Copy).then_inc(da.tick("oT", s), 1)
                turn_loop(eng, body)

            def pool(self, eng, run, base):
                def body(i):
                    wait_slots(eng, base, i)
                    for s in range(SLOTS):
                        eng.wait_ge(dv.sem, dv.value(run, i, "A", s))
                        for n in range(5):
                            ins = eng.tensor_tensor(heads(dcv(s, "off")[:, 512 * n:512 * n + 512], 4), heads(dcv(s, "AT"), 4),
                                                    each(masks[:, M_OFF + n, :], 4), ALU.mult)
                        ins.then_inc(dp.tick("off", s), 1)
                turn_loop(eng, body)

            def tensor(self, eng, run, base):
                def per_head(out_, lhs, rhs, n=128):
                    for h in range(4):
                        ins = eng.matmul(out_[:, n * h:n * h + n], lhs(h), rhs(h), start=True, stop=True)
                    return ins

                def body(i):
                    wait_slots(eng, base, i)
                    blk = lambda ap, n=128: (lambda h: ap[:, n * h:n * h + n])
                    for s in range(SLOTS):
                        eng.wait_ge(dv.sem, dv.value(run, i, "xn", s))
                        eng.transpose(bank(s, 0)[:, 0:128], dcv(s, "xn"), eye).then_inc(dt_.tick("xT", s), 1)
                    for s in range(SLOTS):
                        eng.wait_ge(da.sem, da.value(run, i, "xT", s))
                        eng.matmul(bank(s, 1)[:, 0:388], dcv(s, "xT"), dw[:, :], start=True, stop=True).then_inc(dt_.tick("proj", s), 1)
                    for s in range(SLOTS):
                        eng.wait_ge(dv.sem, dv.value(run, i, "kb", s))
                        for n in range(3):
                            ins = eng.transpose(bank(s, 0)[:, 128 * n:128 * n + 128], dcv(s, "qk")[:, 128 * n:128 * n + 128], eye)
                        ins.then_inc(dt_.tick("tT", s), 1)
                    for s in range(SLOTS):
                        eng.wait_ge(da.sem, da.value(run, i, "tT", s))
                        eng.matmul(bank(s, 0)[:, 384:512], dcv(s, "tT")[:, 256:384], delta_state[:, s, :], start=True, stop=True).then_inc(dt_.tick("kS", s), 1)
                    for s in range(SLOTS):
                        eng.wait_ge(dv.sem, dv.value(run, i, "vS", s))
                        row = lambda n: (lambda h: dcv(s, "tT")[32 * h:32 * h + 32, 128 * n:128 * n + 128])
                        for h in range(4):
                            for n, (a, b_) in enumerate(((1, 2), (1, 0), (2, 1))):
                                ins = eng.matmul(bank(s, h)[:, 128 * n:128 * n + 128], row(a)(h), row(b_)(h), start=True, stop=True)
                        ins.then_inc(dt_.tick("grams", s), 1)
                    for n, (lvl, x_) in enumerate(((2, "X2"), (4, "X4"), (8, "X8"), (16, "X16"))):
                        for s in range(SLOTS):
                            if n == 0:
                                eng.wait_ge(dp.sem, dp.value(run, i, "off", s))
                            eng.wait_ge(dv.sem, dv.value(run, i, x_, s))
                            per_head(bank(s, 0), blk(dcv(s, "off")[:, 512 * n:512 * n + 512]), blk(dcv(s, "X"))).then_inc(dt_.tick(f"AX{lvl}", s), 1)
                        for s in range(SLOTS):
                            eng.wait_ge(da.sem, da.value(run, i, f"M{lvl}", s))
                            if lvl < 16:
                                per_head(bank(s, 1), blk(dcv(s, "XT")), blk(dcv(s, "M")))
                            per_head(bank(s, 2), blk(dcv(s, "M")), blk(dcv(s, "XT"))).then_inc(dt_.tick(f"XAX{lvl}", s), 1)
                    for s in range(SLOTS):
                        eng.wait_ge(dv.sem, dv.value(run, i, "X32", s))
                        per_head(bank(s, 3), blk(dcv(s, "XT")), blk(dcv(s, "v"), 32), 32).then_inc(dt_.tick("U0", s), 1)
                    for n in (1, 2, 3):
                        for s in range(SLOTS):
                            eng.wait_ge(da.sem, da.value(run, i, f"U{n - 1}", s))
                            per_head(bank(s, 3)[:, 128:256], blk(dcv(s, "off")[:, 2048:2560]), blk(dcv(s, "U"), 32), 32)\
                                .then_inc(dt_.tick(f"AU{n}", s), 1)
                        for s in range(SLOTS):
                            eng.wait_ge(dv.sem, dv.value(run, i, f"R{n}", s))
                            per_head(bank(s, 3), blk(dcv(s, "XT")), blk(dcv(s, "R"), 32), 32).then_inc(dt_.tick(f"U{n}", s), 1)
                    for s in range(SLOTS):
                        eng.wait_ge(da.sem, da.value(run, i, "U3", s))
                        eng.matmul(bank(s, 0)[:, 0:128], dcv(s, "tT")[:, 0:128], delta_state[:, s, :], start=True, stop=True)
                        for h in range(4):
                            ins = eng.matmul(bank(s, 0)[:, 32 * h:32 * h + 32], dcv(s, "W")[:, 128 * h:128 * h + 128], dcv(s, "U")[:, 32 * h:32 * h + 32],
                                             start=False, stop=True, skip_group_check=True)
                        ins.then_inc(dt_.tick("O", s), 1)
                    for s in range(SLOTS):
                        eng.matmul(bank(s, 3)[:, 256:384], dcv(s, "qk")[:, 128:256], dcv(s, "U"), start=True, stop=True).then_inc(dt_.tick("KU", s), 1)
                    for s in range(SLOTS):
                        eng.wait_ge(dv.sem, dv.value(run, i, "on", s))
                        eng.transpose(bank(s, 1)[:, 0:128], dcv(s, "on"), eye).then_inc(dt_.tick("oT", s), 1)
                    for s in range(SLOTS):
                        eng.wait_ge(da.sem, da.value(run, i, "oT", s))
                        eng.matmul(bank(s, 2)[:, 0:128], dcv(s, "oT"), dwo[:, :], start=True, stop=True).then_inc(dt_.tick("y", s), 1)
                turn_loop(eng, body)

        NORM2 = ["f" + n for n in NORM]
        win = {}
        for first in (False, True):
            win[first] = (
                steps(f"window{int(first)}_vector", (NORM if first else ["xn"]) + ["hT0", "hT", "ss", "vmax", "nq1", "nq2", "nq3", "kn", "qn", "q0", "q1", "q3", "qT", "max",
                                             "rz", "pT", "o", "h2"] + NORM2),
                steps(f"window{int(first)}_scalar", ["vh"] + ["ln", "rs"] * first + ["hT", "sq", "v", "lnq", "rsq", "kT", "p", "pT", "oT", "fln", "frs"]),
                steps(f"window{int(first)}_pool", ["k0", "k1", "k3"]),
                steps(f"window{int(first)}_tensor", ["hT", "qkv", "qkT", "sim", "pT", "o", "oT", "y", "shift", "gT"]))
        KEYS = WINDOW + T
        wcv = carve([("xn", 128), ("hT", T + 1), ("q", 512), ("k", 512), ("v", 512), ("vh", 512), ("t", 512), ("tk", 512),
                     ("qT", 512), ("kT", 4 * KEYS), ("p", 8 * KEYS), ("pT", 1024), ("pTh", 1024), ("h2", 128), ("g", 128)])
        wsq = lambda s: wcv(s, "p")[:, 0:1024]
        Q16 = (lambda s: (stat(s, 32, 16), stat(s, 48, 16), stat(s, 64, 16), stat(s, 80, 16)))
        MAX, Z, RZ = 96, 112, 128

        def head_place(h):
            return 2 * (h % 2) + h // 4, h // 2 % 2

        class Window:
            loads = ("tables", "window")

            def __init__(self, first, depth):
                self.first, self.depth = first, depth

            def hb(self, i, s):
                return hs[:, bass.ds(i.tile(s), 1), :]

            def vector(self, eng, run, base):
                wv_, wa, wp, wt = win[self.first]
                rope_at = lambda i, n, a, b: turnt[:, self.depth, bass.ds(i.j, 1), n, a:b].broadcast_to([128, 8, b - a])

                def body(i):
                    wait_slots(eng, base, i)
                    if self.first:
                        norm_vector(eng, wv_, wa, run, i, lambda s: [xb(i, s)], lambda s: [wcv(s, "xn")])
                    else:
                        for s in range(SLOTS):
                            eng.tensor_scalar(wcv(s, "xn"), self.hb(i, s), 1.0, None, ALU.mult).then_inc(wv_.tick("xn", s), 1)
                    for s in range(SLOTS):
                        eng.tensor_scalar(wcv(s, "hT")[64:128, 0:1], wcv(s, "hT")[64:128, T:T + 1], began[64:128, bass.ds(i.j, 1)], None, ALU.mult)\
                            .then_inc(wv_.tick("hT0", s), 1)
                    for s in range(SLOTS):
                        eng.wait_ge(wv_.sem, wv_.value(run, i, "hT0", s))
                        eng.wait_ge(wt.sem, wt.value(run, i, "hT", s))
                        eng.tensor_scalar(wcv(s, "hT")[64:128, 1:129], bank(s, 0)[64:128, 0:128], 1.0, None, ALU.mult).then_inc(wv_.tick("hT", s), 1)
                    for s in range(SLOTS):
                        eng.wait_ge(wa.sem, wa.value(run, i, "sq", s))
                        eng.tensor_reduce(Q16(s)[0], heads(wsq(s), 16), AX.X, ALU.add).then_inc(wv_.tick("ss", s), 1)
                    for s in range(SLOTS):
                        eng.wait_ge(wv_.sem, wv_.value(run, i, "ss", s))
                        eng.tensor_scalar(Q16(s)[0], Q16(s)[0], 1e-24, None, ALU.max).then_inc(wv_.tick("vmax", s), 1)
                    newton(eng, wv_, run, i, ["nq1", "nq2", "nq3"], Q16,
                           lambda s: eng.wait_ge(wa.sem, wa.value(run, i, "rsq", s)))
                    for s in range(SLOTS):
                        eng.wait_ge(wv_.sem, wv_.value(run, i, "nq3", s))
                        eng.tensor_tensor(heads(wcv(s, "k"), 8), heads(bank(s, 2), 8), over(Q16(s)[3][:, 8:16], 8, WIN_D), ALU.mult)\
                            .then_inc(wv_.tick("kn", s), 1)
                    for s in range(SLOTS):
                        eng.tensor_tensor(heads(wcv(s, "q"), 8), heads(bank(s, 1), 8), over(Q16(s)[3][:, 0:8], 8, WIN_D), ALU.mult)\
                            .then_inc(wv_.tick("qn", s), 1)
                    for s in range(SLOTS):
                        eng.wait_ge(wv_.sem, wv_.value(run, i, "qn", s))
                        q, t_ = heads(wcv(s, "q"), 8), heads(wcv(s, "t"), 8)
                        eng.tensor_tensor(t_[:, :, 0:32], q[:, :, 32:64], rope_at(i, 1, 0, 32), ALU.mult)
                        eng.tensor_tensor(t_[:, :, 32:64], q[:, :, 0:32], rope_at(i, 1, 32, 64), ALU.mult).then_inc(wv_.tick("q0", s), 1)
                    for s in range(SLOTS):
                        q = heads(wcv(s, "q"), 8)
                        eng.wait_ge(wv_.sem, wv_.value(run, i, "q0", s))
                        eng.tensor_tensor(q, q, rope_at(i, 0, 0, 64), ALU.mult).then_inc(wv_.tick("q1", s), 1)
                    for s in range(SLOTS):
                        eng.wait_ge(wv_.sem, wv_.value(run, i, "q1", s))
                        eng.tensor_tensor(wcv(s, "q"), wcv(s, "q"), wcv(s, "t"), ALU.add).then_inc(wv_.tick("q3", s), 1)
                    for s in range(SLOTS):
                        eng.wait_ge(wt.sem, wt.value(run, i, "qkT", s))
                        eng.tensor_copy(wcv(s, "qT"), bank(s, 0)).then_inc(wv_.tick("qT", s), 1)
                    for s in range(SLOTS):
                        eng.wait_ge(wt.sem, wt.value(run, i, "sim", s))
                        for n in range(4):
                            ins = eng.tensor_reduce(stat(s, MAX + 2 * n, 2), heads(bank(s, n)[:, 0:2 * KEYS], 2), AX.X, ALU.max, negate=True)
                        ins.then_inc(wv_.tick("max", s), 1)
                    for s in range(SLOTS):
                        eng.wait_ge(wa.sem, wa.value(run, i, "p", s))
                        eng.reciprocal(stat(s, RZ, 8), stat(s, Z, 8)).then_inc(wv_.tick("rz", s), 1)
                    for s in range(SLOTS):
                        eng.wait_ge(wt.sem, wt.value(run, i, "pT", s))
                        eng.tensor_copy(wcv(s, "pT")[:, 0:512], bank(s, 0))
                        eng.tensor_copy(wcv(s, "pTh")[0:64, 0:512], bank(s, 2)[0:64, :]).then_inc(wv_.tick("pT", s), 1)
                    for s in range(SLOTS):
                        eng.wait_ge(wt.sem, wt.value(run, i, "o", s))
                        eng.tensor_tensor(heads(wcv(s, "q"), 8), heads(bank(s, 0), 8), over(stat(s, RZ, 8), 8, WIN_D), ALU.mult)\
                            .then_inc(wv_.tick("o", s), 1)
                    for s in range(SLOTS):
                        eng.wait_ge(wt.sem, wt.value(run, i, "y", s))
                        eng.tensor_tensor(wcv(s, "h2"), wcv(s, "xn"), bank(s, 2)[:, 0:128], ALU.add).then_inc(wv_.tick("h2", s), 1)

                    def ready(s):
                        eng.wait_ge(wt.sem, wt.value(run, i, "shift", s))
                        eng.tensor_scalar(self.hb(i, s), wcv(s, "h2"), 1.0, None, ALU.mult)
                        eng.tensor_scalar(upper_before[:, s, :], wcv(s, "h2")[:, 64:128], keep[:, bass.ds(i.j, 1)], None, ALU.mult)
                    norm_vector(eng, wv_, wa, run, i, lambda s: [wcv(s, "h2")[:, 0:64], bank(s, 3)[:, 0:64]],
                                lambda s: [wcv(s, "g")[:, 0:64], wcv(s, "g")[:, 64:128]], first=ready, names=NORM2, acts=("fln", "frs"))
                    for s in range(SLOTS):
                        eng.wait_ge(wt.sem, wt.value(run, i, "gT", s))
                        eng.tensor_scalar(tileT(i, s), bank(s, 3)[:, 128:256], lgb[:, self.depth, 0:1],
                                          lgb[:, self.depth, 1:2], ALU.mult, ALU.add).then_inc(slot_free, 1)
                turn_loop(eng, body)

            def scalar(self, eng, run, base):
                wv_, wa, wp, wt = win[self.first]
                def body(i):
                    wait_slots(eng, base, i)
                    for s in range(SLOTS):
                        eng.activation(heads(wcv(s, "kT"), 4)[:, :, 0:WINDOW], heads(wcv(s, "kT"), 4)[:, :, T:KEYS], ACT.Copy)
                        eng.activation(wcv(s, "vh")[0:64, :], wcv(s, "v")[64:128, :], ACT.Copy).then_inc(wa.tick("vh", s), 1)
                    if self.first:
                        guess_scalar(eng, wv_, wa, run, i, "var", ["ln", "rs"], norm_place)
                    for s in range(SLOTS):
                        eng.wait_ge(wt.sem, wt.value(run, i, "hT", s))
                        eng.activation(wcv(s, "hT")[0:64, 0:T], bank(s, 0)[0:64, 0:128], ACT.Copy).then_inc(wa.tick("hT", s), 1)
                    for s in range(SLOTS):
                        eng.wait_ge(wt.sem, wt.value(run, i, "qkv", s))
                        for n in range(2):
                            ins = eng.activation(wsq(s)[:, 512 * n:512 * n + 512], bank(s, 1 + n), ACT.Square)
                        ins.then_inc(wa.tick("sq", s), 1)
                    for s in range(SLOTS):
                        eng.wait_ge(wa.sem, wa.value(run, i, "vh", s))
                        eng.activation(wcv(s, "v"), bank(s, 3), ACT.Copy).then_inc(wa.tick("v", s), 1)
                    guess_scalar(eng, wv_, wa, run, i, "vmax", ["lnq", "rsq"], Q16)
                    for s in range(SLOTS):
                        eng.wait_ge(wt.sem, wt.value(run, i, "qkT", s))
                        eng.activation(heads(wcv(s, "kT"), 4)[:, :, WINDOW:KEYS], heads(bank(s, 1), 4), ACT.Copy).then_inc(wa.tick("kT", s), 1)
                    for s in range(SLOTS):
                        eng.wait_ge(wv_.sem, wv_.value(run, i, "max", s))
                        for h in range(WIN_H):
                            n, c = head_place(h)
                            ins = eng.activation(wcv(s, "p")[:, KEYS * h:KEYS * h + KEYS], bank(s, n)[:, KEYS * c:KEYS * c + KEYS],
                                                 ACT.Exp, bias=stat(s, MAX + 2 * n + c), accum_out=stat(s, Z + h))
                        ins.then_inc(wa.tick("p", s), 1)
                    for s in range(SLOTS):
                        eng.wait_ge(wt.sem, wt.value(run, i, "pT", s))
                        eng.activation(wcv(s, "pT")[:, 512:1024], bank(s, 1), ACT.Copy)
                        eng.activation(wcv(s, "pTh")[0:64, 512:1024], bank(s, 3)[0:64, :], ACT.Copy).then_inc(wa.tick("pT", s), 1)
                    for s in range(SLOTS):
                        eng.wait_ge(wt.sem, wt.value(run, i, "oT", s))
                        eng.activation(wcv(s, "t"), bank(s, 1), ACT.Copy).then_inc(wa.tick("oT", s), 1)
                    guess_scalar(eng, wv_, wa, run, i, "fvar", ["fln", "frs"], norm_place)
                turn_loop(eng, body)

            def pool(self, eng, run, base):
                wv_, wa, wp, wt = win[self.first]
                rope_at = lambda i, n, a, b: turnt[:, self.depth, bass.ds(i.j, 1), n, a:b].broadcast_to([128, 8, b - a])

                def body(i):
                    wait_slots(eng, base, i)
                    for s in range(SLOTS):
                        eng.wait_ge(wv_.sem, wv_.value(run, i, "kn", s))
                        eng.tensor_tensor(stat(s, 24), stat(s, 25), stat(s, 25), ALU.mult)
                        k, t_ = heads(wcv(s, "k"), 8), heads(wcv(s, "tk"), 8)
                        eng.tensor_tensor(t_[:, :, 0:32], k[:, :, 32:64], rope_at(i, 3, 0, 32), ALU.mult)
                        eng.tensor_tensor(t_[:, :, 32:64], k[:, :, 0:32], rope_at(i, 3, 32, 64), ALU.mult).then_inc(wp.tick("k0", s), 1)
                    for s in range(SLOTS):
                        k = heads(wcv(s, "k"), 8)
                        eng.wait_ge(wp.sem, wp.value(run, i, "k0", s))
                        eng.tensor_tensor(stat(s, 24), stat(s, 25), stat(s, 25), ALU.mult)
                        eng.tensor_tensor(k, k, rope_at(i, 2, 0, 64), ALU.mult).then_inc(wp.tick("k1", s), 1)
                    for s in range(SLOTS):
                        eng.wait_ge(wp.sem, wp.value(run, i, "k1", s))
                        eng.tensor_tensor(wcv(s, "k"), wcv(s, "k"), wcv(s, "tk"), ALU.add).then_inc(wp.tick("k3", s), 1)
                turn_loop(eng, body)

            def tensor(self, eng, run, base):
                wv_, wa, wp, wt = win[self.first]
                def body(i):
                    wait_slots(eng, base, i)
                    for s in range(SLOTS):
                        eng.wait_ge(wv_.sem, wv_.value(run, i, "xn", s))
                        eng.transpose(bank(s, 0)[:, 0:128], wcv(s, "xn"), eye).then_inc(wt.tick("hT", s), 1)
                    for s in range(SLOTS):
                        eng.wait_ge(wv_.sem, wv_.value(run, i, "hT", s))
                        eng.wait_ge(wa.sem, wa.value(run, i, "hT", s))
                        for n in range(3):
                            ins = eng.matmul(bank(s, 1 + n), wcv(s, "hT")[:, 0:T], wqkv[:, self.depth, 512 * n:512 * n + 512], start=True, stop=True)
                        ins.then_inc(wt.tick("qkv", s), 1)
                    for s in range(SLOTS):
                        eng.wait_ge(wv_.sem, wv_.value(run, i, "q3", s))
                        for n in range(4):
                            eng.transpose(bank(s, 0)[:, 128 * n:128 * n + 128], wcv(s, "q")[:, 128 * n:128 * n + 128], eye)
                        eng.wait_ge(wp.sem, wp.value(run, i, "k3", s))
                        for n in range(4):
                            ins = eng.transpose(bank(s, 1)[:, 128 * n:128 * n + 128], wcv(s, "k")[:, 128 * n:128 * n + 128], eye)
                        ins.then_inc(wt.tick("qkT", s), 1)
                    for s in range(SLOTS):
                        eng.wait_ge(wa.sem, wa.value(run, i, "kT", s))
                        eng.wait_ge(wv_.sem, wv_.value(run, i, "qT", s))
                        for n in range(4):
                            eng.matmul(bank(s, n)[:, 0:2 * KEYS], eyeb, window_mask[:, bass.ds(i.j, 1), :], start=True, stop=True)
                        for h in range(WIN_H):
                            (n, c), r, at = head_place(h), 64 * (h % 2), h // 2
                            ins = eng.matmul(bank(s, n)[:, KEYS * c:KEYS * c + KEYS], wcv(s, "qT")[r:r + 64, 128 * at:128 * at + 128],
                                             wcv(s, "kT")[r:r + 64, KEYS * at:KEYS * at + KEYS], start=False, stop=True, skip_group_check=True)
                        ins.then_inc(wt.tick("sim", s), 1)
                    for s in range(SLOTS):
                        eng.wait_ge(wa.sem, wa.value(run, i, "p", s))
                        for h in range(8):
                            c = 128 * (h % 4)
                            eng.transpose(bank(s, h // 4)[:, c:c + 128], wcv(s, "p")[:, KEYS * h + WINDOW:KEYS * h + KEYS], eye)
                            ins = eng.transpose(bank(s, 2 + h // 4)[0:64, c:c + 128], wcv(s, "p")[:, KEYS * h:KEYS * h + WINDOW], eye)
                        ins.then_inc(wt.tick("pT", s), 1)
                    for s in range(SLOTS):
                        eng.wait_ge(wv_.sem, wv_.value(run, i, "pT", s))
                        eng.wait_ge(wa.sem, wa.value(run, i, "pT", s))
                        for h in range(8):
                            o = bank(s, 0)[:, 64 * h:64 * h + 64]
                            eng.matmul(o, wcv(s, "pT")[:, 128 * h:128 * h + 128], wcv(s, "v")[:, 64 * h:64 * h + 64], start=True, stop=False)
                            ins = eng.matmul(o, wcv(s, "pTh")[0:64, 128 * h:128 * h + 128], wcv(s, "vh")[0:64, 64 * h:64 * h + 64], start=False, stop=True)
                        ins.then_inc(wt.tick("o", s), 1)
                    for s in range(SLOTS):
                        eng.wait_ge(wv_.sem, wv_.value(run, i, "o", s))
                        for n in range(4):
                            ins = eng.transpose(bank(s, 1)[:, 128 * n:128 * n + 128], wcv(s, "q")[:, 128 * n:128 * n + 128], eye)
                        ins.then_inc(wt.tick("oT", s), 1)
                    for s in range(SLOTS):
                        eng.wait_ge(wa.sem, wa.value(run, i, "oT", s))
                        for n in range(4):
                            ins = eng.matmul(bank(s, 2)[:, 0:128], wcv(s, "t")[:, 128 * n:128 * n + 128], wwo[:, self.depth, n, :],
                                             start=n == 0, stop=n == 3)
                        ins.then_inc(wt.tick("y", s), 1)
                    for s in range(SLOTS):
                        eng.wait_ge(wv_.sem, wv_.value(run, i, "h2", s))
                        eng.matmul(bank(s, 3)[:, 0:64], masks[:, M_LAST, :], upper_before[:, s, :], start=True, stop=False)
                        eng.matmul(bank(s, 3)[:, 0:64], masks[:, M_SHIFT, :], wcv(s, "h2")[:, 64:128], start=False, stop=True)\
                            .then_inc(wt.tick("shift", s), 1)
                    for s in range(SLOTS):
                        eng.wait_ge(wv_.sem, wv_.value(run, i, "fxn", s))
                        eng.transpose(bank(s, 3)[:, 128:256], wcv(s, "g"), eye).then_inc(wt.tick("gT", s), 1)
                turn_loop(eng, body)

        GPART = [(0, 128), (128, 128), (256, HID - 256)]
        glu = {last: (steps(f"glu{int(last)}_vector", ["u0", "u1", "u2"] + ["h"] * last, turns=PAIRS),
                      steps(f"glu{int(last)}_scalar", ["gelu0", "gelu1", "gelu2"], turns=PAIRS),
                      steps(f"glu{int(last)}_tensor", ["ag0", "ag1", "ag2", "y"], turns=PAIRS)) for last in (False, True)}
        glu_ones = sem("glu_ones")
        gcv = carve([("u", 3 * 512), ("g", 2 * 512)])

        def tiles_of(ap, i, s):
            return ap[:, bass.ds(i * (SLOTS * TILES) + s * TILES, TILES), :]

        class Glu:
            loads = ("window",)

            def __init__(self, depth, last):
                self.depth, self.last = depth, last

            def vector(self, eng, run, base):
                gv, ga, gt = glu[self.last]
                eng.wait_ge(slot_free, base + SLOTS)
                for s in range(SLOTS):
                    ins = eng.memset(gcv(s, "u")[:, 1024:1536], 1.0)
                ins.then_inc(glu_ones, 1)
                eng.wait_ge(glu_ones, 2 * run + self.last + 1)

                def body(i):
                    for c, (lo, n) in enumerate(GPART):
                        for s in range(SLOTS):
                            eng.wait_ge(ga.sem, ga.value(run, i, f"gelu{c}", s))
                            eng.scalar_tensor_tensor(out=gcv(s, "u")[0:n, 512 * c:512 * c + 512], in0=bank(s, 2 * (c % 2))[0:n, :],
                                                     scalar=w1b[0:n, self.depth, c:c + 1], in1=gcv(s, "g")[0:n, 512 * (c % 2):512 * (c % 2) + 512],
                                                     op0=ALU.add, op1=ALU.mult).then_inc(gv.tick(f"u{c}", s), 1)
                    for s in range(SLOTS):
                        eng.wait_ge(gt.sem, gt.value(run, i, "y", s))
                        eng.tensor_tensor(tiles_of(hs, i, s), tiles_of(hs, i, s), heads(bank(s, 2), TILES), ALU.add)\
                            .then_inc(gv.tick("h", s) if self.last else slot_free, 1 if self.last else TILES)
                    if self.last:
                        for s in range(SLOTS):
                            eng.wait_ge(gv.sem, gv.value(run, i, "h", s))
                            eng.tensor_tensor(tiles_of(x, i, s), tiles_of(x, i, s), tiles_of(hs, i, s), ALU.add).then_inc(slot_free, TILES)
                pair_loop(eng, body)

            def scalar(self, eng, run, base):
                gv, ga, gt = glu[self.last]

                def body(i):
                    for c, (lo, n) in enumerate(GPART):
                        for s in range(SLOTS):
                            if c == 2:
                                eng.wait_ge(gv.sem, gv.value(run, i, "u0", s))
                            eng.wait_ge(gt.sem, gt.value(run, i, f"ag{c}", s))
                            eng.activation(gcv(s, "g")[0:n, 512 * (c % 2):512 * (c % 2) + 512], bank(s, 2 * (c % 2) + 1)[0:n, :], ACT.Gelu,
                                           bias=w1b[0:n, self.depth, 3 + c:4 + c]).then_inc(ga.tick(f"gelu{c}", s), 1)
                pair_loop(eng, body)

            def pool(self, eng, run, base):
                pass

            def tensor(self, eng, run, base):
                gv, ga, gt = glu[self.last]
                eng.wait_ge(slot_free, base + SLOTS)

                def body(i):
                    eng.wait_ge(slot_free, i * (SLOTS * TILES) + (base + SLOTS))
                    for c, (lo, n) in enumerate(GPART):
                        for s in range(SLOTS):
                            if c == 2:
                                eng.wait_ge(gv.sem, gv.value(run, i, "u0", s))
                            for half in range(2):
                                ins = eng.matmul(bank(s, 2 * (c % 2) + half)[0:n, :], w1[:, self.depth, HID * half + lo:HID * half + lo + n],
                                                 batch(feedT, i, s), start=True, stop=True)
                            ins.then_inc(gt.tick(f"ag{c}", s), 1)
                    for s in range(SLOTS):
                        eng.wait_ge(gv.sem, gv.value(run, i, "u2", s))
                        for b in range(TILES):
                            for c, (lo, n) in enumerate(GPART):
                                n += c == 2
                                ins = eng.matmul(bank(s, 2)[:, 128 * b:128 * b + 128], gcv(s, "u")[0:n, 512 * c + 128 * b:512 * c + 128 * b + 128],
                                                 w2[0:n, self.depth, c, :], start=c == 0, stop=c == 2)
                        ins.then_inc(gt.tick("y", s), 1)
                pair_loop(eng, body)

        feed = {kind: (steps(f"feed_{kind}_vector", NORM + ["tok"] * (kind == "routed") + ["vss", "nm1", "nm2", "nm3", "xr"] * (kind != "plain")
                                     + ["score"] * (kind == "routed")),
                       steps(f"feed_{kind}_scalar", ["ln", "rs"] + ["ss", "lnr", "rsr"] * (kind != "plain")),
                       steps(f"feed_{kind}_tensor", ["T"])) for kind in ("plain", "gates", "routed")}
        fcv = carve([("xn", 128), ("sq", 128), ("xr", 128), ("tk", 128)])
        R1 = (lambda s: (stat(s, 32), stat(s, 33), stat(s, 34), stat(s, 35)))

        class Feed:
            loads = ("tables",)

            def __init__(self, kind, rms):
                self.kind, self.rms = kind, rms

            def vector(self, eng, run, base):
                fv, fa, ft = feed[self.kind]
                def body(i):
                    wait_slots(eng, base, i)
                    norm_vector(eng, fv, fa, run, i, lambda s: [xb(i, s)], lambda s: [fcv(s, "xn")])
                    if self.kind == "routed":
                        for s in range(SLOTS):
                            eng.wait_ge(fv.sem, fv.value(run, i, "xn", s))
                            eng.tensor_tensor_reduce(out=fcv(s, "tk"), in0=fcv(s, "xn"), in1=token[:, :], scale=1.0, scalar=0.0, op0=ALU.mult,
                                                     op1=ALU.add, accum_out=stat(s, 40)).then_inc(fv.tick("tok", s), 1)
                    if self.rms:
                        scale, offset, least = self.rms
                        for s in range(SLOTS):
                            eng.wait_ge(fa.sem, fa.value(run, i, "ss", s))
                            if least:
                                eng.tensor_scalar(R1(s)[0], R1(s)[0], least, None, ALU.max).then_inc(fv.tick("vss", s), 1)
                            else:
                                eng.tensor_scalar(R1(s)[0], R1(s)[0], scale, offset, ALU.mult, ALU.add).then_inc(fv.tick("vss", s), 1)
                        newton(eng, fv, run, i, ["nm1", "nm2", "nm3"], R1,
                               lambda s: eng.wait_ge(fa.sem, fa.value(run, i, "rsr", s)))
                        for s in range(SLOTS):
                            eng.wait_ge(fv.sem, fv.value(run, i, "nm3", s))
                            eng.tensor_scalar(fcv(s, "xr"), fcv(s, "xn"), R1(s)[3], None, ALU.mult).then_inc(fv.tick("xr", s), 1)
                    if self.kind == "routed":
                        for s in range(SLOTS):
                            eng.wait_ge(fv.sem, fv.value(run, i, "tok", s))
                            eng.tensor_scalar(scores[:, bass.ds(i.tile(s), 1)], stat(s, 40), 1.0, None, ALU.mult).then_inc(fv.tick("score", s), 1)
                    for s in range(SLOTS):
                        eng.wait_ge(ft.sem, ft.value(run, i, "T", s))
                        if self.kind == "gates":
                            eng.tensor_tensor(xb(i, s), xb(i, s), fcv(s, "xn"), ALU.add)
                        eng.tensor_scalar(tileT(i, s), bank(s, 0)[:, 0:128], 1.0, None, ALU.mult).then_inc(slot_free, 1)
                turn_loop(eng, body)

            def scalar(self, eng, run, base):
                fv, fa, ft = feed[self.kind]
                def body(i):
                    wait_slots(eng, base, i)
                    guess_scalar(eng, fv, fa, run, i, "var", ["ln", "rs"], norm_place)
                    if self.rms:
                        for s in range(SLOTS):
                            eng.wait_ge(fv.sem, fv.value(run, i, "xn", s))
                            eng.activation(fcv(s, "sq"), fcv(s, "xn"), ACT.Square, accum_out=R1(s)[0]).then_inc(fa.tick("ss", s), 1)
                        guess_scalar(eng, fv, fa, run, i, "vss", ["lnr", "rsr"], R1)
                turn_loop(eng, body)

            def pool(self, eng, run, base):
                pass

            def tensor(self, eng, run, base):
                fv, fa, ft = feed[self.kind]
                def body(i):
                    wait_slots(eng, base, i)
                    for s in range(SLOTS):
                        eng.wait_ge(fv.sem, fv.value(run, i, "xr" if self.rms else "xn", s))
                        eng.transpose(bank(s, 0)[:, 0:128], fcv(s, "xr" if self.rms else "xn"), eye).then_inc(ft.tick("T", s), 1)
                turn_loop(eng, body)

        sv = steps("state_vector", ["cu", "su", "u", "scan", "p", "y"], turns=PAIRS)
        spl = steps("state_pool", ["q"], turns=PAIRS)
        st = steps("state_tensor", ["u", "y", "out"], turns=PAIRS)
        scv = carve([("a", 512), ("b", 512), ("g", 512), ("p", 512), ("q", 512), ("y", 512)])
        sm = sb("sm", [128, 24])
        smi = sb("smi", [128, 2], I32)
        decay = sb("decay", [128, N])

        class State:
            loads = ("state",)

            def vector(self, eng, run, base):
                eng.wait_ge(slot_free, base + SLOTS)
                cos, sin = turns[:, 0, 1:N + 1], turns[:, 1, 1:N + 1]

                def body(i):
                    for s in range(SLOTS):
                        eng.wait_ge(st.sem, st.value(run, i, "u", s))
                        eng.tensor_tensor(scv(s, "a"), bank(s, 0), cos, ALU.mult).then_inc(sv.tick("cu", s), 1)
                    for s in range(SLOTS):
                        eng.tensor_tensor(scv(s, "b"), bank(s, 1), sin, ALU.mult).then_inc(sv.tick("su", s), 1)
                    for s in range(SLOTS):
                        eng.wait_ge(sv.sem, sv.value(run, i, "su", s))
                        eng.tensor_tensor(scv(s, "a"), scv(s, "a"), scv(s, "b"), ALU.add).then_inc(sv.tick("u", s), 1)
                    for s in range(SLOTS):
                        eng.wait_ge(sv.sem, sv.value(run, i, "u", s))
                        eng.tensor_tensor_scan(scv(s, "g"), decay[:, :], scv(s, "a"), 0.0, ALU.mult, ALU.add).then_inc(sv.tick("scan", s), 1)
                    for s in range(SLOTS):
                        eng.wait_ge(sv.sem, sv.value(run, i, "scan", s))
                        eng.tensor_tensor(scv(s, "p"), scv(s, "g"), cos, ALU.mult).then_inc(sv.tick("p", s), 1)
                    for s in range(SLOTS):
                        eng.wait_ge(st.sem, st.value(run, i, "y", s))
                        eng.scalar_tensor_tensor(out=scv(s, "y"), in0=batch(feedT, i, s), scalar=sD[:, 0:1], in1=bank(s, 2),
                                                 op0=ALU.mult, op1=ALU.add).then_inc(sv.tick("y", s), 1)
                    for s in range(SLOTS):
                        eng.wait_ge(st.sem, st.value(run, i, "out", s))
                        eng.tensor_tensor(tiles_of(x, i, s), tiles_of(x, i, s), heads(bank(s, 3), TILES), ALU.add).then_inc(slot_free, TILES)
                pair_loop(eng, body)

            def scalar(self, eng, run, base):
                pass

            def pool(self, eng, run, base):
                def body(i):
                    for s in range(SLOTS):
                        eng.wait_ge(sv.sem, sv.value(run, i, "scan", s))
                        eng.tensor_tensor(scv(s, "q"), scv(s, "g"), turns[:, 1, 1:N + 1], ALU.mult).then_inc(spl.tick("q", s), 1)
                pair_loop(eng, body)

            def tensor(self, eng, run, base):
                def body(i):
                    eng.wait_ge(slot_free, i * (SLOTS * TILES) + (base + SLOTS))
                    for s in range(SLOTS):
                        eng.matmul(bank(s, 0), sB[:, 0, :], batch(feedT, i, s), start=True, stop=True)
                        eng.matmul(bank(s, 1), sB[:, 1, :], batch(feedT, i, s), start=True, stop=True).then_inc(st.tick("u", s), 1)
                    for s in range(SLOTS):
                        eng.wait_ge(sv.sem, sv.value(run, i, "p", s))
                        eng.matmul(bank(s, 2), sC[:, 0, :], scv(s, "p"), start=True, stop=False)
                        eng.wait_ge(spl.sem, spl.value(run, i, "q", s))
                        eng.matmul(bank(s, 2), sC[:, 1, :], scv(s, "q"), start=False, stop=True).then_inc(st.tick("y", s), 1)
                    for s in range(SLOTS):
                        eng.wait_ge(sv.sem, sv.value(run, i, "y", s))
                        for b in range(TILES):
                            eng.matmul(bank(s, 3)[:, 128 * b:128 * b + 128], scv(s, "y")[:, 128 * b:128 * b + 128], sWo[:, :], start=True, stop=False)
                            ins = eng.matmul(bank(s, 3)[:, 128 * b:128 * b + 128], ones_row[:, :], sbo[:, :], start=False, stop=True)
                        ins.then_inc(st.tick("out", s), 1)
                pair_loop(eng, body)

        QUADS = 4
        cvv = steps("causal_vector", NORM + ["qT"])
        ca = steps("causal_scalar", ["ln", "rs", "xT", "kT", "v"])
        ct = steps("causal_tensor", ["xT", "q", "kv"])
        ccv = carve([("xn", 128), ("xT", 128), ("qT", 512 * TILES), ("kT", 512 * TILES), ("v", 128 * TILES), ("p", 4 * N), ("pT", 4 * N)])
        cvv2 = steps("attend_vector", [x_ for j in range(TILES) for q in range(QUADS) for x_ in (f"max{j}{q}", f"bias{j}{q}", f"pT{j}{q}", f"rz{j}{q}", f"o{j}{q}")], turns=PAIRS)
        ca2 = steps("attend_scalar", [x_ for j in range(TILES) for x_ in [y_ for q in range(QUADS) for y_ in (f"p{j}{q}", f"pT{j}{q}")] + [f"oT{j}"]], turns=PAIRS)
        ct2 = steps("attend_tensor", [x_ for j in range(TILES) for x_ in [y_ for q in range(QUADS) for y_ in (f"sim{j}{q}", f"pT{j}{q}", f"o{j}{q}")] + [f"oT{j}", f"y{j}"]], turns=PAIRS)
        CMAX, CZ, CRZ = 96, 112, 128
        c_scale = CAUSAL_D ** -0.5

        class Causal:
            loads = ("tables", "causal")

            def vector(self, eng, run, base):
                with eng.Fori(0, PAIRS) as pair:
                    for j in range(TILES):
                        i = Turn(pair, j)
                        if j == 0:
                            eng.wait_ge(slot_free, pair * (SLOTS * TILES) + (base + SLOTS))
                        norm_vector(eng, cvv, ca, run, i, lambda s: [xb(i, s)], lambda s: [ccv(s, "xn")])
                        for s in range(SLOTS):
                            eng.wait_ge(ct.sem, ct.value(run, i, "q", s))
                            eng.tensor_copy(ccv(s, "qT")[:, 512 * j:512 * j + 512], bank(s, 1)).then_inc(cvv.tick("qT", s), 1)
                    for j in range(TILES):
                        keys = T * (j + 1)
                        for q in range(QUADS):
                            for s in range(SLOTS):
                                eng.wait_ge(ct2.sem, ct2.value(run, pair, f"sim{j}{q}", s))
                                for h in range(4):
                                    ins = eng.tensor_reduce(stat(s, CMAX + h), bank(s, h)[:, 0:keys], AX.X, ALU.max, negate=True)
                                ins.then_inc(cvv2.tick(f"max{j}{q}", s), 1)
                            for s in range(SLOTS):
                                eng.wait_ge(cvv2.sem, cvv2.value(run, pair, f"max{j}{q}", s))
                                eng.tensor_scalar(stat(s, CMAX, 4), stat(s, CMAX, 4), c_scale, None, ALU.mult).then_inc(cvv2.tick(f"bias{j}{q}", s), 1)
                            for s in range(SLOTS):
                                eng.wait_ge(ct2.sem, ct2.value(run, pair, f"pT{j}{q}", s))
                                for h in range(2):
                                    ins = eng.tensor_copy(ccv(s, "pT")[:, N * h:N * h + keys], bank(s, h)[:, 0:keys])
                                ins.then_inc(cvv2.tick(f"pT{j}{q}", s), 1)
                            for s in range(SLOTS):
                                eng.wait_ge(ca2.sem, ca2.value(run, pair, f"p{j}{q}", s))
                                eng.reciprocal(stat(s, CRZ, 4), stat(s, CZ, 4)).then_inc(cvv2.tick(f"rz{j}{q}", s), 1)
                            for s in range(SLOTS):
                                eng.wait_ge(ct2.sem, ct2.value(run, pair, f"o{j}{q}", s))
                                eng.wait_ge(cvv2.sem, cvv2.value(run, pair, f"rz{j}{q}", s))
                                eng.tensor_tensor(heads(ccv(s, "xn")[:, 32 * q:32 * q + 32], 4), heads(bank(s, 0)[:, 0:32], 4),
                                                  over(stat(s, CRZ, 4), 4, CAUSAL_D), ALU.mult).then_inc(cvv2.tick(f"o{j}{q}", s), 1)
                        for s in range(SLOTS):
                            eng.wait_ge(ct2.sem, ct2.value(run, pair, f"y{j}", s))
                            eng.tensor_tensor(xb(Turn(pair, j), s), xb(Turn(pair, j), s), bank(s, 2)[:, 0:128], ALU.add).then_inc(slot_free, 1)

            def scalar(self, eng, run, base):
                with eng.Fori(0, PAIRS) as pair:
                    for j in range(TILES):
                        i = Turn(pair, j)
                        guess_scalar(eng, cvv, ca, run, i, "var", ["ln", "rs"], norm_place)
                        for s in range(SLOTS):
                            eng.wait_ge(ct.sem, ct.value(run, i, "xT", s))
                            eng.activation(ccv(s, "xT"), bank(s, 0)[:, 0:128], ACT.Copy).then_inc(ca.tick("xT", s), 1)
                        for s in range(SLOTS):
                            eng.wait_ge(ct.sem, ct.value(run, i, "kv", s))
                            eng.activation(ccv(s, "kT")[:, 512 * j:512 * j + 512], bank(s, 2), ACT.Copy).then_inc(ca.tick("kT", s), 1)
                        for s in range(SLOTS):
                            eng.activation(ccv(s, "v")[:, 128 * j:128 * j + 128], bank(s, 3)[:, 0:128], ACT.Copy).then_inc(ca.tick("v", s), 1)
                    for j in range(TILES):
                        keys = T * (j + 1)
                        for q in range(QUADS):
                            for s in range(SLOTS):
                                eng.wait_ge(cvv2.sem, cvv2.value(run, pair, f"bias{j}{q}", s))
                                for h in range(4):
                                    ins = eng.activation(ccv(s, "p")[:, N * h:N * h + keys], bank(s, h)[:, 0:keys], ACT.Exp, bias=stat(s, CMAX + h),
                                                         scale=c_scale, accum_out=stat(s, CZ + h))
                                ins.then_inc(ca2.tick(f"p{j}{q}", s), 1)
                            for s in range(SLOTS):
                                eng.wait_ge(ct2.sem, ct2.value(run, pair, f"pT{j}{q}", s))
                                for h in range(2, 4):
                                    ins = eng.activation(ccv(s, "pT")[:, N * h:N * h + keys], bank(s, h)[:, 0:keys], ACT.Copy)
                                ins.then_inc(ca2.tick(f"pT{j}{q}", s), 1)
                        for s in range(SLOTS):
                            eng.wait_ge(ct2.sem, ct2.value(run, pair, f"oT{j}", s))
                            eng.activation(ccv(s, "xT"), bank(s, 1)[:, 0:128], ACT.Copy).then_inc(ca2.tick(f"oT{j}", s), 1)

            def pool(self, eng, run, base):
                pass

            def tensor(self, eng, run, base):
                with eng.Fori(0, PAIRS) as pair:
                    for j in range(TILES):
                        i = Turn(pair, j)
                        if j == 0:
                            eng.wait_ge(slot_free, pair * (SLOTS * TILES) + (base + SLOTS))
                        for s in range(SLOTS):
                            eng.wait_ge(cvv.sem, cvv.value(run, i, "xn", s))
                            eng.transpose(bank(s, 0)[:, 0:128], ccv(s, "xn"), eye).then_inc(ct.tick("xT", s), 1)
                        for s in range(SLOTS):
                            eng.wait_ge(ca.sem, ca.value(run, i, "xT", s))
                            if j:
                                eng.wait_ge(cvv.sem, cvv.value(run, Turn(pair, j - 1), "qT", s))
                            for n in range(4):
                                ins = eng.matmul(bank(s, 1)[:, 128 * n:128 * n + 128], cqk[:, 0, n, :], ccv(s, "xT"), start=True, stop=True)
                            ins.then_inc(ct.tick("q", s), 1)
                        for s in range(SLOTS):
                            if j:
                                eng.wait_ge(ca.sem, ca.value(run, Turn(pair, j - 1), "v", s))
                            for n in range(4):
                                eng.matmul(bank(s, 2)[:, 128 * n:128 * n + 128], cqk[:, 1, n, :], ccv(s, "xT"), start=True, stop=True)
                            eng.matmul(bank(s, 3)[:, 0:128], ccv(s, "xT"), cv[:, :], start=True, stop=True).then_inc(ct.tick("kv", s), 1)
                    for j in range(TILES):
                        for q in range(QUADS):
                            for s in range(SLOTS):
                                if j == 0 and q == 0:
                                    eng.wait_ge(cvv.sem, cvv.value(run, Turn(pair, TILES - 1), "qT", s))
                                    eng.wait_ge(ca.sem, ca.value(run, Turn(pair, TILES - 1), "v", s))
                                elif q:
                                    eng.wait_ge(cvv2.sem, cvv2.value(run, pair, f"o{j}{q - 1}", s))
                                else:
                                    eng.wait_ge(slot_free, pair * (SLOTS * TILES) + (base + SLOTS * j + s + 1))
                                for h in range(4):
                                    for k in range(j + 1):
                                        o = bank(s, h)[:, 128 * k:128 * k + 128]
                                        ins = eng.matmul(o, ccv(s, "qT")[32 * h:32 * h + 32, 512 * j + 128 * q:512 * j + 128 * q + 128],
                                                         ccv(s, "kT")[32 * h:32 * h + 32, 512 * k + 128 * q:512 * k + 128 * q + 128], start=True, stop=k < j)
                                        if k == j:
                                            ins = eng.matmul(o, eyeb, causal_mask[:, :], start=False, stop=True)
                                ins.then_inc(ct2.tick(f"sim{j}{q}", s), 1)
                            for s in range(SLOTS):
                                eng.wait_ge(ca2.sem, ca2.value(run, pair, f"p{j}{q}", s))
                                for h in range(4):
                                    for k in range(j + 1):
                                        ins = eng.transpose(bank(s, h)[:, 128 * k:128 * k + 128], ccv(s, "p")[:, N * h + 128 * k:N * h + 128 * k + 128], eye)
                                ins.then_inc(ct2.tick(f"pT{j}{q}", s), 1)
                            for s in range(SLOTS):
                                eng.wait_ge(cvv2.sem, cvv2.value(run, pair, f"pT{j}{q}", s))
                                eng.wait_ge(ca2.sem, ca2.value(run, pair, f"pT{j}{q}", s))
                                for h in range(4):
                                    for k in range(j + 1):
                                        at = 128 * k + 32 * q + 8 * h
                                        ins = eng.matmul(bank(s, 0)[:, 8 * h:8 * h + 8], ccv(s, "pT")[:, N * h + 128 * k:N * h + 128 * k + 128],
                                                         ccv(s, "v")[:, at:at + 8], start=k == 0, stop=k == j)
                                ins.then_inc(ct2.tick(f"o{j}{q}", s), 1)
                        for s in range(SLOTS):
                            eng.wait_ge(cvv2.sem, cvv2.value(run, pair, f"o{j}{QUADS - 1}", s))
                            eng.transpose(bank(s, 1)[:, 0:128], ccv(s, "xn"), eye).then_inc(ct2.tick(f"oT{j}", s), 1)
                        for s in range(SLOTS):
                            eng.wait_ge(ca2.sem, ca2.value(run, pair, f"oT{j}", s))
                            eng.matmul(bank(s, 2)[:, 0:128], ccv(s, "xT"), cwo[:, :], start=True, stop=True).then_inc(ct2.tick(f"y{j}", s), 1)

        RPART = [128, 128, 128, 128, LIGHT]
        rv = steps("routed_vector", ["light"], turns=PAIRS)
        ra = steps("routed_scalar", [f"gelu{c}" for c in range(5)], turns=PAIRS)
        rt = steps("routed_tensor", [f"h{c}" for c in range(5)] + ["y"], turns=PAIRS)
        rcv = carve([("u", 5 * 512)])
        rset = sem("routed_ones")
        descent_in = sem("descent_scores")
        dd = sem("descent_vector")
        dac = sem("descent_scalar")
        key_T = sem("descent_back")
        key_cols = sem("descent_columns")
        row_out = sem("rank_row")
        rank_done = sem("rank_step")
        route = sb("route", [B, 12])
        LMAX, NA, MX, ZS, LZ, NMX = 0, 1, 2, 3, 4, 5
        picked = sb("picked", [128, 2, TILES, B])
        rank = sb("rank", [128, 2, 2])
        S_ = lambda: arena[0:B, 0, 0:N]
        T_ = lambda: arena[0:B, 0, N:2 * N]
        E_ = lambda: arena[0:B, 0, 2 * N:3 * N]
        K_ = lambda: arena[0:B, 0, 3 * N:4 * N]
        W_ = lambda: arena[0:B, 0, 4 * N:5 * N]
        CMP = lambda g: arena[:, 0, (5 + g) * N:(6 + g) * N]
        LOGK = float(np.log(np.float32(FETCH)))
        RANKS = B * TILES

        class Routed:
            loads = ("ffn",)

            def vector(self, eng, run, base):
                n = [run * DESCENT]

                def link(ins):
                    n[0] += 1
                    ins.then_inc(dd, 1)
                    eng.wait_ge(dd, n[0])

                eng.wait_ge(slot_free, base + SLOTS)
                for s in range(SLOTS):
                    ins = eng.memset(rcv(s, "u")[64:128, 2048:2560], 1.0)
                ins.then_inc(rset, 1)
                eng.wait_ge(rset, run + 1)
                eng.wait_ge(descent_in, run + 1)
                eng.tensor_copy(S_(), P[0:B, 0, :]).then_inc(dd, 1)
                n[0] += 1
                eng.wait_ge(dd, n[0])
                link(eng.tensor_reduce(route[:, LMAX:LMAX + 1], S_(), AX.X, ALU.max))
                eng.memset(route[:, NA:NA + 1], float(np.log(np.float32(N))) - LOGK)
                eng.memset(route[:, MX:MX + 1], 0.0).then_inc(dd, 1)
                n[0] += 1
                eng.wait_ge(dd, n[0])
                link(eng.tensor_tensor(route[:, MX:MX + 1], route[:, LMAX:LMAX + 1], route[:, NA:NA + 1], ALU.min))
                start = n[0]
                with eng.Fori(0, ITERS - 1) as it:
                    eng.tensor_scalar(T_(), S_(), route[:, NA:NA + 1], route[:, MX:MX + 1], ALU.min, ALU.subtract).then_inc(dd, 1)
                    eng.wait_ge(dac, it * 2 + (run * 2 * (ITERS - 1) + 2))
                    eng.scalar_tensor_tensor(out=route[:, NA:NA + 1], in0=route[:, LZ:LZ + 1], scalar=-LOGK, in1=route[:, MX:MX + 1],
                                             op0=ALU.add, op1=ALU.add).then_inc(dd, 1)
                    eng.wait_ge(dd, it * 3 + (start + 2))
                    eng.tensor_tensor(route[:, MX:MX + 1], route[:, LMAX:LMAX + 1], route[:, NA:NA + 1], ALU.min).then_inc(dd, 1)
                    eng.wait_ge(dd, it * 3 + (start + 3))
                n[0] = start + 3 * (ITERS - 1)
                link(eng.tensor_scalar(T_(), S_(), route[:, NA:NA + 1], 0.0, ALU.subtract, ALU.min))
                link(eng.scalar_tensor_tensor(out=K_(), in0=T_(), scalar=-2.0 ** -25, in1=T_(), op0=ALU.is_lt, op1=ALU.mult))
                eng.wait_ge(exp_key, run + 1)
                link(eng.tensor_scalar(T_(), E_(), -1.0, 1.0, ALU.mult, ALU.add))
                link(eng.tensor_tensor(W_(), T_(), E_(), ALU.add))
                assert n[0] == run * DESCENT + DESCENT, (n[0], DESCENT)
                eng.wait_ge(key_T, run + 1)
                eng.tensor_copy(picked[:, :, :, :].rearrange("p a j b -> p (a j b)"), P[:, 1, 0:2 * TILES * B]).then_inc(key_cols, 1)
                eng.wait_ge(key_cols, run + 1)
                for b in range(B):
                    for j in range(TILES):
                        m = b * TILES + j
                        if j == 0:
                            eng.wait_ge(row_out, run * B + b + 1)
                        row = P[:, 2 + b % 2, :]
                        key = picked[:, 0, j, b:b + 1]
                        g = m % 2
                        eng.tensor_scalar(CMP(0), row, key, 0.0, ALU.is_gt, ALU.add, accum_out=rank[:, g, 0:1])
                        eng.scalar_tensor_tensor(out=CMP(1), in0=row, scalar=key, in1=before[:, 384 - 128 * j:384 - 128 * j + N],
                                                 op0=ALU.is_equal, op1=ALU.mult, accum_out=rank[:, g, 1:2]).then_inc(rank_done, 1)
                        eng.wait_ge(rank_done, (run * RANKS + m) * 3 + 1)
                        eng.tensor_tensor(rank[:, g, 0:1], rank[:, g, 0:1], rank[:, g, 1:2], ALU.add).then_inc(rank_done, 1)
                        eng.wait_ge(rank_done, (run * RANKS + m) * 3 + 2)
                        eng.scalar_tensor_tensor(out=weight[:, m:m + 1], in0=rank[:, g, 0:1], scalar=float(KEEP), in1=picked[:, 1, j, b:b + 1],
                                                 op0=ALU.is_lt, op1=ALU.mult).then_inc(rank_done, 1)
                eng.wait_ge(rank_done, (run + 1) * RANKS * 3)

                def body(i):
                    for s in range(SLOTS):
                        eng.wait_ge(rt.sem, rt.value(run, i, "y", s))
                        eng.tensor_tensor(tiles_of(x, i, s), tiles_of(x, i, s), heads(bank(s, 3), TILES), ALU.add).then_inc(rv.tick("light", s), 1)
                    for s in range(SLOTS):
                        eng.wait_ge(rv.sem, rv.value(run, i, "light", s))
                        for k in range(TILES):
                            at = i * (SLOTS * TILES) + (s * TILES + k)
                            ins = eng.scalar_tensor_tensor(out=x[:, bass.ds(at, 1), :], in0=bank(s, 0)[:, 128 * k:128 * k + 128],
                                                           scalar=weight[:, bass.ds(at, 1)], in1=x[:, bass.ds(at, 1), :], op0=ALU.mult, op1=ALU.add)
                        ins.then_inc(slot_free, TILES)
                pair_loop(eng, body)

            def scalar(self, eng, run, base):
                first = run * DESCENT + 4
                with eng.Fori(0, ITERS - 1) as it:
                    eng.wait_ge(dd, it * 3 + (first + 1))
                    eng.activation(E_(), T_(), ACT.Exp, accum_out=route[:, ZS:ZS + 1]).then_inc(dac, 1)
                    eng.wait_ge(dac, it * 2 + (run * 2 * (ITERS - 1) + 1))
                    eng.activation(route[:, LZ:LZ + 1], route[:, ZS:ZS + 1], ACT.Ln).then_inc(dac, 1)
                eng.wait_ge(dd, first + 3 * (ITERS - 1) + 2)
                eng.activation(E_(), K_(), ACT.Exp).then_inc(exp_key, 1)
                eng.wait_ge(rank_done, (run + 1) * RANKS * 3)

                def body(i):
                    for c, n in enumerate(RPART):
                        for s in range(SLOTS):
                            eng.wait_ge(rt.sem, rt.value(run, i, f"h{c}", s))
                            eng.activation(rcv(s, "u")[0:n, 512 * c:512 * c + 512], bank(s, c % 3)[0:n, :], ACT.Gelu,
                                           bias=fb1[0:n, c:c + 1]).then_inc(ra.tick(f"gelu{c}", s), 1)
                pair_loop(eng, body)

            def pool(self, eng, run, base):
                pass

            def tensor(self, eng, run, base):
                eng.wait_ge(slot_free, base + SLOTS)
                for j in range(TILES):
                    ins = eng.transpose(P[0:B, 0, 128 * j:128 * j + 128], scores[:, :].rearrange("p (b j) -> p j b", j=TILES)[:, j, :], eye)
                ins.then_inc(descent_in, 1)
                eng.wait_ge(dd, run * DESCENT + DESCENT)
                for a, src in enumerate((K_(), W_())):
                    for j in range(TILES):
                        at = (a * TILES + j) * B
                        ins = eng.transpose(P[:, 1, at:at + B], src[:, 128 * j:128 * j + 128], masks[0:B, M_EYE, 0:B])
                ins.then_inc(key_T, 1)
                for b in range(B):
                    if b >= 2:
                        eng.wait_ge(rank_done, (run * RANKS + (b - 1) * TILES) * 3)
                    eng.matmul(P[:, 2 + b % 2, :], pick[:, b, :], K_(), start=True, stop=True).then_inc(row_out, 1)
                eng.wait_ge(rank_done, (run + 1) * RANKS * 3)

                def body(i):
                    eng.wait_ge(slot_free, i * (SLOTS * TILES) + (base + SLOTS))
                    for c, n in enumerate(RPART):
                        for s in range(SLOTS):
                            if c >= 3:
                                eng.wait_ge(ra.sem, ra.value(run, i, f"gelu{c - 3}", s))
                            eng.matmul(bank(s, c % 3), fw1[:, 128 * c:128 * c + 128], batch(feedT, i, s), start=True, stop=True)\
                                .then_inc(rt.tick(f"h{c}", s), 1)
                    for s in range(SLOTS):
                        eng.wait_ge(ra.sem, ra.value(run, i, "gelu4", s))
                        for b in range(TILES):
                            u = lambda c, n: rcv(s, "u")[0:n, 512 * c + 128 * b:512 * c + 128 * b + 128]
                            eng.matmul(bank(s, 3)[:, 128 * b:128 * b + 128], u(4, LIGHT + 1), fw2[0:LIGHT + 1, 4, :], start=True, stop=True)
                            heavy = bank(s, 0)[:, 128 * b:128 * b + 128]
                            for c in range(4):
                                eng.matmul(heavy, u(c, 128), fw2[:, c, :], start=c == 0, stop=False)
                            ins = eng.matmul(heavy, ones_row[:, :], fb2[:, :], start=False, stop=True)
                        ins.then_inc(rt.tick("y", s), 1)
                pair_loop(eng, body)

        DESCENT = 8 + 3 * (ITERS - 1)
        exp_key = sem("descent_exponential")

        SCAN_TURNS = CHUNKS // SLOTS
        mv = steps("gates_vector", ["max", "logits", "z", "rz"], turns=SCAN_TURNS)
        ma = steps("gates_scalar", ["in", "v", "e"], turns=SCAN_TURNS)
        mp = steps("gates_pool", ["g", "gv"], turns=SCAN_TURNS)
        mt = steps("gates_tensor", ["logits"], turns=SCAN_TURNS)
        mcv = carve([("e", GATES), ("in", 128), ("v", 128), ("mx", 128), ("z", 128), ("rz", 128), ("ring", CHUNK * SCAN_M * CELL)])
        chains = B * SCAN_H
        states = sb("states", [chains, SLOTS, CHUNK + 1, SCAN_M])
        chunk_done = sem("chunk_scanned")
        moved_out = [sem(f"gates_out_{s}") for s in range(SLOTS)]
        moved = [sem(f"gates_moved_{s}") for s in range(SLOTS)]
        saved = [sem(f"states_saved_{s}") for s in range(SLOTS)]
        step_done = sem("scan_step")
        saving = sem("states_being_saved")
        BANKED = [(n * BANK_ROWS, min(BANK_ROWS, ROWS - n * BANK_ROWS)) for n in range(-(-ROWS // BANK_ROWS))]
        gates_dram = nc.dram_tensor("gates_by_chain", [SLOTS, B, SCAN_H, CHUNK, SCAN_M * CELL], F32).ap()
        mixed = nc.dram_tensor("scan_by_token", [B, N, SCAN_H, SCAN_M], F32).ap()
        STEPS = 2 * CHUNK + 1

        class Scan:
            loads = ("gates",)

            def vector(self, eng, run, base):
                eng.wait_ge(slot_free, base + SLOTS)
                eng.memset(states[:, :, :, :], 0.0).then_inc(chunk_done, 1)
                eng.wait_ge(chunk_done, 1)
                eng.sem_inc(chunk_done, 1)
                eng.sem_inc(step_done, 1)

                def body(i):
                    for s in range(SLOTS):
                        eng.wait_ge(mt.sem, mt.value(run, i, "logits", s))
                        view = lambda n, k: P[:, n, 0:CELL * k].rearrange("p (r c) -> p r c", c=CELL)
                        for n, (lo, k) in enumerate(BANKED):
                            ins = eng.tensor_reduce(mcv(s, "mx")[:, lo:lo + k], view(n, k), AX.X, ALU.max)
                        ins.then_inc(mv.sem, 1)
                        eng.wait_ge(mv.sem, mv.value(run, i, "max", 0) + 2 * s)
                        for n, (lo, k) in enumerate(BANKED):
                            ins = eng.tensor_tensor(mcv(s, "e")[:, CELL * lo:CELL * (lo + k)].rearrange("p (r c) -> p r c", c=CELL), view(n, k),
                                                    over(mcv(s, "mx")[:, lo:lo + k], k, CELL), ALU.subtract)
                        ins.then_inc(mv.sem, 1)
                    for s in range(SLOTS):
                        eng.wait_ge(ma.sem, ma.value(run, i, "e", s))
                        eng.tensor_reduce(mcv(s, "z"), heads(mcv(s, "e"), ROWS), AX.X, ALU.add).then_inc(mv.sem, 1)
                    for s in range(SLOTS):
                        eng.wait_ge(mv.sem, mv.value(run, i, "z", s))
                        eng.reciprocal(mcv(s, "rz"), mcv(s, "z")).then_inc(mv.sem, 1)
                    for s in range(SLOTS):
                        eng.wait_ge(moved[s], i * (16 * B) + 16 * B)
                        eng.wait_ge(saved[s], i * (16 * B) + 16 * B)
                        ring = mcv(s, "ring").rearrange("p (t r c) -> p t r c", t=CHUNK, c=CELL)
                        at = (i * SLOTS + s) * STEPS
                        eng.wait_ge(step_done, at + 1)
                        eng.tensor_copy(states[:, s, 0, :], states[:, 1 - s, CHUNK, :]).then_inc(step_done, 1)
                        for k in range(CHUNK):
                            eng.wait_ge(step_done, at + (2 * k + 2))
                            eng.tensor_tensor(ring[0:chains, k, :, 1:CELL], ring[0:chains, k, :, 1:CELL],
                                              each(states[:, s, k, :], SCAN_M), ALU.mult).then_inc(step_done, 1)
                            eng.wait_ge(step_done, at + (2 * k + 3))
                            ins = eng.tensor_reduce(states[:, s, k + 1, :], ring[0:chains, k, :, :], AX.X, ALU.add).then_inc(step_done, 1)
                        eng.wait_ge(step_done, at + STEPS + 1)
                        eng.sem_inc(chunk_done, 1)
                with eng.Fori(0, SCAN_TURNS) as i:
                    body(i)
                eng.wait_ge(y_moved, 16 * B)
                eng.sem_inc(slot_free, B * TILES)

            def scalar(self, eng, run, base):
                eng.wait_ge(slot_free, base + SLOTS)
                with eng.Fori(0, SCAN_TURNS) as i:
                    for s in range(SLOTS):
                        eng.wait_ge(chunk_done, i * SLOTS + (s + 1))
                        eng.activation(mcv(s, "in").rearrange("p (b t) -> p b t", b=B), feedT[:, :, bass.ds((i * SLOTS + s) * CHUNK, CHUNK)],
                                       ACT.Copy).then_inc(ma.tick("in", s), 1)
                    for s in range(SLOTS):
                        eng.wait_ge(mt.sem, mt.value(run, i, "logits", s))
                        eng.activation(mcv(s, "v"), P[:, 5, 0:128], ACT.Copy).then_inc(ma.tick("v", s), 1)
                    for s in range(SLOTS):
                        eng.wait_ge(mv.sem, mv.value(run, i, "max", 0) + (2 * s + 1))
                        eng.activation(mcv(s, "e"), mcv(s, "e"), ACT.Exp).then_inc(ma.tick("e", s), 1)

            def pool(self, eng, run, base):
                with eng.Fori(0, SCAN_TURNS) as i:
                    for s in range(SLOTS):
                        eng.wait_ge(mv.sem, mv.value(run, i, "rz", s))
                        eng.tensor_tensor(heads(mcv(s, "e"), ROWS), heads(mcv(s, "e"), ROWS), over(mcv(s, "rz"), ROWS, CELL), ALU.mult)\
                            .then_inc(mp.tick("g", s), 1)
                    for s in range(SLOTS):
                        eng.wait_ge(mp.sem, mp.value(run, i, "g", s))
                        first = heads(mcv(s, "e"), ROWS)[:, :, 0:1]
                        eng.tensor_tensor(first, first, mcv(s, "v").unsqueeze(2), ALU.mult).then_inc(mp.tick("gv", s), 1)

            def sync(self, eng, run, base):
                eng.wait_ge(slot_free, base + SLOTS)
                for s in range(SLOTS):
                    eng.sem_inc(saved[s], 16 * B)
                with eng.Fori(0, SCAN_TURNS) as i:
                    for s in range(SLOTS):
                        eng.wait_ge(mp.sem, mp.value(run, i, "gv", s))
                        for b in range(B):
                            eng.dma_start(gates_dram[s, b].rearrange("h t e -> t h e"),
                                          mcv(s, "e")[CHUNK * b:CHUNK * b + CHUNK, :].rearrange("t (h e) -> t h e", h=SCAN_H)).then_inc(moved_out[s], 16)
                        eng.wait_ge(moved_out[s], i * (16 * B) + 16 * B)
                        eng.sem_inc(saving, 1)
                        eng.wait_ge(chunk_done, i * SLOTS + (s + 1))
                        for b in range(B):
                            eng.dma_start(mcv(s, "ring")[SCAN_H * b:SCAN_H * b + SCAN_H, :].rearrange("h (t e) -> h t e", t=CHUNK),
                                          gates_dram[s, b]).then_inc(moved[s], 16)
                    for s in range(SLOTS):
                        eng.wait_ge(chunk_done, i * SLOTS + (s + 3))
                        eng.sem_inc(saving, 1)
                        for b in range(B):
                            eng.dma_start(mixed[b, bass.ds((i * SLOTS + s) * CHUNK, CHUNK), :, :].rearrange("t h m -> h t m"),
                                          states[SCAN_H * b:SCAN_H * b + SCAN_H, s, 1:CHUNK + 1, :]).then_inc(saved[s], 16)

            def tensor(self, eng, run, base):
                eng.wait_ge(slot_free, base + SLOTS)
                with eng.Fori(0, SCAN_TURNS) as i:
                    for s in range(SLOTS):
                        eng.wait_ge(ma.sem, ma.value(run, i, "in", s))
                        if s:
                            eng.wait_ge(mv.sem, mv.value(run, i, "max", 0) + 1)
                            eng.wait_ge(ma.sem, ma.value(run, i, "v", s - 1))
                        for n, (lo, k) in enumerate(BANKED):
                            eng.matmul(P[:, n, 0:CELL * k], mcv(s, "in"), gwa[:, CELL * lo:CELL * (lo + k)], start=True, stop=True)
                        eng.matmul(P[:, 5, 0:128], mcv(s, "in"), gwv[:, :], start=True, stop=True).then_inc(mt.tick("logits", s), 1)

        ov = steps("mix_vector", ["in"])
        oa = steps("mix_scalar", ["T"])
        ot = steps("mix_tensor", ["T", "y"])
        ocv = carve([("in", 128), ("T", 128)])

        class Mix:
            loads = ()

            def vector(self, eng, run, base):
                def body(i):
                    wait_slots(eng, base, i)
                    for s in range(SLOTS):
                        eng.tensor_scalar(ocv(s, "in"), hs[:, bass.ds(i.tile(s), 1), :], 1.0, None, ALU.mult).then_inc(ov.tick("in", s), 1)
                    for s in range(SLOTS):
                        eng.wait_ge(ot.sem, ot.value(run, i, "y", s))
                        eng.tensor_tensor(xb(i, s), xb(i, s), bank(s, 1)[:, 0:128], ALU.add).then_inc(slot_free, 1)
                turn_loop(eng, body)

            def scalar(self, eng, run, base):
                def body(i):
                    for s in range(SLOTS):
                        eng.wait_ge(ot.sem, ot.value(run, i, "T", s))
                        eng.activation(ocv(s, "T"), bank(s, 0)[:, 0:128], ACT.Copy).then_inc(oa.tick("T", s), 1)
                turn_loop(eng, body)

            def pool(self, eng, run, base):
                pass

            def tensor(self, eng, run, base):
                def body(i):
                    wait_slots(eng, base, i)
                    for s in range(SLOTS):
                        eng.wait_ge(ov.sem, ov.value(run, i, "in", s))
                        eng.transpose(bank(s, 0)[:, 0:128], ocv(s, "in"), eye).then_inc(ot.tick("T", s), 1)
                    for s in range(SLOTS):
                        eng.wait_ge(oa.sem, oa.value(run, i, "T", s))
                        eng.matmul(bank(s, 1)[:, 0:128], ocv(s, "T"), gwo[:, :], start=True, stop=True).then_inc(ot.tick("y", s), 1)
                turn_loop(eng, body)

        rms_norm = (None, None, 1e-24)
        rms_mean = (1.0 / D, LN_EPS, None)
        program = [
            (Delta(), 0),
            (Window(True, 0), 0), (Glu(0, False), 0), (Window(False, 1), 0), (Glu(1, True), 0),
            (Feed("plain", None), 0), (State(), 0),
            (Window(True, 0), 1), (Glu(0, False), 1), (Window(False, 1), 1), (Glu(1, True), 1),
            (Causal(), 0),
            (Feed("routed", rms_norm), 0), (Routed(), 0),
            (Feed("gates", rms_mean), 0), (Scan(), 0), (Mix(), 0),
            (Feed("routed", rms_norm), 1), (Routed(), 1),
        ]

        loads = {
            "x": [(x[:, TILES * b:TILES * b + TILES, :], t["x"][b].rearrange("(j t) d -> t j d", t=T)) for b in range(B)],
            "tables": [(masks[:, :, :], t["masks"]), (window_mask[:, :, :], t["window_mask"]), (causal_mask[:, :], t["causal_mask"]), (eye_bf16[:, :], t["eye_bf16"]),
                       (before[:, :], t["before"]), (turnt[:, 0, :, :, :], t["rope"]), (turnt[:, 1, :, :, :], t["rope"]), (pick[:, :, :], t["pick"]),
                       (keep[:, :], t["keep"]), (began[:, 1:TILES], t["keep"][:, 0:TILES - 1]), (began[:, 0:1], t["keep"][:, TILES - 1:TILES])],
            "delta": [(dw[:, :], t["delta_w"]), (dwo[:, :], t["L0_attn_a_Wo"])]
            + [(dg[32 * h:32 * h + 32, :], t["L0_attn_a_g_norm"].unsqueeze(1)) for h in range(4)],
            "window": [(wqkv[:, :, :], t["L0_ffn_wqkv"].rearrange("l d n -> d l n")),
                       (wwo[:, :, :, :], t["L0_ffn_wo"].rearrange("l (c p) n -> p l c n", c=4)),
                       (w1[:, :, :], t["L0_ffn_w1"].rearrange("l d n -> d l n")),
                       (lgb[:, :, 0], t["L0_ffn_ln_g"].rearrange("l d -> d l")), (lgb[:, :, 1], t["L0_ffn_ln_b"].rearrange("l d -> d l"))]
            + [(w2[0:n, l, c, :], t["L0_ffn_w2"][l, lo:lo + n, :]) for l in range(DEPTH) for c, (lo, n) in enumerate(GPART)]
            + [(w2[HID - 256:HID - 255, l, 2, :], t["L0_ffn_b2"][l:l + 1, :]) for l in range(DEPTH)]
            + [(w1b[0:n, l, 3 * half + c:3 * half + c + 1], t["L0_ffn_b1"][l, HID * half + lo:HID * half + lo + n].unsqueeze(1))
               for l in range(DEPTH) for half in range(2) for c, (lo, n) in enumerate(GPART)]
            + [(qk_scale[:, l, 2 * w, :], t[nm][l, :].partition_broadcast(128)) for l in range(DEPTH) for w, nm in enumerate(("L0_ffn_q_scale", "L0_ffn_k_scale"))]
            + [(qk_scale[:, l, 2 * w + 1, 32 * h:32 * h + 32], t[nm][l, 32 - 32 * h:64 - 32 * h].partition_broadcast(128))
               for l in range(DEPTH) for w, nm in enumerate(("L0_ffn_q_scale", "L0_ffn_k_scale")) for h in range(2)],
            "state": [(sB[:, :, :], t["state_b"]), (sC[:, :, :], t["state_c"]), (sD[:, :], t["L0_attn_b_D"].unsqueeze(1)), (sWo[:, :], t["state_wo"]),
                      (sbo[:, :], t["L0_attn_b_b_out"].unsqueeze(0)), (sp_[:, 1:2], t["L0_attn_b_log_dt"].partition_broadcast(128))]
            + [(sp_[64 * h:64 * h + 64, c:c + 1], t[nm].unsqueeze(1)) for h in range(2) for c, nm in ((0, "L0_attn_b_log_Lam_real"), (2, "L0_attn_b_Lam_imag"))],
            "causal": [(cqk[:, :, :, :], t["causal_qk"]), (cv[:, :], t["causal_v"]), (cwo[:, :], t["causal_wo"])],
            "ffn": [(fw1[:, :], t["routed_w1"]), (fb1[:, 0:4], t["L1_ffn_b1_h"].rearrange("(c p) -> p c", c=4)), (fb1[0:64, 4:5], t["L1_ffn_b1_l"].unsqueeze(1)),
                    (fw2[:, 0:4, :], t["routed_w2h"].rearrange("(c p) n -> p c n", c=4)), (fw2[0:64, 4, :], t["routed_w2l"]),
                    (fb2[:, :], t["L1_ffn_b2_h"].unsqueeze(0)), (fw2[64:65, 4, :], t["L1_ffn_b2_l"].unsqueeze(0)),
                    (token[:, :], t["L1_ffn_routing_token"].partition_broadcast(128)),
                    (fgam[:, 0:1], t["L1_ffn_gamma_h"].unsqueeze(1)), (fgam[:, 1:2], t["L1_ffn_gamma_l"].unsqueeze(1))],
            "gates": [(gwn[:, :], t["L1_attn_b_norm_w"].unsqueeze(1)), (gwv[:, :], t["gates_v"]), (gwa[:, :], t["gates_a"]), (gwo[:, :], t["gates_wo"])],
        }
        total = {k: 16 * len(v) for k, v in loads.items()}

        block = ctx.enter_context(nc.Block())

        def bases():
            base = 0
            for stage, run in program:
                yield stage, run, base
                base += B * TILES

        @block.sync
        def _(eng):
            for key in ("x", "tables", "delta", "window", "state"):
                for dst, src in loads[key]:
                    eng.dma_start(dst, src).then_inc(loaded[key], 16)
            for stage, run, base in bases():
                if isinstance(stage, Scan):
                    stage.sync(eng, run, base)
                    for s in range(SLOTS):
                        eng.wait_ge(saved[s], 16 * B * (SCAN_TURNS + 1))
                    for b in range(B):
                        eng.dma_start(hs[:, TILES * b:TILES * b + TILES, :], mixed[b].rearrange("(j t) h m -> t j (h m)", t=T)).then_inc(y_moved, 16)
            eng.wait_ge(slot_free, B * TILES * len(program) + SLOTS)
            for b in range(B):
                eng.dma_start(out[b].rearrange("(j t) d -> t j d", t=T), x[:, TILES * b:TILES * b + TILES, :]).then_inc(stored, 16)
            eng.wait_ge(stored, 16 * B)

        @block.gpsimd
        def _(eng):
            for key in ("causal", "ffn", "gates"):
                for dst, src in loads[key]:
                    eng.dma_start(dst, src).then_inc(loaded[key], 16)
            for s in range(SLOTS):
                for name in ("kT", "v", "hT"):
                    eng.memset(wcv(s, name), 0.0)
            eng.memset(upper_before[:, :, :], 0.0)
            for s in range(SLOTS):
                eng.memset(stat(s, 25), 0.0)
            eng.memset(delta_state[:, :, :], 0.0).then_inc(cleared, 1)
            eng.wait_ge(cleared, 1)
            for stage, run, base in bases():
                stage.pool(eng, run, base)

        @block.scalar
        def _(eng):
            eng.wait_ge(theta_ready, 1)
            eng.activation(turns[:, 1, 1:2], sm[:, 12:13], ACT.Sin)
            eng.activation(turns[:, 0, 1:2], sm[:, 13:14], ACT.Sin).then_inc(tables_act, 1)
            for stage, run, base in bases():
                stage.scalar(eng, run, base)

        @block.tensor
        def _(eng):
            for k in loads:
                eng.wait_ge(loaded[k], total[k])
            eng.wait_ge(prep, 1)
            for stage, run, base in bases():
                stage.tensor(eng, run, base)

        @block.vector
        def _(eng):
            eng.memset(ones_row[:, :], 1.0)
            for k in loads:
                eng.wait_ge(loaded[k], total[k])
            eng.tensor_scalar(dwo[:, :], dwo[:, :], dg[:, 0:1], None, ALU.mult)
            for l in range(DEPTH):
                for j in range(TILES):
                    eng.tensor_tensor(turnt[:, l, j, :, :], turnt[:, l, j, :, :], qk_scale[:, l, :, :], ALU.mult)
            eng.tensor_scalar(fw1[:, 0:HEAVY], fw1[:, 0:HEAVY], fgam[:, 0:1], float(D) ** 0.5, ALU.mult, ALU.mult)
            eng.tensor_scalar(fw1[:, HEAVY:], fw1[:, HEAVY:], fgam[:, 1:2], float(D) ** 0.5, ALU.mult, ALU.mult)
            eng.tensor_scalar(gwa[:, :], gwa[:, :], gwn[:, 0:1], None, ALU.mult)
            eng.tensor_scalar(gwv[:, :], gwv[:, :], gwn[:, 0:1], None, ALU.mult)
            eng.tensor_scalar(sB[:, 1, STATES:], sB[:, 1, STATES:], -1.0, None, ALU.mult)
            eng.tensor_scalar(sC[64:128, 0, :], sC[64:128, 0, :], -1.0, None, ALU.mult)
            eng.tensor_scalar(sC[:, 1, :], sC[:, 1, :], -1.0, None, ALU.mult)
            n = [0]

            def chain(ins):
                n[0] += 1
                ins.then_inc(tables, 1)
                eng.wait_ge(tables, n[0])

            def exp(dst, src, a, b, c, w):
                chain(eng.tensor_scalar(b, src, 87.0, -87.0, ALU.min, ALU.max))
                chain(eng.tensor_scalar(a, b, 1.4426950408889634, 12582912.0, ALU.mult, ALU.add))
                chain(eng.tensor_scalar(a, a, 12582912.0, None, ALU.subtract))
                chain(eng.scalar_tensor_tensor(out=b, in0=a, scalar=-0.693359375, in1=b, op0=ALU.mult, op1=ALU.add))
                chain(eng.scalar_tensor_tensor(out=b, in0=a, scalar=2.12194440e-4, in1=b, op0=ALU.mult, op1=ALU.add))
                chain(eng.tensor_scalar(c, b, 1.0 / 5040, 1.0 / 720, ALU.mult, ALU.add))
                for f in (120.0, 24.0, 6.0, 2.0, 1.0, 1.0):
                    chain(eng.tensor_tensor(c, c, b, ALU.mult))
                    chain(eng.tensor_scalar(c, c, 1.0 / f, None, ALU.add))
                chain(eng.tensor_scalar(a, a, 127.0, 8388608.0, ALU.add, ALU.mult))
                chain(eng.tensor_copy(smi[:, 0:w], a))
                chain(eng.tensor_tensor(dst, c, smi[:, 0:w].bitcast(F32), ALU.mult))

            exp(sm[:, 0:2], sp_[:, 0:2], sm[:, 2:4], sm[:, 4:6], sm[:, 6:8], 2)
            chain(eng.scalar_tensor_tensor(out=sm[:, 8:9], in0=sm[:, 0:1], scalar=-1.0, in1=sm[:, 1:2], op0=ALU.mult, op1=ALU.mult))
            exp(sm[:, 9:10], sm[:, 8:9], sm[:, 2:3], sm[:, 4:5], sm[:, 6:7], 1)
            eng.tensor_scalar(sB[:, :, :], sB[:, :, :], sm[:, 1:2], None, ALU.mult)
            chain(eng.memset(decay[:, :], 1.0))
            chain(eng.tensor_scalar(decay[:, :], decay[:, :], sm[:, 9:10], None, ALU.mult))
            chain(eng.memset(decay[:, :].rearrange("p (b t) -> p b t", b=1)[:, :, 0:1], 0.0))
            chain(eng.tensor_tensor(sm[:, 10:11], sp_[:, 2:3], sm[:, 1:2], ALU.mult))
            chain(eng.tensor_scalar(sm[:, 11:12], sm[:, 10:11], float(1 / (2 * np.pi)), 12582912.0, ALU.mult, ALU.add))
            chain(eng.tensor_scalar(sm[:, 11:12], sm[:, 11:12], 12582912.0, None, ALU.subtract))
            two_pi = 2 * np.pi
            c1 = np.floor(two_pi * 2 ** 8) / 2 ** 8
            c2 = np.floor((two_pi - c1) * 2 ** 20) / 2 ** 20
            for part in (c1, c2, two_pi - c1 - c2):
                chain(eng.scalar_tensor_tensor(out=sm[:, 10:11], in0=sm[:, 11:12], scalar=float(-part), in1=sm[:, 10:11], op0=ALU.mult, op1=ALU.add))
            chain(eng.tensor_scalar(sm[:, 12:13], sm[:, 10:11], 3.1415925, -3.1415925, ALU.min, ALU.max))
            chain(eng.tensor_scalar(sm[:, 14:15], sm[:, 12:13], -1.0, None, ALU.mult))
            chain(eng.tensor_tensor(sm[:, 13:14], sm[:, 14:15], sm[:, 12:13], ALU.min))
            eng.tensor_scalar(sm[:, 13:14], sm[:, 13:14], float(np.pi / 2), None, ALU.add).then_inc(theta_ready, 1)
            eng.wait_ge(tables_act, 1)
            scr = lambda n, w: arena[:, 0, 8192 + 256 * n:8192 + 256 * n + w]
            L = 1
            while L < N:
                m_ = min(L, N - L)
                cL, sL = turns[:, 0, L:L + 1], turns[:, 1, L:L + 1]
                lo = lambda w: turns[:, w, 1:1 + m_]
                chain(eng.tensor_scalar(scr(0, m_), lo(1), sL, None, ALU.mult))
                chain(eng.tensor_scalar(scr(1, m_), lo(1), cL, None, ALU.mult))
                chain(eng.scalar_tensor_tensor(out=turns[:, 0, L + 1:L + 1 + m_], in0=lo(0), scalar=cL, in1=scr(0, m_), op0=ALU.mult, op1=ALU.subtract))
                chain(eng.scalar_tensor_tensor(out=turns[:, 1, L + 1:L + 1 + m_], in0=lo(0), scalar=sL, in1=scr(1, m_), op0=ALU.mult, op1=ALU.add))
                L += m_
            eng.memset(stat(0, 250), 0.0).then_inc(prep, 1)
            eng.wait_ge(prep, 1)
            eng.wait_ge(cleared, 1)
            for _ in range(SLOTS):
                eng.sem_inc(slot_free, 1)
            for stage, run, base in bases():
                stage.vector(eng, run, base)


def kernel(**inputs):
    import concourse.bacc as bacc
    from concourse.bass_utils import run_bass_kernel_spmd

    a = {k: np.ascontiguousarray(v) for k, v in inputs.items()}
    host = dict(constants())
    host["x"] = a["L0_attn_a_x"]
    host["delta_w"] = np.concatenate([a["L0_attn_a_Wq"], a["L0_attn_a_Wk"], a["L0_attn_a_Wv"], a["L0_attn_a_Wbeta"]], axis=1)
    br, bi, cr, ci = (a[f"L0_attn_b_{k}"].T for k in ("B_real", "B_imag", "C_real", "C_imag"))
    host["state_b"] = np.stack([np.concatenate([br, bi], 1), np.concatenate([bi, br], 1)], axis=1)
    host["state_c"] = np.stack([np.concatenate([cr, ci], 0), np.concatenate([ci, cr], 0)], axis=1)
    host["state_wo"] = a["L0_attn_b_W_out"].T
    spread = np.zeros((D, 2, CAUSAL_H, 32), np.float32)
    for n, w in enumerate((a["L1_attn_a_Wq"], a["L1_attn_a_Wk"])):
        spread[:, n, :, :CAUSAL_D] = w.T.reshape(D, CAUSAL_H, CAUSAL_D)
    host["causal_qk"] = spread.reshape(D, 2, 4, 128)
    host["causal_v"], host["causal_wo"] = a["L1_attn_a_Wv"].T, a["L1_attn_a_Wo"].T
    host["routed_w1"] = np.concatenate([a["L1_ffn_w1_h"].T, a["L1_ffn_w1_l"].T, np.zeros((D, 128 - LIGHT), np.float32)], axis=1)
    host["routed_w2h"], host["routed_w2l"] = a["L1_ffn_w2_h"].T, a["L1_ffn_w2_l"].T
    host["gates_v"], host["gates_a"], host["gates_wo"] = a["L1_attn_b_W_v"].T, a["L1_attn_b_W_a"].T, a["L1_attn_b_W_out"].T
    for k in ("L0_attn_a_Wo", "L0_attn_a_g_norm", "L0_ffn_wqkv", "L0_ffn_wo", "L0_ffn_w1", "L0_ffn_ln_g", "L0_ffn_ln_b", "L0_ffn_w2", "L0_ffn_b2",
              "L0_ffn_b1", "L0_ffn_q_scale", "L0_ffn_k_scale", "L0_attn_b_D", "L0_attn_b_b_out", "L0_attn_b_log_dt", "L0_attn_b_log_Lam_real",
              "L0_attn_b_Lam_imag", "L1_ffn_routing_token", "L1_ffn_b1_h", "L1_ffn_b1_l", "L1_ffn_b2_h", "L1_ffn_b2_l", "L1_ffn_gamma_h", "L1_ffn_gamma_l", "L1_attn_b_norm_w"):
        host[k] = a[k]

    nc = bacc.Bacc("TRN2", target_bir_lowering=False, num_devices=1)
    arrays, aps = {}, {}
    for k, v in host.items():
        v = np.ascontiguousarray(v)
        arrays[f"in_{k}"] = v
        aps[k] = nc.dram_tensor(f"in_{k}", v.shape, mybir.dt.from_np(v.dtype), kind="ExternalInput").ap()
    out = nc.dram_tensor("out_0", (B, N, D), F32, kind="ExternalOutput").ap()
    hybrid_layers(nc, aps, out)
    result = run_bass_kernel_spmd(nc, [arrays], core_ids=[0])
    return result.results[0]["out_0"]
```

```python
from contextlib import ExitStack

import numpy as np

import concourse.bass as bass
from concourse import mybir

F32 = mybir.dt.float32
BF16 = mybir.dt.bfloat16
I32 = mybir.dt.int32
ALU = mybir.AluOpType
ACT = mybir.ActivationFunctionType
AX = mybir.AxisListType

B = 8
N = 512
T = 128
TILES = N // T
D = 128
SLOTS = 2
PAIRS = B // SLOTS
BANKS = 8 // SLOTS

DELTA_H, DELTA_D = 4, 32
WIN_H, WIN_D, WINDOW, DEPTH = 8, 64, 64, 2
HID = 341
STATES = 64
KEEP = 128
FETCH = 144
ITERS = 50
CAUSAL_H, CAUSAL_D = 16, 8
LIGHT, HEAVY = 64, 512
SCAN_H, SCAN_M = 8, 16
CELL = SCAN_M + 1
ROWS = SCAN_H * SCAN_M
GATES = ROWS * CELL
CHUNK = 16
CHUNKS = N // CHUNK
BANK_ROWS = 30

LN_EPS = 1e-5
MASKED = -1e30



class Steps:

    def __init__(self, sem, names, turns=PAIRS * TILES, slots=SLOTS):
        self.sem, self.names, self.turns, self.slots = sem, names, turns, slots
        self.at = 0

    def value(self, run, i, name, s):
        i = i.n if isinstance(i, Turn) else i
        per = len(self.names) * self.slots
        return i * per + (run * self.turns * per + self.names.index(name) * self.slots + s + 1)

    def tick(self, name, s):
        assert (self.names[self.at // self.slots], self.at % self.slots) == (name, s), (name, s, self.names[self.at // self.slots])
        self.at = (self.at + 1) % (len(self.names) * self.slots)
        return self.sem


class Turn:

    def __init__(self, pair, j):
        self.pair, self.j, self.n = pair, j, pair * TILES + j

    def tile(self, s):
        return self.pair * (SLOTS * TILES) + self.j + s * TILES


NORM = ["stats", "mean", "var", "xn"]


def constants():
    p, f = np.arange(128)[:, None], np.arange(128)[None, :]
    same = lambda n: p // n == f // n
    masks = [p == f, p < f, p <= f, -(same(2) & (p < f)).astype(np.float32), -(same(2) & (p > f)).astype(np.float32)]
    for n in (2, 4, 8, 16):
        masks.append(same(2 * n) & (p // n < f // n))
    masks.append(p // 32 < f // 32)
    masks.append(p + 1 == f)
    masks.append((p == 127) & (f == 0))
    masks.append(same(32))
    masks = np.stack([m.astype(np.float32) for m in masks], axis=1)
    k = np.arange(WINDOW + T)[None, :] - WINDOW
    seen = (k <= p) & (p - k <= WINDOW)
    window = np.stack([np.tile(np.where(seen & ((k >= 0) | (j > 0)), 0.0, MASKED), (1, 2)) for j in range(TILES)], axis=1)
    causal = np.where(f <= p, 0.0, MASKED)
    bf16 = mybir.dt.np(BF16)
    before = (np.arange(N + 384)[None, :] < 384 + p).astype(np.float32)
    half = np.arange(0, WIN_D, 2, dtype=np.float32)
    inv_freq = (1.0 / np.float32(10000.0) ** (half / np.float32(WIN_D))).astype(np.float32)
    t = np.arange(N, dtype=np.float32)
    freqs = (t[:, None] * inv_freq[None, :]).astype(np.float32)
    base = ((half + np.float32(0.4 * WIN_D)) / np.float32(1.4 * WIN_D)).astype(np.float32)
    power = ((t - N // 2) / np.float32(WINDOW // 2)).astype(np.float32)
    scale = (base[None, :] ** power[:, None]).astype(np.float32)
    cos, sin = np.cos(freqs), np.sin(freqs)
    both = lambda lo, hi: np.concatenate([lo, hi], axis=1)
    rope = np.stack([both(8 * cos * scale, 8 * cos * scale), both(-8 * sin * scale, 8 * sin * scale),
                     both(cos / scale, cos / scale), both(-sin / scale, sin / scale)], axis=1).astype(np.float32)
    rope = rope.reshape(TILES, T, 4, WIN_D).transpose(1, 0, 2, 3)
    pick = np.zeros((B, B, 128), np.float32)
    pick[np.arange(B), np.arange(B), :] = 1.0
    keep = np.tile((np.arange(TILES) < TILES - 1).astype(np.float32), (128, 1))
    return {"masks": masks, "window_mask": window.astype(bf16), "causal_mask": causal.astype(bf16), "eye_bf16": np.eye(128).astype(bf16),
            "before": before.astype(bf16), "rope": rope, "pick": pick, "keep": keep}


M_EYE, M_STRICT, M_UPPER, M_PAIR_U, M_PAIR_L, M_OFF, M_FAR, M_SHIFT, M_LAST, M_HEADS = 0, 1, 2, 3, 4, 5, 9, 10, 11, 12


def hybrid_layers(nc, t, out):
    ctx = ExitStack()
    with ctx:
        ctx.enter_context(nc.allow_non_contiguous_dma(reason="biases and scales, a column of values each"))

        def sb(name, shape, dt=F32):
            return ctx.enter_context(nc.sbuf_tensor(name, shape, dt))

        def sem(name):
            return ctx.enter_context(nc.semaphore(name))

        x = sb("x", [128, B * TILES, D])
        hs = sb("hs", [128, B * TILES, D])
        feedT = sb("feedT", [128, B, N])
        masks = sb("masks", [128, 13, 128])
        window_mask = sb("window_mask", [128, TILES, 2 * (WINDOW + T)], BF16)
        causal_mask = sb("causal_mask", [128, 128], BF16)
        eye_bf16 = sb("eye_bf16", [128, 128], BF16)
        before = sb("before", [128, N + 384], BF16)
        pick = sb("pick", [B, B, 128])
        keep = sb("keep", [128, TILES])
        began = sb("began", [128, TILES])
        ones_row = sb("ones_row", [1, 128])
        dw = sb("dw", [128, 3 * D + DELTA_H])
        dwo = sb("dwo", [128, D])
        dg = sb("dg", [128, 1])
        wqkv = sb("wqkv", [128, DEPTH, 3 * WIN_H * WIN_D])
        wwo = sb("wwo", [128, DEPTH, 4, D])
        qk_scale = sb("qk_scale", [128, DEPTH, 4, WIN_D])
        turnt = sb("turnt", [128, DEPTH, TILES, 4, WIN_D])
        lgb = sb("lgb", [128, DEPTH, 2])
        w1 = sb("w1", [128, DEPTH, 2 * HID])
        w1b = sb("w1b", [128, DEPTH, 6])
        w2 = sb("w2", [128, DEPTH, 3, D])
        sB = sb("sB", [128, 2, 2 * STATES])
        sC = sb("sC", [128, 2, D])
        sD = sb("sD", [128, 1])
        sWo = sb("sWo", [128, D])
        sbo = sb("sbo", [1, D])
        sp_ = sb("sp_", [128, 3])
        turns = sb("turns", [128, 2, N + 1])
        cqk = sb("cqk", [128, 2, 4, 128])
        cv = sb("cv", [128, D])
        cwo = sb("cwo", [128, D])
        fw1 = sb("fw1", [128, HEAVY + 128])
        fgam = sb("fgam", [128, 2])
        fb2 = sb("fb2", [1, D])
        token = sb("token", [128, D])
        scores = sb("scores", [128, B * TILES])
        weight = sb("weight", [128, B * TILES])
        fb1 = sb("fb1", [128, 5])
        fw2 = sb("fw2", [128, 5, D])
        gwn = sb("gwn", [128, 1])
        gwv = sb("gwv", [128, D])
        gwa = sb("gwa", [128, GATES])
        gwo = sb("gwo", [128, D])
        ARENA = 8960
        delta_state = sb("delta_state", [128, SLOTS, 128])
        upper_before = sb("upper_before", [128, SLOTS, 64])
        arena = sb("arena", [128, SLOTS, ARENA])
        small = sb("small", [128, SLOTS, 256])
        minus_half = sb("minus_half", [128, 16])
        P = ctx.enter_context(nc.psum_tensor("P", [128, 8, 512], F32))

        def carve(sizes):
            at, views = 0, {}
            for name, size in sizes:
                views[name] = at, size
                at += size
            assert at <= ARENA, at
            return lambda s, name: arena[:, s, views[name][0]:views[name][0] + views[name][1]]

        def bank(s, k):
            return P[:, BANKS * s + k, :]

        def heads(ap, n):
            return ap.rearrange("p (h d) -> p h d", h=n)

        def over(ap, n, size):
            return ap.unsqueeze(2).broadcast_to([128, n, size])

        def each(ap, n):
            return ap.unsqueeze(1).broadcast_to([ap.shape[0], n, ap.shape[-1]])

        eye = masks[:, M_EYE, :]
        eyeb = eye_bf16[:, :]

        loaded = {k: sem(f"loaded_{k}") for k in ("x", "tables", "delta", "window", "state", "causal", "ffn", "gates")}
        prep = sem("weights_prepared")
        tables = sem("state_tables_step")
        tables_act = sem("state_tables_sine")
        theta_ready = sem("theta_ready")
        cleared = sem("carries_cleared")
        slot_free = sem("slot_free")
        y_moved = sem("scan_output_moved")
        stored = sem("stored")

        ln_act = ["ln", "rs"]
        SV = {}
        def steps(key, names, **kw):
            SV[key] = Steps(sem(key), names, **kw)
            return SV[key]

        done_before = [0]

        def stat(s, a, n=1):
            return small[:, s, a:a + n]

        BN, MV, VAR, RS, TMP, RSTD = 0, 12, 14, 16, 18, 20
        def wait_slots(eng, base, i):
            eng.wait_ge(slot_free, (i.n if isinstance(i, Turn) else i) * SLOTS + (base + SLOTS))

        def settle(eng):
            eng.wait_ge(slot_free, 1)

        def root_pool(eng, v, p, run, i, name, get, done):
            for s in range(SLOTS):
                eng.wait_ge(v.sem, v.value(run, i, name, s))
                eng.tensor_tensor(get(s), get(s), minus_half[:, 0:get(s).shape[-1]], ALU.pow).then_inc(p.tick(done, s), 1)

        def variance(s):
            return stat(s, VAR)

        def norm_vector(eng, v, p, run, i, src, dst, first=None, names=NORM, root="rstd"):
            for s in range(SLOTS):
                if first:
                    first(s)
                parts = src(s)
                for n, part in enumerate(parts):
                    ins = eng.bn_stats(stat(s, BN + 6 * n, 6), part)
                ins.then_inc(v.tick(names[0], s), 1)
            for s in range(SLOTS):
                eng.wait_ge(v.sem, v.value(run, i, names[0], s))
                eng.memset(stat(s, 22), 0.0)
                eng.bn_aggr(stat(s, MV, 2), stat(s, BN, 6 * len(src(s)))).then_inc(v.tick(names[1], s), 1)
            for s in range(SLOTS):
                eng.wait_ge(v.sem, v.value(run, i, names[1], s))
                eng.tensor_scalar(variance(s), stat(s, MV + 1), LN_EPS, None, ALU.add).then_inc(v.tick(names[2], s), 1)
            for s in range(SLOTS):
                eng.wait_ge(p.sem, p.value(run, i, root, s))
                for o, part in zip(dst(s), src(s)):
                    ins = eng.tensor_scalar(o, part, stat(s, MV), variance(s), ALU.subtract, ALU.mult)
                ins.then_inc(v.tick(names[3], s), 1)

        def xb(i, s):
            return x[:, bass.ds(i.tile(s), 1), :]

        def batch(ap, i, s):
            return ap[:, bass.ds(i * SLOTS + s, 1), :]

        def turn_loop(eng, body):
            with eng.Fori(0, PAIRS) as pair:
                with eng.Fori(0, TILES) as j:
                    body(Turn(pair, j))

        def tileT(i, s):
            return feedT[:, :, :].rearrange("p b (j t) -> p (b j) t", j=TILES)[:, bass.ds(i.tile(s), 1), :]

        def pair_loop(eng, body):
            with eng.Fori(0, PAIRS) as i:
                body(i)

        stages = []
        dv = steps("delta_vector", NORM + ["ss", "one_e", "vqk", "beta", "qkn", "kb", "A", "pair", "X2", "vS",
                                           "X4", "X8", "X16", "X32", "R1", "R2", "R3", "oss", "vo", "on", "S1", "S2", "S3"])
        da = steps("delta_scalar", ["xT", "sq", "tT", "M2", "M4", "M8", "M16", "U0", "U1", "U2", "U3", "osq", "oT"])
        dp = steps("delta_pool", ["rstd", "rqk", "off2", "off", "ro"])
        dt_ = steps("delta_tensor", ["xT", "proj", "tT", "grams", "kS", "AX2", "XAX2", "AX4", "XAX4", "AX8", "XAX8", "AX16", "XAX16", "U0",
                                     "AU1", "U1", "AU2", "U2", "AU3", "U3", "O", "KU", "oT", "y"])
        dcv = carve([("xn", 128), ("xT", 128), ("sq", 256), ("qk", 384), ("v", 128), ("tT", 384), ("AT", 512), ("W", 512),
                     ("X", 512), ("XT", 512), ("M", 512), ("off", 2560), ("U", 128), ("R", 128), ("osq", 128), ("on", 128), ("oT", 128)])
        Q8 = lambda s: stat(s, 32, 8)
        O4 = lambda s: stat(s, 72, 4)
        BETA = 64

        def gram(s, n):
            return P[:, BANKS * s:BANKS * s + 4, 128 * n:128 * n + 128]

        class Delta:
            loads = ("x", "tables", "delta")

            def vector(self, eng, run, base):
                def body(i):
                    wait_slots(eng, base, i)
                    norm_vector(eng, dv, dp, run, i, lambda s: [xb(i, s)], lambda s: [dcv(s, "xn")])
                    for s in range(SLOTS):
                        eng.wait_ge(da.sem, da.value(run, i, "sq", s))
                        eng.tensor_reduce(Q8(s), heads(dcv(s, "sq"), 8), AX.X, ALU.add).then_inc(dv.tick("ss", s), 1)
                    for s in range(SLOTS):
                        eng.tensor_scalar(stat(s, BETA, 4), stat(s, BETA, 4), 1.0, None, ALU.add).then_inc(dv.tick("one_e", s), 1)
                    for s in range(SLOTS):
                        eng.wait_ge(dv.sem, dv.value(run, i, "ss", s))
                        eng.tensor_scalar(Q8(s), Q8(s), 1e-24, None, ALU.max).then_inc(dv.tick("vqk", s), 1)
                    for s in range(SLOTS):
                        eng.wait_ge(dv.sem, dv.value(run, i, "one_e", s))
                        eng.reciprocal(stat(s, BETA, 4), stat(s, BETA, 4)).then_inc(dv.tick("beta", s), 1)
                    for s in range(SLOTS):
                        eng.wait_ge(dp.sem, dp.value(run, i, "rqk", s))
                        eng.tensor_tensor(heads(dcv(s, "qk")[:, 0:256], 8), heads(bank(s, 1)[:, 0:256], 8),
                                          over(Q8(s), 8, DELTA_D), ALU.mult).then_inc(dv.tick("qkn", s), 1)
                    for s in range(SLOTS):
                        eng.wait_ge(dv.sem, dv.value(run, i, "qkn", s))
                        eng.tensor_tensor(heads(dcv(s, "v"), 4), heads(bank(s, 1)[:, 256:384], 4),
                                          over(stat(s, BETA, 4), 4, DELTA_D), ALU.mult)
                        eng.tensor_tensor(heads(dcv(s, "qk")[:, 256:384], 4), heads(dcv(s, "qk")[:, 128:256], 4),
                                          over(stat(s, BETA, 4), 4, DELTA_D), ALU.mult).then_inc(dv.tick("kb", s), 1)
                    for s in range(SLOTS):
                        eng.wait_ge(dt_.sem, dt_.value(run, i, "grams", s))
                        eng.tensor_tensor(heads(dcv(s, "AT"), 4), gram(s, 0), each(masks[:, M_STRICT, :], 4), ALU.mult)\
                            .then_inc(dv.tick("A", s), 1)
                    for s in range(SLOTS):
                        eng.wait_ge(dv.sem, dv.value(run, i, "A", s))
                        eng.tensor_tensor(heads(dcv(s, "W"), 4), gram(s, 1), each(masks[:, M_UPPER, :], 4), ALU.mult)
                        eng.tensor_tensor(heads(dcv(s, "X"), 4), gram(s, 2), each(masks[:, M_PAIR_L, :], 4), ALU.mult)
                        eng.tensor_tensor(heads(dcv(s, "XT"), 4), heads(dcv(s, "AT"), 4), each(masks[:, M_PAIR_U, :], 4), ALU.mult)\
                            .then_inc(dv.tick("pair", s), 1)
                    for s in range(SLOTS):
                        eng.wait_ge(dv.sem, dv.value(run, i, "pair", s))
                        eng.tensor_tensor(heads(dcv(s, "X"), 4), heads(dcv(s, "X"), 4), each(eye, 4), ALU.add)
                        eng.tensor_tensor(heads(dcv(s, "XT"), 4), heads(dcv(s, "XT"), 4), each(eye, 4), ALU.add)\
                            .then_inc(dv.tick("X2", s), 1)
                    for s in range(SLOTS):
                        eng.wait_ge(dt_.sem, dt_.value(run, i, "kS", s))
                        eng.tensor_tensor(dcv(s, "v"), dcv(s, "v"), bank(s, 3)[:, 384:512], ALU.subtract).then_inc(dv.tick("vS", s), 1)
                    for n, nn in ((2, 4), (4, 8), (8, 16), (16, 32)):
                        for s in range(SLOTS):
                            eng.wait_ge(dt_.sem, dt_.value(run, i, f"XAX{n}", s))
                            if nn < 32:
                                eng.tensor_tensor(dcv(s, "X"), dcv(s, "X"), bank(s, 1), ALU.subtract)
                            eng.tensor_tensor(dcv(s, "XT"), dcv(s, "XT"), bank(s, 2), ALU.subtract).then_inc(dv.tick(f"X{nn}", s), 1)
                    for n in (1, 2, 3):
                        for s in range(SLOTS):
                            eng.wait_ge(dt_.sem, dt_.value(run, i, f"AU{n}", s))
                            eng.tensor_tensor(dcv(s, "R"), dcv(s, "v"), bank(s, 3)[:, 128:256], ALU.subtract).then_inc(dv.tick(f"R{n}", s), 1)
                    for s in range(SLOTS):
                        eng.wait_ge(da.sem, da.value(run, i, "osq", s))
                        eng.tensor_reduce(O4(s), heads(dcv(s, "osq"), 4), AX.X, ALU.add).then_inc(dv.tick("oss", s), 1)
                    for s in range(SLOTS):
                        eng.wait_ge(dv.sem, dv.value(run, i, "oss", s))
                        eng.tensor_scalar(O4(s), O4(s), LN_EPS, None, ALU.add).then_inc(dv.tick("vo", s), 1)
                    for s in range(SLOTS):
                        eng.wait_ge(dp.sem, dp.value(run, i, "ro", s))
                        eng.tensor_tensor(heads(dcv(s, "on"), 4), heads(bank(s, 0)[:, 0:128], 4),
                                          over(O4(s), 4, DELTA_D), ALU.mult).then_inc(dv.tick("on", s), 1)
                    for s in range(SLOTS):
                        eng.wait_ge(dt_.sem, dt_.value(run, i, "KU", s))
                        eng.tensor_tensor(dcv(s, "R"), bank(s, 3)[:, 256:384], masks[:, M_HEADS, :], ALU.mult).then_inc(dv.tick("S1", s), 1)
                    for s in range(SLOTS):
                        eng.wait_ge(dv.sem, dv.value(run, i, "S1", s))
                        eng.tensor_tensor(dcv(s, "R"), dcv(s, "R"), delta_state[:, s, :], ALU.add).then_inc(dv.tick("S2", s), 1)
                    for s in range(SLOTS):
                        eng.wait_ge(dv.sem, dv.value(run, i, "S2", s))
                        eng.tensor_scalar(delta_state[:, s, :], dcv(s, "R"), keep[:, bass.ds(i.j, 1)], None, ALU.mult).then_inc(dv.tick("S3", s), 1)
                    for s in range(SLOTS):
                        eng.wait_ge(dt_.sem, dt_.value(run, i, "y", s))
                        eng.tensor_tensor(xb(i, s), xb(i, s), bank(s, 2)[:, 0:128], ALU.add).then_inc(slot_free, 1)
                turn_loop(eng, body)

            def scalar(self, eng, run, base):
                def body(i):
                    wait_slots(eng, base, i)
                    for s in range(SLOTS):
                        eng.wait_ge(dt_.sem, dt_.value(run, i, "xT", s))
                        eng.activation(dcv(s, "xT"), bank(s, 0)[:, 0:128], ACT.Copy).then_inc(da.tick("xT", s), 1)
                    for s in range(SLOTS):
                        eng.wait_ge(dt_.sem, dt_.value(run, i, "proj", s))
                        eng.activation(stat(s, BETA, 4), bank(s, 1)[:, 384:388], ACT.Exp, scale=-1.0)
                        eng.activation(dcv(s, "sq"), bank(s, 1)[:, 0:256], ACT.Square).then_inc(da.tick("sq", s), 1)
                    for s in range(SLOTS):
                        eng.wait_ge(dt_.sem, dt_.value(run, i, "tT", s))
                        eng.activation(dcv(s, "tT"), bank(s, 0)[:, 0:384], ACT.Copy).then_inc(da.tick("tT", s), 1)
                    for n in (2, 4, 8, 16):
                        for s in range(SLOTS):
                            eng.wait_ge(dt_.sem, dt_.value(run, i, f"AX{n}", s))
                            eng.activation(dcv(s, "M"), bank(s, 0), ACT.Copy).then_inc(da.tick(f"M{n}", s), 1)
                    for n in (0, 1, 2, 3):
                        for s in range(SLOTS):
                            eng.wait_ge(dt_.sem, dt_.value(run, i, f"U{n}", s))
                            eng.activation(dcv(s, "U"), bank(s, 3)[:, 0:128], ACT.Copy).then_inc(da.tick(f"U{n}", s), 1)
                    for s in range(SLOTS):
                        eng.wait_ge(dt_.sem, dt_.value(run, i, "O", s))
                        eng.activation(dcv(s, "osq"), bank(s, 0)[:, 0:128], ACT.Square, scale=DELTA_D ** -0.5).then_inc(da.tick("osq", s), 1)
                    for s in range(SLOTS):
                        eng.wait_ge(dt_.sem, dt_.value(run, i, "oT", s))
                        eng.activation(dcv(s, "oT"), bank(s, 1)[:, 0:128], ACT.Copy).then_inc(da.tick("oT", s), 1)
                turn_loop(eng, body)

            def pool(self, eng, run, base):
                def body(i):
                    wait_slots(eng, base, i)
                    root_pool(eng, dv, dp, run, i, "var", variance, "rstd")
                    root_pool(eng, dv, dp, run, i, "vqk", Q8, "rqk")
                    for s in range(SLOTS):
                        eng.wait_ge(dv.sem, dv.value(run, i, "A", s))
                        eng.tensor_tensor(heads(dcv(s, "off")[:, 0:512], 4), heads(dcv(s, "AT"), 4), each(masks[:, M_OFF, :], 4), ALU.mult)\
                            .then_inc(dp.tick("off2", s), 1)
                    for s in range(SLOTS):
                        for n in range(1, 5):
                            ins = eng.tensor_tensor(heads(dcv(s, "off")[:, 512 * n:512 * n + 512], 4), heads(dcv(s, "AT"), 4),
                                                    each(masks[:, M_OFF + n, :], 4), ALU.mult)
                        ins.then_inc(dp.tick("off", s), 1)
                    root_pool(eng, dv, dp, run, i, "vo", O4, "ro")
                turn_loop(eng, body)

            def tensor(self, eng, run, base):
                def per_head(out_, lhs, rhs, n=128):
                    for h in range(4):
                        ins = eng.matmul(out_[:, n * h:n * h + n], lhs(h), rhs(h), start=True, stop=True)
                    return ins

                def body(i):
                    wait_slots(eng, base, i)
                    blk = lambda ap, n=128: (lambda h: ap[:, n * h:n * h + n])
                    for s in range(SLOTS):
                        eng.wait_ge(dv.sem, dv.value(run, i, "xn", s))
                        eng.transpose(bank(s, 0)[:, 0:128], dcv(s, "xn"), eye).then_inc(dt_.tick("xT", s), 1)
                    for s in range(SLOTS):
                        eng.wait_ge(da.sem, da.value(run, i, "xT", s))
                        eng.matmul(bank(s, 1)[:, 0:388], dcv(s, "xT"), dw[:, :], start=True, stop=True).then_inc(dt_.tick("proj", s), 1)
                    for s in range(SLOTS):
                        eng.wait_ge(dv.sem, dv.value(run, i, "kb", s))
                        for n in range(3):
                            ins = eng.transpose(bank(s, 0)[:, 128 * n:128 * n + 128], dcv(s, "qk")[:, 128 * n:128 * n + 128], eye)
                        ins.then_inc(dt_.tick("tT", s), 1)
                    for s in range(SLOTS):
                        eng.wait_ge(da.sem, da.value(run, i, "tT", s))
                        row = lambda n: (lambda h: dcv(s, "tT")[32 * h:32 * h + 32, 128 * n:128 * n + 128])
                        for h in range(4):
                            for n, (a, b_) in enumerate(((1, 2), (1, 0), (2, 1))):
                                ins = eng.matmul(bank(s, h)[:, 128 * n:128 * n + 128], row(a)(h), row(b_)(h), start=True, stop=True)
                        ins.then_inc(dt_.tick("grams", s), 1)
                    for n, (lvl, x_) in enumerate(((2, "X2"), (4, "X4"), (8, "X8"), (16, "X16"))):
                        if n == 0:
                            for s in range(SLOTS):
                                eng.wait_ge(dv.sem, dv.value(run, i, "X2", s))
                                eng.matmul(bank(s, 3)[:, 384:512], dcv(s, "tT")[:, 256:384], delta_state[:, s, :], start=True, stop=True)\
                                    .then_inc(dt_.tick("kS", s), 1)
                        for s in range(SLOTS):
                            if n < 2:
                                eng.wait_ge(dp.sem, dp.value(run, i, ("off2", "off")[n], s))
                            eng.wait_ge(dv.sem, dv.value(run, i, x_, s))
                            per_head(bank(s, 0), blk(dcv(s, "off")[:, 512 * n:512 * n + 512]), blk(dcv(s, "X"))).then_inc(dt_.tick(f"AX{lvl}", s), 1)
                        for s in range(SLOTS):
                            eng.wait_ge(da.sem, da.value(run, i, f"M{lvl}", s))
                            if lvl < 16:
                                per_head(bank(s, 1), blk(dcv(s, "XT")), blk(dcv(s, "M")))
                            per_head(bank(s, 2), blk(dcv(s, "M")), blk(dcv(s, "XT"))).then_inc(dt_.tick(f"XAX{lvl}", s), 1)
                    for s in range(SLOTS):
                        eng.wait_ge(dv.sem, dv.value(run, i, "X32", s))
                        per_head(bank(s, 3), blk(dcv(s, "XT")), blk(dcv(s, "v"), 32), 32).then_inc(dt_.tick("U0", s), 1)
                    for n in (1, 2, 3):
                        for s in range(SLOTS):
                            eng.wait_ge(da.sem, da.value(run, i, f"U{n - 1}", s))
                            per_head(bank(s, 3)[:, 128:256], blk(dcv(s, "off")[:, 2048:2560]), blk(dcv(s, "U"), 32), 32)\
                                .then_inc(dt_.tick(f"AU{n}", s), 1)
                        for s in range(SLOTS):
                            eng.wait_ge(dv.sem, dv.value(run, i, f"R{n}", s))
                            per_head(bank(s, 3), blk(dcv(s, "XT")), blk(dcv(s, "R"), 32), 32).then_inc(dt_.tick(f"U{n}", s), 1)
                    for s in range(SLOTS):
                        eng.wait_ge(da.sem, da.value(run, i, "U3", s))
                        eng.matmul(bank(s, 0)[:, 0:128], dcv(s, "tT")[:, 0:128], delta_state[:, s, :], start=True, stop=True)
                        for h in range(4):
                            ins = eng.matmul(bank(s, 0)[:, 32 * h:32 * h + 32], dcv(s, "W")[:, 128 * h:128 * h + 128], dcv(s, "U")[:, 32 * h:32 * h + 32],
                                             start=False, stop=True, skip_group_check=True)
                        ins.then_inc(dt_.tick("O", s), 1)
                    for s in range(SLOTS):
                        eng.matmul(bank(s, 3)[:, 256:384], dcv(s, "qk")[:, 128:256], dcv(s, "U"), start=True, stop=True).then_inc(dt_.tick("KU", s), 1)
                    for s in range(SLOTS):
                        eng.wait_ge(dv.sem, dv.value(run, i, "on", s))
                        eng.transpose(bank(s, 1)[:, 0:128], dcv(s, "on"), eye).then_inc(dt_.tick("oT", s), 1)
                    for s in range(SLOTS):
                        eng.wait_ge(da.sem, da.value(run, i, "oT", s))
                        eng.matmul(bank(s, 2)[:, 0:128], dcv(s, "oT"), dwo[:, :], start=True, stop=True).then_inc(dt_.tick("y", s), 1)
                turn_loop(eng, body)

        NORM2 = ["f" + n for n in NORM]
        win = {}
        for first in (False, True):
            win[first] = (
                steps(f"window{int(first)}_vector", (NORM if first else ["xn"]) + ["hT0", "hT", "q1", "ss", "vqk", "q3", "qn", "kn", "qT", "max",
                                             "rz", "pT", "o", "h2"] + NORM2),
                steps(f"window{int(first)}_scalar", ["vh", "hT", "k", "v", "sq", "kT", "p", "pT", "oT"]),
                steps(f"window{int(first)}_pool", ["rstd"] * first + ["k1", "rqk", "k3", "frstd"]),
                steps(f"window{int(first)}_tensor", ["hT", "qkv", "qkT", "sim", "pT", "o", "oT", "y", "shift", "gT"]))
        KEYS = WINDOW + T
        wcv = carve([("xn", 128), ("hT", T + 1), ("q", 512), ("k", 512), ("v", 512), ("vh", 512), ("t", 512), ("tk", 512),
                     ("qT", 512), ("kT", 4 * KEYS), ("p", 8 * KEYS), ("pT", 1024), ("pTh", 1024), ("h2", 128), ("g", 128)])
        turned = lambda s: wcv(s, "pTh")[:, 0:512]
        wsq = lambda s: wcv(s, "p")[:, 0:1024]
        Q16 = lambda s: stat(s, 32, 16)
        MAX, Z, RZ = 96, 112, 128

        def head_place(h):
            return 2 * (h % 2) + h // 4, h // 2 % 2

        class Window:
            loads = ("tables", "window")

            def __init__(self, first, depth):
                self.first, self.depth = first, depth

            def hb(self, i, s):
                return hs[:, bass.ds(i.tile(s), 1), :]

            def vector(self, eng, run, base):
                wv_, wa, wp, wt = win[self.first]
                rope_at = lambda i, n, a, b: turnt[:, self.depth, bass.ds(i.j, 1), n, a:b].broadcast_to([128, 8, b - a])

                def body(i):
                    wait_slots(eng, base, i)
                    if self.first:
                        norm_vector(eng, wv_, wp, run, i, lambda s: [xb(i, s)], lambda s: [wcv(s, "xn")])
                    else:
                        for s in range(SLOTS):
                            eng.tensor_scalar(wcv(s, "xn"), self.hb(i, s), 1.0, None, ALU.mult).then_inc(wv_.tick("xn", s), 1)
                    for s in range(SLOTS):
                        eng.tensor_scalar(wcv(s, "hT")[64:128, 0:1], wcv(s, "hT")[64:128, T:T + 1], began[64:128, bass.ds(i.j, 1)], None, ALU.mult)\
                            .then_inc(wv_.tick("hT0", s), 1)
                    for s in range(SLOTS):
                        eng.wait_ge(wv_.sem, wv_.value(run, i, "hT0", s))
                        eng.wait_ge(wt.sem, wt.value(run, i, "hT", s))
                        eng.tensor_scalar(wcv(s, "hT")[64:128, 1:129], bank(s, 0)[64:128, 0:128], 1.0, None, ALU.mult).then_inc(wv_.tick("hT", s), 1)
                    for s in range(SLOTS):
                        eng.wait_ge(wt.sem, wt.value(run, i, "qkv", s))
                        raw, q, t_ = heads(bank(s, 1), 8), heads(wcv(s, "q"), 8), heads(wcv(s, "t"), 8)
                        eng.tensor_tensor(t_[:, :, 0:32], raw[:, :, 32:64], rope_at(i, 1, 0, 32), ALU.mult)
                        eng.tensor_tensor(t_[:, :, 32:64], raw[:, :, 0:32], rope_at(i, 1, 32, 64), ALU.mult)
                        eng.tensor_tensor(q, raw, rope_at(i, 0, 0, 64), ALU.mult).then_inc(wv_.tick("q1", s), 1)
                    for s in range(SLOTS):
                        eng.wait_ge(wa.sem, wa.value(run, i, "sq", s))
                        eng.tensor_reduce(Q16(s), heads(wsq(s), 16), AX.X, ALU.add).then_inc(wv_.tick("ss", s), 1)
                    for s in range(SLOTS):
                        eng.wait_ge(wv_.sem, wv_.value(run, i, "ss", s))
                        eng.tensor_scalar(Q16(s), Q16(s), 1e-24, None, ALU.max).then_inc(wv_.tick("vqk", s), 1)
                    for s in range(SLOTS):
                        eng.tensor_tensor(wcv(s, "q"), wcv(s, "q"), wcv(s, "t"), ALU.add).then_inc(wv_.tick("q3", s), 1)
                    for s in range(SLOTS):
                        eng.wait_ge(wv_.sem, wv_.value(run, i, "q3", s))
                        eng.wait_ge(wp.sem, wp.value(run, i, "rqk", s))
                        eng.tensor_tensor(heads(wcv(s, "q"), 8), heads(wcv(s, "q"), 8), over(Q16(s)[:, 0:8], 8, WIN_D), ALU.mult)\
                            .then_inc(wv_.tick("qn", s), 1)
                    for s in range(SLOTS):
                        eng.wait_ge(wp.sem, wp.value(run, i, "k3", s))
                        eng.tensor_tensor(heads(turned(s), 8), heads(turned(s), 8), over(Q16(s)[:, 8:16], 8, WIN_D), ALU.mult)\
                            .then_inc(wv_.tick("kn", s), 1)
                    for s in range(SLOTS):
                        eng.wait_ge(wt.sem, wt.value(run, i, "qkT", s))
                        eng.tensor_copy(wcv(s, "qT"), bank(s, 0)).then_inc(wv_.tick("qT", s), 1)
                    for s in range(SLOTS):
                        eng.wait_ge(wt.sem, wt.value(run, i, "sim", s))
                        for n in range(4):
                            ins = eng.tensor_reduce(stat(s, MAX + 2 * n, 2), heads(bank(s, n)[:, 0:2 * KEYS], 2), AX.X, ALU.max, negate=True)
                        ins.then_inc(wv_.tick("max", s), 1)
                    for s in range(SLOTS):
                        eng.wait_ge(wa.sem, wa.value(run, i, "p", s))
                        eng.reciprocal(stat(s, RZ, 8), stat(s, Z, 8)).then_inc(wv_.tick("rz", s), 1)
                    for s in range(SLOTS):
                        eng.wait_ge(wt.sem, wt.value(run, i, "pT", s))
                        eng.tensor_copy(wcv(s, "pT")[:, 0:512], bank(s, 0))
                        eng.tensor_copy(wcv(s, "pTh")[0:64, 0:512], bank(s, 2)[0:64, :]).then_inc(wv_.tick("pT", s), 1)
                    for s in range(SLOTS):
                        eng.wait_ge(wt.sem, wt.value(run, i, "o", s))
                        eng.tensor_tensor(heads(wcv(s, "q"), 8), heads(bank(s, 0), 8), over(stat(s, RZ, 8), 8, WIN_D), ALU.mult)\
                            .then_inc(wv_.tick("o", s), 1)
                    for s in range(SLOTS):
                        eng.wait_ge(wt.sem, wt.value(run, i, "y", s))
                        eng.tensor_tensor(wcv(s, "h2"), wcv(s, "xn"), bank(s, 2)[:, 0:128], ALU.add).then_inc(wv_.tick("h2", s), 1)

                    def ready(s):
                        eng.wait_ge(wt.sem, wt.value(run, i, "shift", s))
                        eng.tensor_scalar(self.hb(i, s), wcv(s, "h2"), 1.0, None, ALU.mult)
                        eng.tensor_scalar(upper_before[:, s, :], wcv(s, "h2")[:, 64:128], keep[:, bass.ds(i.j, 1)], None, ALU.mult)
                    norm_vector(eng, wv_, wp, run, i, lambda s: [wcv(s, "h2")[:, 0:64], bank(s, 3)[:, 0:64]],
                                lambda s: [wcv(s, "g")[:, 0:64], wcv(s, "g")[:, 64:128]], first=ready, names=NORM2, root="frstd")
                    for s in range(SLOTS):
                        eng.wait_ge(wt.sem, wt.value(run, i, "gT", s))
                        eng.tensor_scalar(tileT(i, s), bank(s, 3)[:, 128:256], lgb[:, self.depth, 0:1],
                                          lgb[:, self.depth, 1:2], ALU.mult, ALU.add).then_inc(slot_free, 1)
                turn_loop(eng, body)

            def scalar(self, eng, run, base):
                wv_, wa, wp, wt = win[self.first]
                def body(i):
                    wait_slots(eng, base, i)
                    for s in range(SLOTS):
                        eng.activation(heads(wcv(s, "kT"), 4)[:, :, 0:WINDOW], heads(wcv(s, "kT"), 4)[:, :, T:KEYS], ACT.Copy)
                        eng.activation(wcv(s, "vh")[0:64, :], wcv(s, "v")[64:128, :], ACT.Copy).then_inc(wa.tick("vh", s), 1)
                    for s in range(SLOTS):
                        eng.wait_ge(wt.sem, wt.value(run, i, "hT", s))
                        eng.activation(wcv(s, "hT")[0:64, 0:T], bank(s, 0)[0:64, 0:128], ACT.Copy).then_inc(wa.tick("hT", s), 1)
                    for s in range(SLOTS):
                        eng.wait_ge(wt.sem, wt.value(run, i, "qkv", s))
                        eng.activation(wcv(s, "k"), bank(s, 2), ACT.Copy).then_inc(wa.tick("k", s), 1)
                    for s in range(SLOTS):
                        eng.wait_ge(wa.sem, wa.value(run, i, "vh", s))
                        eng.activation(wcv(s, "v"), bank(s, 3), ACT.Copy).then_inc(wa.tick("v", s), 1)
                    for s in range(SLOTS):
                        eng.activation(wsq(s)[:, 512:1024], bank(s, 2), ACT.Square)
                        eng.wait_ge(wv_.sem, wv_.value(run, i, "q1", s))
                        eng.activation(wsq(s)[:, 0:512], bank(s, 1), ACT.Square).then_inc(wa.tick("sq", s), 1)
                    for s in range(SLOTS):
                        eng.wait_ge(wt.sem, wt.value(run, i, "qkT", s))
                        eng.activation(heads(wcv(s, "kT"), 4)[:, :, WINDOW:KEYS], heads(bank(s, 1), 4), ACT.Copy).then_inc(wa.tick("kT", s), 1)
                    for s in range(SLOTS):
                        eng.wait_ge(wv_.sem, wv_.value(run, i, "max", s))
                        for h in range(WIN_H):
                            n, c = head_place(h)
                            ins = eng.activation(wcv(s, "p")[:, KEYS * h:KEYS * h + KEYS], bank(s, n)[:, KEYS * c:KEYS * c + KEYS],
                                                 ACT.Exp, bias=stat(s, MAX + 2 * n + c), accum_out=stat(s, Z + h))
                        ins.then_inc(wa.tick("p", s), 1)
                    for s in range(SLOTS):
                        eng.wait_ge(wt.sem, wt.value(run, i, "pT", s))
                        eng.activation(wcv(s, "pT")[:, 512:1024], bank(s, 1), ACT.Copy)
                        eng.activation(wcv(s, "pTh")[0:64, 512:1024], bank(s, 3)[0:64, :], ACT.Copy).then_inc(wa.tick("pT", s), 1)
                    for s in range(SLOTS):
                        eng.wait_ge(wt.sem, wt.value(run, i, "oT", s))
                        eng.activation(wcv(s, "t"), bank(s, 1), ACT.Copy).then_inc(wa.tick("oT", s), 1)
                turn_loop(eng, body)

            def pool(self, eng, run, base):
                wv_, wa, wp, wt = win[self.first]
                rope_at = lambda i, n, a, b: turnt[:, self.depth, bass.ds(i.j, 1), n, a:b].broadcast_to([128, 8, b - a])

                def body(i):
                    wait_slots(eng, base, i)
                    if self.first:
                        root_pool(eng, wv_, wp, run, i, "var", variance, "rstd")
                    for s in range(SLOTS):
                        eng.wait_ge(wa.sem, wa.value(run, i, "k", s))
                        eng.tensor_tensor(stat(s, 24), stat(s, 25), stat(s, 25), ALU.mult)
                        k, t_ = heads(wcv(s, "k"), 8), heads(wcv(s, "tk"), 8)
                        eng.tensor_tensor(t_[:, :, 0:32], k[:, :, 32:64], rope_at(i, 3, 0, 32), ALU.mult)
                        eng.tensor_tensor(t_[:, :, 32:64], k[:, :, 0:32], rope_at(i, 3, 32, 64), ALU.mult)
                        eng.tensor_tensor(heads(turned(s), 8), k, rope_at(i, 2, 0, 64), ALU.mult).then_inc(wp.tick("k1", s), 1)
                    root_pool(eng, wv_, wp, run, i, "vqk", Q16, "rqk")
                    for s in range(SLOTS):
                        eng.wait_ge(wp.sem, wp.value(run, i, "k1", s))
                        eng.tensor_tensor(turned(s), turned(s), wcv(s, "tk"), ALU.add).then_inc(wp.tick("k3", s), 1)
                    root_pool(eng, wv_, wp, run, i, "fvar", variance, "frstd")
                turn_loop(eng, body)

            def tensor(self, eng, run, base):
                wv_, wa, wp, wt = win[self.first]
                def body(i):
                    wait_slots(eng, base, i)
                    for s in range(SLOTS):
                        eng.wait_ge(wv_.sem, wv_.value(run, i, "xn", s))
                        eng.transpose(bank(s, 0)[:, 0:128], wcv(s, "xn"), eye).then_inc(wt.tick("hT", s), 1)
                    for s in range(SLOTS):
                        eng.wait_ge(wv_.sem, wv_.value(run, i, "hT", s))
                        eng.wait_ge(wa.sem, wa.value(run, i, "hT", s))
                        for n in range(3):
                            ins = eng.matmul(bank(s, 1 + n), wcv(s, "hT")[:, 0:T], wqkv[:, self.depth, 512 * n:512 * n + 512], start=True, stop=True)
                        ins.then_inc(wt.tick("qkv", s), 1)
                    for s in range(SLOTS):
                        eng.wait_ge(wv_.sem, wv_.value(run, i, "qn", s))
                        for n in range(4):
                            eng.transpose(bank(s, 0)[:, 128 * n:128 * n + 128], wcv(s, "q")[:, 128 * n:128 * n + 128], eye)
                        eng.wait_ge(wv_.sem, wv_.value(run, i, "kn", s))
                        for n in range(4):
                            ins = eng.transpose(bank(s, 1)[:, 128 * n:128 * n + 128], turned(s)[:, 128 * n:128 * n + 128], eye)
                        ins.then_inc(wt.tick("qkT", s), 1)
                    for s in range(SLOTS):
                        eng.wait_ge(wa.sem, wa.value(run, i, "kT", s))
                        eng.wait_ge(wv_.sem, wv_.value(run, i, "qT", s))
                        for n in range(4):
                            eng.matmul(bank(s, n)[:, 0:2 * KEYS], eyeb, window_mask[:, bass.ds(i.j, 1), :], start=True, stop=True)
                        for h in range(WIN_H):
                            (n, c), r, at = head_place(h), 64 * (h % 2), h // 2
                            ins = eng.matmul(bank(s, n)[:, KEYS * c:KEYS * c + KEYS], wcv(s, "qT")[r:r + 64, 128 * at:128 * at + 128],
                                             wcv(s, "kT")[r:r + 64, KEYS * at:KEYS * at + KEYS], start=False, stop=True, skip_group_check=True)
                        ins.then_inc(wt.tick("sim", s), 1)
                    for s in range(SLOTS):
                        eng.wait_ge(wa.sem, wa.value(run, i, "p", s))
                        for h in range(8):
                            c = 128 * (h % 4)
                            eng.transpose(bank(s, h // 4)[:, c:c + 128], wcv(s, "p")[:, KEYS * h + WINDOW:KEYS * h + KEYS], eye)
                            ins = eng.transpose(bank(s, 2 + h // 4)[0:64, c:c + 128], wcv(s, "p")[:, KEYS * h:KEYS * h + WINDOW], eye)
                        ins.then_inc(wt.tick("pT", s), 1)
                    for s in range(SLOTS):
                        eng.wait_ge(wv_.sem, wv_.value(run, i, "pT", s))
                        eng.wait_ge(wa.sem, wa.value(run, i, "pT", s))
                        for h in range(8):
                            o = bank(s, 0)[:, 64 * h:64 * h + 64]
                            eng.matmul(o, wcv(s, "pT")[:, 128 * h:128 * h + 128], wcv(s, "v")[:, 64 * h:64 * h + 64], start=True, stop=False)
                            ins = eng.matmul(o, wcv(s, "pTh")[0:64, 128 * h:128 * h + 128], wcv(s, "vh")[0:64, 64 * h:64 * h + 64], start=False, stop=True)
                        ins.then_inc(wt.tick("o", s), 1)
                    for s in range(SLOTS):
                        eng.wait_ge(wv_.sem, wv_.value(run, i, "o", s))
                        for n in range(4):
                            ins = eng.transpose(bank(s, 1)[:, 128 * n:128 * n + 128], wcv(s, "q")[:, 128 * n:128 * n + 128], eye)
                        ins.then_inc(wt.tick("oT", s), 1)
                    for s in range(SLOTS):
                        eng.wait_ge(wa.sem, wa.value(run, i, "oT", s))
                        for n in range(4):
                            ins = eng.matmul(bank(s, 2)[:, 0:128], wcv(s, "t")[:, 128 * n:128 * n + 128], wwo[:, self.depth, n, :],
                                             start=n == 0, stop=n == 3)
                        ins.then_inc(wt.tick("y", s), 1)
                    for s in range(SLOTS):
                        eng.wait_ge(wv_.sem, wv_.value(run, i, "h2", s))
                        eng.matmul(bank(s, 3)[:, 0:64], masks[:, M_LAST, :], upper_before[:, s, :], start=True, stop=False)
                        eng.matmul(bank(s, 3)[:, 0:64], masks[:, M_SHIFT, :], wcv(s, "h2")[:, 64:128], start=False, stop=True)\
                            .then_inc(wt.tick("shift", s), 1)
                    for s in range(SLOTS):
                        eng.wait_ge(wv_.sem, wv_.value(run, i, "fxn", s))
                        eng.transpose(bank(s, 3)[:, 128:256], wcv(s, "g"), eye).then_inc(wt.tick("gT", s), 1)
                turn_loop(eng, body)

        GPART = [(0, 128), (128, 128), (256, HID - 256)]
        glu = {last: (steps(f"glu{int(last)}_vector", ["u0", "u1", "u2"] + ["h"] * last, turns=PAIRS),
                      steps(f"glu{int(last)}_scalar", ["gelu0", "gelu1", "gelu2"], turns=PAIRS),
                      steps(f"glu{int(last)}_tensor", ["ag0", "ag1", "ag2", "y"], turns=PAIRS)) for last in (False, True)}
        glu_ones = sem("glu_ones")
        gcv = carve([("u", 3 * 512), ("g", 2 * 512)])

        def tiles_of(ap, i, s):
            return ap[:, bass.ds(i * (SLOTS * TILES) + s * TILES, TILES), :]

        class Glu:
            loads = ("window",)

            def __init__(self, depth, last):
                self.depth, self.last = depth, last

            def vector(self, eng, run, base):
                gv, ga, gt = glu[self.last]
                eng.wait_ge(slot_free, base + SLOTS)
                for s in range(SLOTS):
                    ins = eng.memset(gcv(s, "u")[:, 1024:1536], 1.0)
                ins.then_inc(glu_ones, 1)
                eng.wait_ge(glu_ones, 2 * run + self.last + 1)

                def body(i):
                    for c, (lo, n) in enumerate(GPART):
                        for s in range(SLOTS):
                            eng.wait_ge(ga.sem, ga.value(run, i, f"gelu{c}", s))
                            eng.scalar_tensor_tensor(out=gcv(s, "u")[0:n, 512 * c:512 * c + 512], in0=bank(s, 2 * (c % 2))[0:n, :],
                                                     scalar=w1b[0:n, self.depth, c:c + 1], in1=gcv(s, "g")[0:n, 512 * (c % 2):512 * (c % 2) + 512],
                                                     op0=ALU.add, op1=ALU.mult).then_inc(gv.tick(f"u{c}", s), 1)
                    for s in range(SLOTS):
                        eng.wait_ge(gt.sem, gt.value(run, i, "y", s))
                        eng.tensor_tensor(tiles_of(hs, i, s), tiles_of(hs, i, s), heads(bank(s, 2), TILES), ALU.add)\
                            .then_inc(gv.tick("h", s) if self.last else slot_free, 1 if self.last else TILES)
                    if self.last:
                        for s in range(SLOTS):
                            eng.wait_ge(gv.sem, gv.value(run, i, "h", s))
                            eng.tensor_tensor(tiles_of(x, i, s), tiles_of(x, i, s), tiles_of(hs, i, s), ALU.add).then_inc(slot_free, TILES)
                pair_loop(eng, body)

            def scalar(self, eng, run, base):
                gv, ga, gt = glu[self.last]

                def body(i):
                    for c, (lo, n) in enumerate(GPART):
                        for s in range(SLOTS):
                            if c == 2:
                                eng.wait_ge(gv.sem, gv.value(run, i, "u0", s))
                            eng.wait_ge(gt.sem, gt.value(run, i, f"ag{c}", s))
                            eng.activation(gcv(s, "g")[0:n, 512 * (c % 2):512 * (c % 2) + 512], bank(s, 2 * (c % 2) + 1)[0:n, :], ACT.Gelu,
                                           bias=w1b[0:n, self.depth, 3 + c:4 + c]).then_inc(ga.tick(f"gelu{c}", s), 1)
                pair_loop(eng, body)

            def pool(self, eng, run, base):
                pass

            def tensor(self, eng, run, base):
                gv, ga, gt = glu[self.last]
                eng.wait_ge(slot_free, base + SLOTS)

                def body(i):
                    eng.wait_ge(slot_free, i * (SLOTS * TILES) + (base + SLOTS))
                    for c, (lo, n) in enumerate(GPART):
                        for s in range(SLOTS):
                            if c == 2:
                                eng.wait_ge(gv.sem, gv.value(run, i, "u0", s))
                            for half in range(2):
                                ins = eng.matmul(bank(s, 2 * (c % 2) + half)[0:n, :], w1[:, self.depth, HID * half + lo:HID * half + lo + n],
                                                 batch(feedT, i, s), start=True, stop=True)
                            ins.then_inc(gt.tick(f"ag{c}", s), 1)
                    for s in range(SLOTS):
                        eng.wait_ge(gv.sem, gv.value(run, i, "u2", s))
                        for b in range(TILES):
                            for c, (lo, n) in enumerate(GPART):
                                n += c == 2
                                ins = eng.matmul(bank(s, 2)[:, 128 * b:128 * b + 128], gcv(s, "u")[0:n, 512 * c + 128 * b:512 * c + 128 * b + 128],
                                                 w2[0:n, self.depth, c, :], start=c == 0, stop=c == 2)
                        ins.then_inc(gt.tick("y", s), 1)
                pair_loop(eng, body)

        feed = {kind: (steps(f"feed_{kind}_vector", NORM + ["tok"] * (kind == "routed") + ["vms", "xr"] * (kind != "plain")
                                     + ["score"] * (kind == "routed")),
                       steps(f"feed_{kind}_scalar", ["ss"]),
                       steps(f"feed_{kind}_pool", ["rstd"] + ["rms"] * (kind != "plain")),
                       steps(f"feed_{kind}_tensor", ["T"])) for kind in ("plain", "gates", "routed")}
        fcv = carve([("xn", 128), ("sq", 128), ("xr", 128), ("tk", 128)])
        R1 = lambda s: stat(s, 32)

        class Feed:
            loads = ("tables",)

            def __init__(self, kind, rms):
                self.kind, self.rms = kind, rms

            def vector(self, eng, run, base):
                fv, fa, fp, ft = feed[self.kind]
                def body(i):
                    wait_slots(eng, base, i)
                    norm_vector(eng, fv, fp, run, i, lambda s: [xb(i, s)], lambda s: [fcv(s, "xn")])
                    if self.kind == "routed":
                        for s in range(SLOTS):
                            eng.wait_ge(fv.sem, fv.value(run, i, "xn", s))
                            eng.tensor_tensor_reduce(out=fcv(s, "tk"), in0=fcv(s, "xn"), in1=token[:, :], scale=1.0, scalar=0.0, op0=ALU.mult,
                                                     op1=ALU.add, accum_out=stat(s, 40)).then_inc(fv.tick("tok", s), 1)
                    if self.rms:
                        scale, offset, least = self.rms
                        for s in range(SLOTS):
                            eng.wait_ge(fa.sem, fa.value(run, i, "ss", s))
                            if least:
                                eng.tensor_scalar(R1(s), R1(s), least, None, ALU.max).then_inc(fv.tick("vms", s), 1)
                            else:
                                eng.tensor_scalar(R1(s), R1(s), offset, None, ALU.add).then_inc(fv.tick("vms", s), 1)
                        for s in range(SLOTS):
                            eng.wait_ge(fp.sem, fp.value(run, i, "rms", s))
                            eng.tensor_scalar(fcv(s, "xr"), fcv(s, "xn"), R1(s), None, ALU.mult).then_inc(fv.tick("xr", s), 1)
                    if self.kind == "routed":
                        for s in range(SLOTS):
                            eng.wait_ge(fv.sem, fv.value(run, i, "tok", s))
                            eng.tensor_scalar(scores[:, bass.ds(i.tile(s), 1)], stat(s, 40), 1.0, None, ALU.mult).then_inc(fv.tick("score", s), 1)
                    for s in range(SLOTS):
                        eng.wait_ge(ft.sem, ft.value(run, i, "T", s))
                        if self.kind == "gates":
                            eng.tensor_tensor(xb(i, s), xb(i, s), fcv(s, "xn"), ALU.add)
                        eng.tensor_scalar(tileT(i, s), bank(s, 0)[:, 0:128], 1.0, None, ALU.mult).then_inc(slot_free, 1)
                turn_loop(eng, body)

            def scalar(self, eng, run, base):
                fv, fa, fp, ft = feed[self.kind]
                def body(i):
                    wait_slots(eng, base, i)
                    if self.rms:
                        for s in range(SLOTS):
                            eng.wait_ge(fv.sem, fv.value(run, i, "xn", s))
                            eng.activation(fcv(s, "sq"), fcv(s, "xn"), ACT.Square, scale=self.rms[0] ** 0.5, accum_out=R1(s)).then_inc(fa.tick("ss", s), 1)
                turn_loop(eng, body)

            def pool(self, eng, run, base):
                fv, fa, fp, ft = feed[self.kind]
                def body(i):
                    wait_slots(eng, base, i)
                    root_pool(eng, fv, fp, run, i, "var", variance, "rstd")
                    if self.rms:
                        root_pool(eng, fv, fp, run, i, "vms", R1, "rms")
                turn_loop(eng, body)

            def tensor(self, eng, run, base):
                fv, fa, fp, ft = feed[self.kind]
                def body(i):
                    wait_slots(eng, base, i)
                    for s in range(SLOTS):
                        eng.wait_ge(fv.sem, fv.value(run, i, "xr" if self.rms else "xn", s))
                        eng.transpose(bank(s, 0)[:, 0:128], fcv(s, "xr" if self.rms else "xn"), eye).then_inc(ft.tick("T", s), 1)
                turn_loop(eng, body)

        sv = steps("state_vector", ["cu", "su", "u", "scan", "p", "y"], turns=PAIRS)
        spl = steps("state_pool", ["q"], turns=PAIRS)
        st = steps("state_tensor", ["u", "y", "out"], turns=PAIRS)
        scv = carve([("a", 512), ("b", 512), ("g", 512), ("p", 512), ("q", 512), ("y", 512)])
        sm = sb("sm", [128, 24])
        smi = sb("smi", [128, 2], I32)
        decay = sb("decay", [128, N])

        class State:
            loads = ("state",)

            def vector(self, eng, run, base):
                eng.wait_ge(slot_free, base + SLOTS)
                cos, sin = turns[:, 0, 1:N + 1], turns[:, 1, 1:N + 1]

                def body(i):
                    for s in range(SLOTS):
                        eng.wait_ge(st.sem, st.value(run, i, "u", s))
                        eng.tensor_tensor(scv(s, "a"), bank(s, 0), cos, ALU.mult).then_inc(sv.tick("cu", s), 1)
                    for s in range(SLOTS):
                        eng.tensor_tensor(scv(s, "b"), bank(s, 1), sin, ALU.mult).then_inc(sv.tick("su", s), 1)
                    for s in range(SLOTS):
                        eng.wait_ge(sv.sem, sv.value(run, i, "su", s))
                        eng.tensor_tensor(scv(s, "a"), scv(s, "a"), scv(s, "b"), ALU.add).then_inc(sv.tick("u", s), 1)
                    for s in range(SLOTS):
                        eng.wait_ge(sv.sem, sv.value(run, i, "u", s))
                        eng.tensor_tensor_scan(scv(s, "g"), decay[:, :], scv(s, "a"), 0.0, ALU.mult, ALU.add).then_inc(sv.tick("scan", s), 1)
                    for s in range(SLOTS):
                        eng.wait_ge(sv.sem, sv.value(run, i, "scan", s))
                        eng.tensor_tensor(scv(s, "p"), scv(s, "g"), cos, ALU.mult).then_inc(sv.tick("p", s), 1)
                    for s in range(SLOTS):
                        eng.wait_ge(st.sem, st.value(run, i, "y", s))
                        eng.scalar_tensor_tensor(out=scv(s, "y"), in0=batch(feedT, i, s), scalar=sD[:, 0:1], in1=bank(s, 2),
                                                 op0=ALU.mult, op1=ALU.add).then_inc(sv.tick("y", s), 1)
                    for s in range(SLOTS):
                        eng.wait_ge(st.sem, st.value(run, i, "out", s))
                        eng.tensor_tensor(tiles_of(x, i, s), tiles_of(x, i, s), heads(bank(s, 3), TILES), ALU.add).then_inc(slot_free, TILES)
                pair_loop(eng, body)

            def scalar(self, eng, run, base):
                pass

            def pool(self, eng, run, base):
                def body(i):
                    for s in range(SLOTS):
                        eng.wait_ge(sv.sem, sv.value(run, i, "scan", s))
                        eng.tensor_tensor(scv(s, "q"), scv(s, "g"), turns[:, 1, 1:N + 1], ALU.mult).then_inc(spl.tick("q", s), 1)
                pair_loop(eng, body)

            def tensor(self, eng, run, base):
                def body(i):
                    eng.wait_ge(slot_free, i * (SLOTS * TILES) + (base + SLOTS))
                    for s in range(SLOTS):
                        eng.matmul(bank(s, 0), sB[:, 0, :], batch(feedT, i, s), start=True, stop=True)
                        eng.matmul(bank(s, 1), sB[:, 1, :], batch(feedT, i, s), start=True, stop=True).then_inc(st.tick("u", s), 1)
                    for s in range(SLOTS):
                        eng.wait_ge(sv.sem, sv.value(run, i, "p", s))
                        eng.matmul(bank(s, 2), sC[:, 0, :], scv(s, "p"), start=True, stop=False)
                        eng.wait_ge(spl.sem, spl.value(run, i, "q", s))
                        eng.matmul(bank(s, 2), sC[:, 1, :], scv(s, "q"), start=False, stop=True).then_inc(st.tick("y", s), 1)
                    for s in range(SLOTS):
                        eng.wait_ge(sv.sem, sv.value(run, i, "y", s))
                        for b in range(TILES):
                            eng.matmul(bank(s, 3)[:, 128 * b:128 * b + 128], scv(s, "y")[:, 128 * b:128 * b + 128], sWo[:, :], start=True, stop=False)
                            ins = eng.matmul(bank(s, 3)[:, 128 * b:128 * b + 128], ones_row[:, :], sbo[:, :], start=False, stop=True)
                        ins.then_inc(st.tick("out", s), 1)
                pair_loop(eng, body)

        QUADS = 4
        cvv = steps("causal_vector", NORM + ["qT"])
        ca = steps("causal_scalar", ["xT", "kT", "v"])
        cp = steps("causal_pool", ["rstd"])
        ct = steps("causal_tensor", ["xT", "q", "kv"])
        ccv = carve([("xn", 128), ("xT", 128), ("qT", 512 * TILES), ("kT", 512 * TILES), ("v", 128 * TILES), ("p", 4 * N), ("pT", 4 * N)])
        cvv2 = steps("attend_vector", [x_ for j in range(TILES) for q in range(QUADS) for x_ in (f"max{j}{q}", f"pT{j}{q}", f"rz{j}{q}", f"o{j}{q}")], turns=PAIRS)
        ca2 = steps("attend_scalar", [x_ for j in range(TILES) for x_ in [y_ for q in range(QUADS) for y_ in (f"p{j}{q}", f"pT{j}{q}")] + [f"oT{j}"]], turns=PAIRS)
        ct2 = steps("attend_tensor", [x_ for j in range(TILES) for x_ in [y_ for q in range(QUADS) for y_ in (f"sim{j}{q}", f"pT{j}{q}", f"o{j}{q}")] + [f"oT{j}", f"y{j}"]], turns=PAIRS)
        CMAX, CZ, CRZ = 96, 112, 128
        c_scale = CAUSAL_D ** -0.5

        class Causal:
            loads = ("tables", "causal")

            def vector(self, eng, run, base):
                with eng.Fori(0, PAIRS) as pair:
                    for j in range(TILES):
                        i = Turn(pair, j)
                        if j == 0:
                            eng.wait_ge(slot_free, pair * (SLOTS * TILES) + (base + SLOTS))
                        norm_vector(eng, cvv, cp, run, i, lambda s: [xb(i, s)], lambda s: [ccv(s, "xn")])
                        for s in range(SLOTS):
                            eng.wait_ge(ct.sem, ct.value(run, i, "q", s))
                            eng.tensor_scalar(ccv(s, "qT")[:, 512 * j:512 * j + 512], bank(s, 1), c_scale, None, ALU.mult).then_inc(cvv.tick("qT", s), 1)
                    for j in range(TILES):
                        keys = T * (j + 1)
                        for q in range(QUADS):
                            for s in range(SLOTS):
                                eng.wait_ge(ct2.sem, ct2.value(run, pair, f"sim{j}{q}", s))
                                for h in range(4):
                                    ins = eng.tensor_reduce(stat(s, CMAX + h), bank(s, h)[:, 0:keys], AX.X, ALU.max, negate=True)
                                ins.then_inc(cvv2.tick(f"max{j}{q}", s), 1)
                            for s in range(SLOTS):
                                eng.wait_ge(ct2.sem, ct2.value(run, pair, f"pT{j}{q}", s))
                                for h in range(2):
                                    ins = eng.tensor_copy(ccv(s, "pT")[:, N * h:N * h + keys], bank(s, h)[:, 0:keys])
                                ins.then_inc(cvv2.tick(f"pT{j}{q}", s), 1)
                            for s in range(SLOTS):
                                eng.wait_ge(ca2.sem, ca2.value(run, pair, f"p{j}{q}", s))
                                eng.reciprocal(stat(s, CRZ, 4), stat(s, CZ, 4)).then_inc(cvv2.tick(f"rz{j}{q}", s), 1)
                            for s in range(SLOTS):
                                eng.wait_ge(ct2.sem, ct2.value(run, pair, f"o{j}{q}", s))
                                eng.wait_ge(cvv2.sem, cvv2.value(run, pair, f"rz{j}{q}", s))
                                eng.tensor_tensor(heads(ccv(s, "xn")[:, 32 * q:32 * q + 32], 4), heads(bank(s, 0)[:, 0:32], 4),
                                                  over(stat(s, CRZ, 4), 4, CAUSAL_D), ALU.mult).then_inc(cvv2.tick(f"o{j}{q}", s), 1)
                        for s in range(SLOTS):
                            eng.wait_ge(ct2.sem, ct2.value(run, pair, f"y{j}", s))
                            eng.tensor_tensor(xb(Turn(pair, j), s), xb(Turn(pair, j), s), bank(s, 2)[:, 0:128], ALU.add).then_inc(slot_free, 1)

            def scalar(self, eng, run, base):
                with eng.Fori(0, PAIRS) as pair:
                    for j in range(TILES):
                        i = Turn(pair, j)
                        for s in range(SLOTS):
                            eng.wait_ge(ct.sem, ct.value(run, i, "xT", s))
                            eng.activation(ccv(s, "xT"), bank(s, 0)[:, 0:128], ACT.Copy).then_inc(ca.tick("xT", s), 1)
                        for s in range(SLOTS):
                            eng.wait_ge(ct.sem, ct.value(run, i, "kv", s))
                            eng.activation(ccv(s, "kT")[:, 512 * j:512 * j + 512], bank(s, 2), ACT.Copy).then_inc(ca.tick("kT", s), 1)
                        for s in range(SLOTS):
                            eng.activation(ccv(s, "v")[:, 128 * j:128 * j + 128], bank(s, 3)[:, 0:128], ACT.Copy).then_inc(ca.tick("v", s), 1)
                    for j in range(TILES):
                        keys = T * (j + 1)
                        for q in range(QUADS):
                            for s in range(SLOTS):
                                eng.wait_ge(cvv2.sem, cvv2.value(run, pair, f"max{j}{q}", s))
                                for h in range(4):
                                    ins = eng.activation(ccv(s, "p")[:, N * h:N * h + keys], bank(s, h)[:, 0:keys], ACT.Exp, bias=stat(s, CMAX + h),
                                                         accum_out=stat(s, CZ + h))
                                ins.then_inc(ca2.tick(f"p{j}{q}", s), 1)
                            for s in range(SLOTS):
                                eng.wait_ge(ct2.sem, ct2.value(run, pair, f"pT{j}{q}", s))
                                for h in range(2, 4):
                                    ins = eng.activation(ccv(s, "pT")[:, N * h:N * h + keys], bank(s, h)[:, 0:keys], ACT.Copy)
                                ins.then_inc(ca2.tick(f"pT{j}{q}", s), 1)
                        for s in range(SLOTS):
                            eng.wait_ge(ct2.sem, ct2.value(run, pair, f"oT{j}", s))
                            eng.activation(ccv(s, "xT"), bank(s, 1)[:, 0:128], ACT.Copy).then_inc(ca2.tick(f"oT{j}", s), 1)

            def pool(self, eng, run, base):
                with eng.Fori(0, PAIRS) as pair:
                    for j in range(TILES):
                        root_pool(eng, cvv, cp, run, Turn(pair, j), "var", variance, "rstd")

            def tensor(self, eng, run, base):
                with eng.Fori(0, PAIRS) as pair:
                    for j in range(TILES):
                        i = Turn(pair, j)
                        if j == 0:
                            eng.wait_ge(slot_free, pair * (SLOTS * TILES) + (base + SLOTS))
                        for s in range(SLOTS):
                            eng.wait_ge(cvv.sem, cvv.value(run, i, "xn", s))
                            eng.transpose(bank(s, 0)[:, 0:128], ccv(s, "xn"), eye).then_inc(ct.tick("xT", s), 1)
                        for s in range(SLOTS):
                            eng.wait_ge(ca.sem, ca.value(run, i, "xT", s))
                            if j:
                                eng.wait_ge(cvv.sem, cvv.value(run, Turn(pair, j - 1), "qT", s))
                            for n in range(4):
                                ins = eng.matmul(bank(s, 1)[:, 128 * n:128 * n + 128], cqk[:, 0, n, :], ccv(s, "xT"), start=True, stop=True)
                            ins.then_inc(ct.tick("q", s), 1)
                        for s in range(SLOTS):
                            if j:
                                eng.wait_ge(ca.sem, ca.value(run, Turn(pair, j - 1), "v", s))
                            for n in range(4):
                                eng.matmul(bank(s, 2)[:, 128 * n:128 * n + 128], cqk[:, 1, n, :], ccv(s, "xT"), start=True, stop=True)
                            eng.matmul(bank(s, 3)[:, 0:128], ccv(s, "xT"), cv[:, :], start=True, stop=True).then_inc(ct.tick("kv", s), 1)
                    for j in range(TILES):
                        for q in range(QUADS):
                            for s in range(SLOTS):
                                if j == 0 and q == 0:
                                    eng.wait_ge(cvv.sem, cvv.value(run, Turn(pair, TILES - 1), "qT", s))
                                    eng.wait_ge(ca.sem, ca.value(run, Turn(pair, TILES - 1), "v", s))
                                elif q:
                                    eng.wait_ge(cvv2.sem, cvv2.value(run, pair, f"o{j}{q - 1}", s))
                                else:
                                    eng.wait_ge(slot_free, pair * (SLOTS * TILES) + (base + SLOTS * j + s + 1))
                                for h in range(4):
                                    for k in range(j + 1):
                                        o = bank(s, h)[:, 128 * k:128 * k + 128]
                                        ins = eng.matmul(o, ccv(s, "qT")[32 * h:32 * h + 32, 512 * j + 128 * q:512 * j + 128 * q + 128],
                                                         ccv(s, "kT")[32 * h:32 * h + 32, 512 * k + 128 * q:512 * k + 128 * q + 128], start=True, stop=k < j)
                                        if k == j:
                                            ins = eng.matmul(o, eyeb, causal_mask[:, :], start=False, stop=True)
                                ins.then_inc(ct2.tick(f"sim{j}{q}", s), 1)
                            for s in range(SLOTS):
                                eng.wait_ge(ca2.sem, ca2.value(run, pair, f"p{j}{q}", s))
                                for h in range(4):
                                    for k in range(j + 1):
                                        ins = eng.transpose(bank(s, h)[:, 128 * k:128 * k + 128], ccv(s, "p")[:, N * h + 128 * k:N * h + 128 * k + 128], eye)
                                ins.then_inc(ct2.tick(f"pT{j}{q}", s), 1)
                            for s in range(SLOTS):
                                eng.wait_ge(cvv2.sem, cvv2.value(run, pair, f"pT{j}{q}", s))
                                eng.wait_ge(ca2.sem, ca2.value(run, pair, f"pT{j}{q}", s))
                                for h in range(4):
                                    for k in range(j + 1):
                                        at = 128 * k + 32 * q + 8 * h
                                        ins = eng.matmul(bank(s, 0)[:, 8 * h:8 * h + 8], ccv(s, "pT")[:, N * h + 128 * k:N * h + 128 * k + 128],
                                                         ccv(s, "v")[:, at:at + 8], start=k == 0, stop=k == j)
                                ins.then_inc(ct2.tick(f"o{j}{q}", s), 1)
                        for s in range(SLOTS):
                            eng.wait_ge(cvv2.sem, cvv2.value(run, pair, f"o{j}{QUADS - 1}", s))
                            eng.transpose(bank(s, 1)[:, 0:128], ccv(s, "xn"), eye).then_inc(ct2.tick(f"oT{j}", s), 1)
                        for s in range(SLOTS):
                            eng.wait_ge(ca2.sem, ca2.value(run, pair, f"oT{j}", s))
                            eng.matmul(bank(s, 2)[:, 0:128], ccv(s, "xT"), cwo[:, :], start=True, stop=True).then_inc(ct2.tick(f"y{j}", s), 1)

        RPART = [128, 128, 128, 128, LIGHT]
        rv = steps("routed_vector", ["light"], turns=PAIRS)
        ra = steps("routed_scalar", [f"gelu{c}" for c in range(5)], turns=PAIRS)
        rt = steps("routed_tensor", [f"h{c}" for c in range(5)] + ["y"], turns=PAIRS)
        rcv = carve([("u", 5 * 512)])
        rset = sem("routed_ones")
        descent_in = sem("descent_scores")
        dd = sem("descent_vector")
        dac = sem("descent_scalar")
        key_T = sem("descent_back")
        key_cols = sem("descent_columns")
        row_out = sem("rank_row")
        rank_done = sem("rank_step")
        route = sb("route", [B, 12])
        LMAX, NA, MX, ZS, LZ, NMX = 0, 1, 2, 3, 4, 5
        picked = sb("picked", [128, 2, TILES, B])
        rank = sb("rank", [128, 2, 2])
        S_ = lambda: arena[0:B, 0, 0:N]
        T_ = lambda: arena[0:B, 0, N:2 * N]
        E_ = lambda: arena[0:B, 0, 2 * N:3 * N]
        K_ = lambda: arena[0:B, 0, 3 * N:4 * N]
        W_ = lambda: arena[0:B, 0, 4 * N:5 * N]
        CMP = lambda g: arena[:, 0, (5 + g) * N:(6 + g) * N]
        LOGK = float(np.log(np.float32(FETCH)))
        RANKS = B * TILES

        class Routed:
            loads = ("ffn",)

            def vector(self, eng, run, base):
                n = [run * DESCENT]

                def link(ins):
                    n[0] += 1
                    ins.then_inc(dd, 1)
                    eng.wait_ge(dd, n[0])

                eng.wait_ge(slot_free, base + SLOTS)
                for s in range(SLOTS):
                    ins = eng.memset(rcv(s, "u")[64:128, 2048:2560], 1.0)
                ins.then_inc(rset, 1)
                eng.wait_ge(rset, run + 1)
                eng.wait_ge(descent_in, run + 1)
                eng.tensor_copy(S_(), P[0:B, 0, :]).then_inc(dd, 1)
                n[0] += 1
                eng.wait_ge(dd, n[0])
                link(eng.tensor_reduce(route[:, LMAX:LMAX + 1], S_(), AX.X, ALU.max))
                eng.memset(route[:, NA:NA + 1], float(np.log(np.float32(N))) - LOGK)
                eng.memset(route[:, MX:MX + 1], 0.0).then_inc(dd, 1)
                n[0] += 1
                eng.wait_ge(dd, n[0])
                link(eng.tensor_tensor(route[:, MX:MX + 1], route[:, LMAX:LMAX + 1], route[:, NA:NA + 1], ALU.min))
                start = n[0]
                with eng.Fori(0, ITERS - 1) as it:
                    eng.tensor_scalar(T_(), S_(), route[:, NA:NA + 1], route[:, MX:MX + 1], ALU.min, ALU.subtract).then_inc(dd, 1)
                    eng.wait_ge(dac, it * 2 + (run * 2 * (ITERS - 1) + 2))
                    eng.scalar_tensor_tensor(out=route[:, NA:NA + 1], in0=route[:, LZ:LZ + 1], scalar=-LOGK, in1=route[:, MX:MX + 1],
                                             op0=ALU.add, op1=ALU.add).then_inc(dd, 1)
                    eng.wait_ge(dd, it * 3 + (start + 2))
                    eng.tensor_tensor(route[:, MX:MX + 1], route[:, LMAX:LMAX + 1], route[:, NA:NA + 1], ALU.min).then_inc(dd, 1)
                    eng.wait_ge(dd, it * 3 + (start + 3))
                n[0] = start + 3 * (ITERS - 1)
                link(eng.tensor_scalar(T_(), S_(), route[:, NA:NA + 1], 0.0, ALU.subtract, ALU.min))
                link(eng.scalar_tensor_tensor(out=K_(), in0=T_(), scalar=-2.0 ** -25, in1=T_(), op0=ALU.is_lt, op1=ALU.mult))
                eng.wait_ge(exp_key, run + 1)
                link(eng.tensor_scalar(T_(), E_(), -1.0, 1.0, ALU.mult, ALU.add))
                link(eng.tensor_tensor(W_(), T_(), E_(), ALU.add))
                assert n[0] == run * DESCENT + DESCENT, (n[0], DESCENT)
                eng.wait_ge(key_T, run + 1)
                eng.tensor_copy(picked[:, :, :, :].rearrange("p a j b -> p (a j b)"), P[:, 1, 0:2 * TILES * B]).then_inc(key_cols, 1)
                eng.wait_ge(key_cols, run + 1)
                for b in range(B):
                    for j in range(TILES):
                        m = b * TILES + j
                        if j == 0:
                            eng.wait_ge(row_out, run * B + b + 1)
                        row = P[:, 2 + b % 2, :]
                        key = picked[:, 0, j, b:b + 1]
                        g = m % 2
                        eng.tensor_scalar(CMP(0), row, key, 0.0, ALU.is_gt, ALU.add, accum_out=rank[:, g, 0:1])
                        eng.scalar_tensor_tensor(out=CMP(1), in0=row, scalar=key, in1=before[:, 384 - 128 * j:384 - 128 * j + N],
                                                 op0=ALU.is_equal, op1=ALU.mult, accum_out=rank[:, g, 1:2]).then_inc(rank_done, 1)
                        eng.wait_ge(rank_done, (run * RANKS + m) * 3 + 1)
                        eng.tensor_tensor(rank[:, g, 0:1], rank[:, g, 0:1], rank[:, g, 1:2], ALU.add).then_inc(rank_done, 1)
                        eng.wait_ge(rank_done, (run * RANKS + m) * 3 + 2)
                        eng.scalar_tensor_tensor(out=weight[:, m:m + 1], in0=rank[:, g, 0:1], scalar=float(KEEP), in1=picked[:, 1, j, b:b + 1],
                                                 op0=ALU.is_lt, op1=ALU.mult).then_inc(rank_done, 1)
                eng.wait_ge(rank_done, (run + 1) * RANKS * 3)

                def body(i):
                    for s in range(SLOTS):
                        eng.wait_ge(rt.sem, rt.value(run, i, "y", s))
                        eng.tensor_tensor(tiles_of(x, i, s), tiles_of(x, i, s), heads(bank(s, 3), TILES), ALU.add).then_inc(rv.tick("light", s), 1)
                    for s in range(SLOTS):
                        eng.wait_ge(rv.sem, rv.value(run, i, "light", s))
                        for k in range(TILES):
                            at = i * (SLOTS * TILES) + (s * TILES + k)
                            ins = eng.scalar_tensor_tensor(out=x[:, bass.ds(at, 1), :], in0=bank(s, 0)[:, 128 * k:128 * k + 128],
                                                           scalar=weight[:, bass.ds(at, 1)], in1=x[:, bass.ds(at, 1), :], op0=ALU.mult, op1=ALU.add)
                        ins.then_inc(slot_free, TILES)
                pair_loop(eng, body)

            def scalar(self, eng, run, base):
                first = run * DESCENT + 4
                eng.preload_act_table_set("natural_log_exp_and_others")
                with eng.Fori(0, ITERS - 1) as it:
                    eng.wait_ge(dd, it * 3 + (first + 1))
                    eng.activation(E_(), T_(), ACT.Exp, accum_out=route[:, ZS:ZS + 1]).then_inc(dac, 1)
                    eng.wait_ge(dac, it * 2 + (run * 2 * (ITERS - 1) + 1))
                    eng.activation(route[:, LZ:LZ + 1], route[:, ZS:ZS + 1], ACT.Ln).then_inc(dac, 1)
                eng.wait_ge(dd, first + 3 * (ITERS - 1) + 2)
                eng.activation(E_(), K_(), ACT.Exp).then_inc(exp_key, 1)
                eng.wait_ge(rank_done, (run + 1) * RANKS * 3)

                def body(i):
                    for c, n in enumerate(RPART):
                        for s in range(SLOTS):
                            eng.wait_ge(rt.sem, rt.value(run, i, f"h{c}", s))
                            eng.activation(rcv(s, "u")[0:n, 512 * c:512 * c + 512], bank(s, c % 3)[0:n, :], ACT.Gelu,
                                           bias=fb1[0:n, c:c + 1]).then_inc(ra.tick(f"gelu{c}", s), 1)
                pair_loop(eng, body)

            def pool(self, eng, run, base):
                pass

            def tensor(self, eng, run, base):
                eng.wait_ge(slot_free, base + SLOTS)
                for j in range(TILES):
                    ins = eng.transpose(P[0:B, 0, 128 * j:128 * j + 128], scores[:, :].rearrange("p (b j) -> p j b", j=TILES)[:, j, :], eye)
                ins.then_inc(descent_in, 1)
                eng.wait_ge(dd, run * DESCENT + DESCENT)
                for a, src in enumerate((K_(), W_())):
                    for j in range(TILES):
                        at = (a * TILES + j) * B
                        ins = eng.transpose(P[:, 1, at:at + B], src[:, 128 * j:128 * j + 128], masks[0:B, M_EYE, 0:B])
                ins.then_inc(key_T, 1)
                for b in range(B):
                    if b >= 2:
                        eng.wait_ge(rank_done, (run * RANKS + (b - 1) * TILES) * 3)
                    eng.matmul(P[:, 2 + b % 2, :], pick[:, b, :], K_(), start=True, stop=True).then_inc(row_out, 1)
                eng.wait_ge(rank_done, (run + 1) * RANKS * 3)

                def body(i):
                    eng.wait_ge(slot_free, i * (SLOTS * TILES) + (base + SLOTS))
                    for c, n in enumerate(RPART):
                        for s in range(SLOTS):
                            if c >= 3:
                                eng.wait_ge(ra.sem, ra.value(run, i, f"gelu{c - 3}", s))
                            eng.matmul(bank(s, c % 3), fw1[:, 128 * c:128 * c + 128], batch(feedT, i, s), start=True, stop=True)\
                                .then_inc(rt.tick(f"h{c}", s), 1)
                    for s in range(SLOTS):
                        eng.wait_ge(ra.sem, ra.value(run, i, "gelu4", s))
                        for b in range(TILES):
                            u = lambda c, n: rcv(s, "u")[0:n, 512 * c + 128 * b:512 * c + 128 * b + 128]
                            eng.matmul(bank(s, 3)[:, 128 * b:128 * b + 128], u(4, LIGHT + 1), fw2[0:LIGHT + 1, 4, :], start=True, stop=True)
                            heavy = bank(s, 0)[:, 128 * b:128 * b + 128]
                            for c in range(4):
                                eng.matmul(heavy, u(c, 128), fw2[:, c, :], start=c == 0, stop=False)
                            ins = eng.matmul(heavy, ones_row[:, :], fb2[:, :], start=False, stop=True)
                        ins.then_inc(rt.tick("y", s), 1)
                pair_loop(eng, body)

        DESCENT = 8 + 3 * (ITERS - 1)
        exp_key = sem("descent_exponential")

        SCAN_TURNS = CHUNKS // SLOTS
        gates_vector = sem("gates_vector")
        gates_scalar = sem("gates_scalar")
        gates_pool = sem("gates_pool")
        gates_tensor = sem("gates_tensor")
        GATE_STEPS = {"max": (gates_vector, 4, 1), "less": (gates_vector, 4, 2), "z": (gates_vector, 4, 3), "rz": (gates_vector, 4, 4),
                      "in": (gates_scalar, 3, 1), "v": (gates_scalar, 3, 2), "e": (gates_scalar, 3, 3),
                      "g": (gates_pool, 2, 1), "gv": (gates_pool, 2, 2), "logits": (gates_tensor, 1, 1)}

        def gates_wait(eng, i, name, s, turns_back=0):
            sem_, per, at = GATE_STEPS[name]
            eng.wait_ge(sem_, i * (SLOTS * per) + (SLOTS * per * (1 - turns_back) + per * s + at))

        mcv = carve([("e", GATES), ("in", 128), ("v", 128), ("mx", 128), ("z", 128), ("rz", 128), ("ring", CHUNK * SCAN_M * CELL)])
        chains = B * SCAN_H
        states = sb("states", [chains, SLOTS, CHUNK + 1, SCAN_M])
        chunk_done = sem("chunk_scanned")
        moved_out = [sem(f"gates_out_{s}") for s in range(SLOTS)]
        moved = [sem(f"gates_moved_{s}") for s in range(SLOTS)]
        saved = [sem(f"states_saved_{s}") for s in range(SLOTS)]
        step_done = sem("scan_step")
        saving = sem("states_being_saved")
        BANKED = [(n * BANK_ROWS, min(BANK_ROWS, ROWS - n * BANK_ROWS)) for n in range(-(-ROWS // BANK_ROWS))]
        gates_dram = nc.dram_tensor("gates_by_chain", [SLOTS, B, SCAN_H, CHUNK, SCAN_M * CELL], F32).ap()
        mixed = nc.dram_tensor("scan_by_token", [B, N, SCAN_H, SCAN_M], F32).ap()
        STEPS = 2 * CHUNK + 1

        MOVES = 16 * B

        class Scan:

            def vector(self, eng, run, base):
                eng.wait_ge(slot_free, base + SLOTS)
                eng.memset(states[:, :, :, :], 0.0).then_inc(chunk_done, 1)
                eng.wait_ge(chunk_done, 1)
                eng.sem_inc(chunk_done, 1)
                eng.sem_inc(step_done, 1)
                for sem_, per in ((gates_vector, 4), (gates_scalar, 3), (gates_pool, 2), (gates_tensor, 1)):
                    eng.sem_inc(sem_, SLOTS * per)
                view = lambda n, k: P[:, n, 0:CELL * k].rearrange("p (r c) -> p r c", c=CELL)

                def less_max(i, s):
                    gates_wait(eng, i, "logits", s)
                    for n, (lo, k) in enumerate(BANKED):
                        ins = eng.tensor_reduce(mcv(s, "mx")[:, lo:lo + k], view(n, k), AX.X, ALU.max)
                    ins.then_inc(gates_vector, 1)
                    gates_wait(eng, i, "max", s)
                    eng.wait_ge(moved_out[s], i * MOVES + MOVES)
                    for n, (lo, k) in enumerate(BANKED):
                        ins = eng.tensor_tensor(mcv(s, "e")[:, CELL * lo:CELL * (lo + k)].rearrange("p (r c) -> p r c", c=CELL), view(n, k),
                                                over(mcv(s, "mx")[:, lo:lo + k], k, CELL), ALU.subtract)
                    ins.then_inc(gates_vector, 1)

                def sums(i, s):
                    gates_wait(eng, i, "e", s)
                    eng.tensor_reduce(mcv(s, "z"), heads(mcv(s, "e"), ROWS), AX.X, ALU.add).then_inc(gates_vector, 1)
                    gates_wait(eng, i, "z", s)
                    eng.reciprocal(mcv(s, "rz"), mcv(s, "z")).then_inc(gates_vector, 1)

                def scan(i, s):
                    eng.wait_ge(moved[s], i * MOVES + 2 * MOVES)
                    eng.wait_ge(saved[s], i * MOVES + MOVES)
                    ring = mcv(s, "ring").rearrange("p (t r c) -> p t r c", t=CHUNK, c=CELL)
                    at = (i * SLOTS + s) * STEPS
                    eng.wait_ge(step_done, at + 1)
                    eng.tensor_copy(states[:, s, 0, :], states[:, 1 - s, CHUNK, :]).then_inc(step_done, 1)
                    for k in range(CHUNK):
                        eng.wait_ge(step_done, at + (2 * k + 2))
                        eng.tensor_tensor(ring[0:chains, k, :, 1:CELL], ring[0:chains, k, :, 1:CELL],
                                          each(states[:, s, k, :], SCAN_M), ALU.mult).then_inc(step_done, 1)
                        eng.wait_ge(step_done, at + (2 * k + 3))
                        eng.tensor_reduce(states[:, s, k + 1, :], ring[0:chains, k, :, :], AX.X, ALU.add).then_inc(step_done, 1)
                    eng.wait_ge(step_done, at + STEPS + 1)
                    eng.sem_inc(chunk_done, 1)

                for s in range(SLOTS):
                    less_max(0, s)
                    sums(0, s)
                with eng.Fori(0, SCAN_TURNS - 1) as i:
                    for s in range(SLOTS):
                        less_max(i + 1, s)
                        scan(i, s)
                        sums(i + 1, s)
                for s in range(SLOTS):
                    scan(SCAN_TURNS - 1, s)
                eng.wait_ge(y_moved, 16 * B)
                eng.sem_inc(slot_free, B * TILES)

            def scalar(self, eng, run, base):
                eng.wait_ge(slot_free, base + SLOTS)
                with eng.Fori(0, SCAN_TURNS) as i:
                    for s in range(SLOTS):
                        gates_wait(eng, i, "logits", s, 1)
                        eng.activation(mcv(s, "in").rearrange("p (b t) -> p b t", b=B), feedT[:, :, bass.ds((i * SLOTS + s) * CHUNK, CHUNK)],
                                       ACT.Copy).then_inc(gates_scalar, 1)
                        gates_wait(eng, i, "logits", s)
                        gates_wait(eng, i, "gv", s, 1)
                        eng.activation(mcv(s, "v"), P[:, 5, 0:128], ACT.Copy).then_inc(gates_scalar, 1)
                        gates_wait(eng, i, "less", s)
                        eng.activation(mcv(s, "e"), mcv(s, "e"), ACT.Exp).then_inc(gates_scalar, 1)

            def pool(self, eng, run, base):
                with eng.Fori(0, SCAN_TURNS) as i:
                    for s in range(SLOTS):
                        gates_wait(eng, i, "rz", s)
                        eng.tensor_tensor(heads(mcv(s, "e"), ROWS), heads(mcv(s, "e"), ROWS), over(mcv(s, "rz"), ROWS, CELL), ALU.mult)\
                            .then_inc(gates_pool, 1)
                        gates_wait(eng, i, "g", s)
                        first = heads(mcv(s, "e"), ROWS)[:, :, 0:1]
                        eng.tensor_tensor(first, first, mcv(s, "v").unsqueeze(2), ALU.mult).then_inc(gates_pool, 1)

            def sync(self, eng, run, base):
                eng.wait_ge(slot_free, base + SLOTS)
                for s in range(SLOTS):
                    eng.sem_inc(saved[s], MOVES)
                    eng.sem_inc(moved[s], MOVES)
                    eng.sem_inc(moved_out[s], MOVES)

                def save(c, s):
                    for b in range(B):
                        eng.dma_start(mixed[b, bass.ds(c * CHUNK, CHUNK), :, :].rearrange("t h m -> h t m"),
                                      states[SCAN_H * b:SCAN_H * b + SCAN_H, s, 1:CHUNK + 1, :]).then_inc(saved[s], 16)

                def body(i, first):
                    for s in range(SLOTS):
                        gates_wait(eng, i, "gv", s)
                        eng.sem_inc(saving, 1)
                        eng.wait_ge(moved[s], i * MOVES + MOVES)
                        for b in range(B):
                            eng.dma_start(gates_dram[s, b].rearrange("h t e -> t h e"),
                                          mcv(s, "e")[CHUNK * b:CHUNK * b + CHUNK, :].rearrange("t (h e) -> t h e", h=SCAN_H)).then_inc(moved_out[s], 16)
                        eng.wait_ge(chunk_done, i * SLOTS + (s + 1))
                        eng.sem_inc(saving, 1)
                        if not first:
                            save(i * SLOTS + (s - SLOTS), s)
                        eng.wait_ge(moved_out[s], i * MOVES + 2 * MOVES)
                        for b in range(B):
                            eng.dma_start(mcv(s, "ring")[SCAN_H * b:SCAN_H * b + SCAN_H, :].rearrange("h (t e) -> h t e", t=CHUNK),
                                          gates_dram[s, b]).then_inc(moved[s], 16)

                body(0, True)
                with eng.Fori(1, SCAN_TURNS) as i:
                    body(i, False)
                for s in range(SLOTS):
                    eng.wait_ge(chunk_done, CHUNKS + s + 1)
                    save(CHUNKS - SLOTS + s, s)

            def tensor(self, eng, run, base):
                eng.wait_ge(slot_free, base + SLOTS)
                with eng.Fori(0, SCAN_TURNS) as i:
                    for s in range(SLOTS):
                        gates_wait(eng, i, "in", s)
                        gates_wait(eng, i, "less", 1 - s, 1 - s)
                        gates_wait(eng, i, "v", 1 - s, 1 - s)
                        for n, (lo, k) in enumerate(BANKED):
                            eng.matmul(P[:, n, 0:CELL * k], mcv(s, "in"), gwa[:, CELL * lo:CELL * (lo + k)], start=True, stop=True)
                        eng.matmul(P[:, 5, 0:128], mcv(s, "in"), gwv[:, :], start=True, stop=True).then_inc(gates_tensor, 1)

        ov = steps("mix_vector", ["in"])
        oa = steps("mix_scalar", ["T"])
        ot = steps("mix_tensor", ["T", "y"])
        ocv = carve([("in", 128), ("T", 128)])

        class Mix:
            loads = ()

            def vector(self, eng, run, base):
                def body(i):
                    wait_slots(eng, base, i)
                    for s in range(SLOTS):
                        eng.tensor_scalar(ocv(s, "in"), hs[:, bass.ds(i.tile(s), 1), :], 1.0, None, ALU.mult).then_inc(ov.tick("in", s), 1)
                    for s in range(SLOTS):
                        eng.wait_ge(ot.sem, ot.value(run, i, "y", s))
                        eng.tensor_tensor(xb(i, s), xb(i, s), bank(s, 1)[:, 0:128], ALU.add).then_inc(slot_free, 1)
                turn_loop(eng, body)

            def scalar(self, eng, run, base):
                def body(i):
                    for s in range(SLOTS):
                        eng.wait_ge(ot.sem, ot.value(run, i, "T", s))
                        eng.activation(ocv(s, "T"), bank(s, 0)[:, 0:128], ACT.Copy).then_inc(oa.tick("T", s), 1)
                turn_loop(eng, body)

            def pool(self, eng, run, base):
                pass

            def tensor(self, eng, run, base):
                def body(i):
                    wait_slots(eng, base, i)
                    for s in range(SLOTS):
                        eng.wait_ge(ov.sem, ov.value(run, i, "in", s))
                        eng.transpose(bank(s, 0)[:, 0:128], ocv(s, "in"), eye).then_inc(ot.tick("T", s), 1)
                    for s in range(SLOTS):
                        eng.wait_ge(oa.sem, oa.value(run, i, "T", s))
                        eng.matmul(bank(s, 1)[:, 0:128], ocv(s, "T"), gwo[:, :], start=True, stop=True).then_inc(ot.tick("y", s), 1)
                turn_loop(eng, body)

        rms_norm = (1.0, None, 1e-24)
        rms_mean = (1.0 / D, LN_EPS, None)
        program = [
            (Delta(), 0),
            (Window(True, 0), 0), (Glu(0, False), 0), (Window(False, 1), 0), (Glu(1, True), 0),
            (Feed("plain", None), 0), (State(), 0),
            (Window(True, 0), 1), (Glu(0, False), 1), (Window(False, 1), 1), (Glu(1, True), 1),
            (Causal(), 0),
            (Feed("routed", rms_norm), 0), (Routed(), 0),
            (Feed("gates", rms_mean), 0), (Scan(), 0), (Mix(), 0),
            (Feed("routed", rms_norm), 1), (Routed(), 1),
        ]

        loads = {
            "x": [(x[:, TILES * b:TILES * b + TILES, :], t["x"][b].rearrange("(j t) d -> t j d", t=T)) for b in range(B)],
            "tables": [(masks[:, :, :], t["masks"]), (window_mask[:, :, :], t["window_mask"]), (causal_mask[:, :], t["causal_mask"]), (eye_bf16[:, :], t["eye_bf16"]),
                       (before[:, :], t["before"]), (turnt[:, 0, :, :, :], t["rope"]), (turnt[:, 1, :, :, :], t["rope"]), (pick[:, :, :], t["pick"]),
                       (keep[:, :], t["keep"]), (began[:, 1:TILES], t["keep"][:, 0:TILES - 1]), (began[:, 0:1], t["keep"][:, TILES - 1:TILES])],
            "delta": [(dw[:, :], t["delta_w"]), (dwo[:, :], t["L0_attn_a_Wo"])]
            + [(dg[32 * h:32 * h + 32, :], t["L0_attn_a_g_norm"].unsqueeze(1)) for h in range(4)],
            "window": [(wqkv[:, :, :], t["L0_ffn_wqkv"].rearrange("l d n -> d l n")),
                       (wwo[:, :, :, :], t["L0_ffn_wo"].rearrange("l (c p) n -> p l c n", c=4)),
                       (w1[:, :, :], t["L0_ffn_w1"].rearrange("l d n -> d l n")),
                       (lgb[:, :, 0], t["L0_ffn_ln_g"].rearrange("l d -> d l")), (lgb[:, :, 1], t["L0_ffn_ln_b"].rearrange("l d -> d l"))]
            + [(w2[0:n, l, c, :], t["L0_ffn_w2"][l, lo:lo + n, :]) for l in range(DEPTH) for c, (lo, n) in enumerate(GPART)]
            + [(w2[HID - 256:HID - 255, l, 2, :], t["L0_ffn_b2"][l:l + 1, :]) for l in range(DEPTH)]
            + [(w1b[0:n, l, 3 * half + c:3 * half + c + 1], t["L0_ffn_b1"][l, HID * half + lo:HID * half + lo + n].unsqueeze(1))
               for l in range(DEPTH) for half in range(2) for c, (lo, n) in enumerate(GPART)]
            + [(qk_scale[:, l, 2 * w, :], t[nm][l, :].partition_broadcast(128)) for l in range(DEPTH) for w, nm in enumerate(("L0_ffn_q_scale", "L0_ffn_k_scale"))]
            + [(qk_scale[:, l, 2 * w + 1, 32 * h:32 * h + 32], t[nm][l, 32 - 32 * h:64 - 32 * h].partition_broadcast(128))
               for l in range(DEPTH) for w, nm in enumerate(("L0_ffn_q_scale", "L0_ffn_k_scale")) for h in range(2)],
            "state": [(sB[:, :, :], t["state_b"]), (sC[:, :, :], t["state_c"]), (sD[:, :], t["L0_attn_b_D"].unsqueeze(1)), (sWo[:, :], t["state_wo"]),
                      (sbo[:, :], t["L0_attn_b_b_out"].unsqueeze(0)), (sp_[:, 1:2], t["L0_attn_b_log_dt"].partition_broadcast(128))]
            + [(sp_[64 * h:64 * h + 64, c:c + 1], t[nm].unsqueeze(1)) for h in range(2) for c, nm in ((0, "L0_attn_b_log_Lam_real"), (2, "L0_attn_b_Lam_imag"))],
            "causal": [(cqk[:, :, :, :], t["causal_qk"]), (cv[:, :], t["causal_v"]), (cwo[:, :], t["causal_wo"])],
            "ffn": [(fw1[:, :], t["routed_w1"]), (fb1[:, 0:4], t["L1_ffn_b1_h"].rearrange("(c p) -> p c", c=4)), (fb1[0:64, 4:5], t["L1_ffn_b1_l"].unsqueeze(1)),
                    (fw2[:, 0:4, :], t["routed_w2h"].rearrange("(c p) n -> p c n", c=4)), (fw2[0:64, 4, :], t["routed_w2l"]),
                    (fb2[:, :], t["L1_ffn_b2_h"].unsqueeze(0)), (fw2[64:65, 4, :], t["L1_ffn_b2_l"].unsqueeze(0)),
                    (token[:, :], t["L1_ffn_routing_token"].partition_broadcast(128)),
                    (fgam[:, 0:1], t["L1_ffn_gamma_h"].unsqueeze(1)), (fgam[:, 1:2], t["L1_ffn_gamma_l"].unsqueeze(1))],
            "gates": [(gwn[:, :], t["L1_attn_b_norm_w"].unsqueeze(1)), (gwv[:, :], t["gates_v"]), (gwa[:, :], t["gates_a"]), (gwo[:, :], t["gates_wo"])],
        }
        total = {k: 16 * len(v) for k, v in loads.items()}

        block = ctx.enter_context(nc.Block())

        def bases():
            base = 0
            for stage, run in program:
                yield stage, run, base
                base += B * TILES

        @block.sync
        def _(eng):
            for key in ("x", "tables", "delta", "window", "state"):
                for dst, src in loads[key]:
                    eng.dma_start(dst, src).then_inc(loaded[key], 16)
            for stage, run, base in bases():
                if isinstance(stage, Scan):
                    stage.sync(eng, run, base)
                    for s in range(SLOTS):
                        eng.wait_ge(saved[s], MOVES * (SCAN_TURNS + 1))
                    for b in range(B):
                        eng.dma_start(hs[:, TILES * b:TILES * b + TILES, :], mixed[b].rearrange("(j t) h m -> t j (h m)", t=T)).then_inc(y_moved, 16)
            eng.wait_ge(slot_free, B * TILES * len(program) + SLOTS)
            for b in range(B):
                eng.dma_start(out[b].rearrange("(j t) d -> t j d", t=T), x[:, TILES * b:TILES * b + TILES, :]).then_inc(stored, 16)
            eng.wait_ge(stored, 16 * B)

        @block.gpsimd
        def _(eng):
            for key in ("causal", "ffn", "gates"):
                for dst, src in loads[key]:
                    eng.dma_start(dst, src).then_inc(loaded[key], 16)
            for s in range(SLOTS):
                for name in ("kT", "v", "hT"):
                    eng.memset(wcv(s, name), 0.0)
            eng.memset(upper_before[:, :, :], 0.0)
            eng.memset(minus_half[:, :], -0.5)
            for s in range(SLOTS):
                eng.memset(stat(s, 25), 0.0)
            eng.memset(delta_state[:, :, :], 0.0).then_inc(cleared, 1)
            eng.wait_ge(cleared, 1)
            for stage, run, base in bases():
                stage.pool(eng, run, base)

        @block.scalar
        def _(eng):
            eng.wait_ge(theta_ready, 1)
            eng.activation(turns[:, 1, 1:2], sm[:, 12:13], ACT.Sin)
            eng.activation(turns[:, 0, 1:2], sm[:, 13:14], ACT.Sin).then_inc(tables_act, 1)
            for stage, run, base in bases():
                stage.scalar(eng, run, base)

        @block.tensor
        def _(eng):
            for k in loads:
                eng.wait_ge(loaded[k], total[k])
            eng.wait_ge(prep, 1)
            for stage, run, base in bases():
                stage.tensor(eng, run, base)

        @block.vector
        def _(eng):
            eng.memset(ones_row[:, :], 1.0)
            for k in loads:
                eng.wait_ge(loaded[k], total[k])
            eng.tensor_scalar(dwo[:, :], dwo[:, :], dg[:, 0:1], None, ALU.mult)
            for l in range(DEPTH):
                for j in range(TILES):
                    eng.tensor_tensor(turnt[:, l, j, :, :], turnt[:, l, j, :, :], qk_scale[:, l, :, :], ALU.mult)
            eng.tensor_scalar(fw1[:, 0:HEAVY], fw1[:, 0:HEAVY], fgam[:, 0:1], float(D) ** 0.5, ALU.mult, ALU.mult)
            eng.tensor_scalar(fw1[:, HEAVY:], fw1[:, HEAVY:], fgam[:, 1:2], float(D) ** 0.5, ALU.mult, ALU.mult)
            eng.tensor_scalar(gwa[:, :], gwa[:, :], gwn[:, 0:1], None, ALU.mult)
            eng.tensor_scalar(gwv[:, :], gwv[:, :], gwn[:, 0:1], None, ALU.mult)
            eng.tensor_scalar(sB[:, 1, STATES:], sB[:, 1, STATES:], -1.0, None, ALU.mult)
            eng.tensor_scalar(sC[64:128, 0, :], sC[64:128, 0, :], -1.0, None, ALU.mult)
            eng.tensor_scalar(sC[:, 1, :], sC[:, 1, :], -1.0, None, ALU.mult)
            n = [0]

            def chain(ins):
                n[0] += 1
                ins.then_inc(tables, 1)
                eng.wait_ge(tables, n[0])

            def exp(dst, src, a, b, c, w):
                chain(eng.tensor_scalar(b, src, 87.0, -87.0, ALU.min, ALU.max))
                chain(eng.tensor_scalar(a, b, 1.4426950408889634, 12582912.0, ALU.mult, ALU.add))
                chain(eng.tensor_scalar(a, a, 12582912.0, None, ALU.subtract))
                chain(eng.scalar_tensor_tensor(out=b, in0=a, scalar=-0.693359375, in1=b, op0=ALU.mult, op1=ALU.add))
                chain(eng.scalar_tensor_tensor(out=b, in0=a, scalar=2.12194440e-4, in1=b, op0=ALU.mult, op1=ALU.add))
                chain(eng.tensor_scalar(c, b, 1.0 / 5040, 1.0 / 720, ALU.mult, ALU.add))
                for f in (120.0, 24.0, 6.0, 2.0, 1.0, 1.0):
                    chain(eng.tensor_tensor(c, c, b, ALU.mult))
                    chain(eng.tensor_scalar(c, c, 1.0 / f, None, ALU.add))
                chain(eng.tensor_scalar(a, a, 127.0, 8388608.0, ALU.add, ALU.mult))
                chain(eng.tensor_copy(smi[:, 0:w], a))
                chain(eng.tensor_tensor(dst, c, smi[:, 0:w].bitcast(F32), ALU.mult))

            exp(sm[:, 0:2], sp_[:, 0:2], sm[:, 2:4], sm[:, 4:6], sm[:, 6:8], 2)
            chain(eng.scalar_tensor_tensor(out=sm[:, 8:9], in0=sm[:, 0:1], scalar=-1.0, in1=sm[:, 1:2], op0=ALU.mult, op1=ALU.mult))
            exp(sm[:, 9:10], sm[:, 8:9], sm[:, 2:3], sm[:, 4:5], sm[:, 6:7], 1)
            eng.tensor_scalar(sB[:, :, :], sB[:, :, :], sm[:, 1:2], None, ALU.mult)
            chain(eng.memset(decay[:, :], 1.0))
            chain(eng.tensor_scalar(decay[:, :], decay[:, :], sm[:, 9:10], None, ALU.mult))
            chain(eng.memset(decay[:, :].rearrange("p (b t) -> p b t", b=1)[:, :, 0:1], 0.0))
            chain(eng.tensor_tensor(sm[:, 10:11], sp_[:, 2:3], sm[:, 1:2], ALU.mult))
            chain(eng.tensor_scalar(sm[:, 11:12], sm[:, 10:11], float(1 / (2 * np.pi)), 12582912.0, ALU.mult, ALU.add))
            chain(eng.tensor_scalar(sm[:, 11:12], sm[:, 11:12], 12582912.0, None, ALU.subtract))
            two_pi = 2 * np.pi
            c1 = np.floor(two_pi * 2 ** 8) / 2 ** 8
            c2 = np.floor((two_pi - c1) * 2 ** 20) / 2 ** 20
            for part in (c1, c2, two_pi - c1 - c2):
                chain(eng.scalar_tensor_tensor(out=sm[:, 10:11], in0=sm[:, 11:12], scalar=float(-part), in1=sm[:, 10:11], op0=ALU.mult, op1=ALU.add))
            chain(eng.tensor_scalar(sm[:, 12:13], sm[:, 10:11], 3.1415925, -3.1415925, ALU.min, ALU.max))
            chain(eng.tensor_scalar(sm[:, 14:15], sm[:, 12:13], -1.0, None, ALU.mult))
            chain(eng.tensor_tensor(sm[:, 13:14], sm[:, 14:15], sm[:, 12:13], ALU.min))
            eng.tensor_scalar(sm[:, 13:14], sm[:, 13:14], float(np.pi / 2), None, ALU.add).then_inc(theta_ready, 1)
            eng.wait_ge(tables_act, 1)
            scr = lambda n, w: arena[:, 0, 8192 + 256 * n:8192 + 256 * n + w]
            L = 1
            while L < N:
                m_ = min(L, N - L)
                cL, sL = turns[:, 0, L:L + 1], turns[:, 1, L:L + 1]
                lo = lambda w: turns[:, w, 1:1 + m_]
                chain(eng.tensor_scalar(scr(0, m_), lo(1), sL, None, ALU.mult))
                chain(eng.tensor_scalar(scr(1, m_), lo(1), cL, None, ALU.mult))
                chain(eng.scalar_tensor_tensor(out=turns[:, 0, L + 1:L + 1 + m_], in0=lo(0), scalar=cL, in1=scr(0, m_), op0=ALU.mult, op1=ALU.subtract))
                chain(eng.scalar_tensor_tensor(out=turns[:, 1, L + 1:L + 1 + m_], in0=lo(0), scalar=sL, in1=scr(1, m_), op0=ALU.mult, op1=ALU.add))
                L += m_
            eng.memset(stat(0, 250), 0.0).then_inc(prep, 1)
            eng.wait_ge(prep, 1)
            eng.wait_ge(cleared, 1)
            for _ in range(SLOTS):
                eng.sem_inc(slot_free, 1)
            for stage, run, base in bases():
                stage.vector(eng, run, base)


def kernel(**inputs):
    import concourse.bacc as bacc
    from concourse.bass_utils import run_bass_kernel_spmd

    a = {k: np.ascontiguousarray(v) for k, v in inputs.items()}
    host = dict(constants())
    host["x"] = a["L0_attn_a_x"]
    host["delta_w"] = np.concatenate([a["L0_attn_a_Wq"], a["L0_attn_a_Wk"], a["L0_attn_a_Wv"], a["L0_attn_a_Wbeta"]], axis=1)
    br, bi, cr, ci = (a[f"L0_attn_b_{k}"].T for k in ("B_real", "B_imag", "C_real", "C_imag"))
    host["state_b"] = np.stack([np.concatenate([br, bi], 1), np.concatenate([bi, br], 1)], axis=1)
    host["state_c"] = np.stack([np.concatenate([cr, ci], 0), np.concatenate([ci, cr], 0)], axis=1)
    host["state_wo"] = a["L0_attn_b_W_out"].T
    spread = np.zeros((D, 2, CAUSAL_H, 32), np.float32)
    for n, w in enumerate((a["L1_attn_a_Wq"], a["L1_attn_a_Wk"])):
        spread[:, n, :, :CAUSAL_D] = w.T.reshape(D, CAUSAL_H, CAUSAL_D)
    host["causal_qk"] = spread.reshape(D, 2, 4, 128)
    host["causal_v"], host["causal_wo"] = a["L1_attn_a_Wv"].T, a["L1_attn_a_Wo"].T
    host["routed_w1"] = np.concatenate([a["L1_ffn_w1_h"].T, a["L1_ffn_w1_l"].T, np.zeros((D, 128 - LIGHT), np.float32)], axis=1)
    host["routed_w2h"], host["routed_w2l"] = a["L1_ffn_w2_h"].T, a["L1_ffn_w2_l"].T
    host["gates_v"], host["gates_a"], host["gates_wo"] = a["L1_attn_b_W_v"].T, a["L1_attn_b_W_a"].T, a["L1_attn_b_W_out"].T
    for k in ("L0_attn_a_Wo", "L0_attn_a_g_norm", "L0_ffn_wqkv", "L0_ffn_wo", "L0_ffn_w1", "L0_ffn_ln_g", "L0_ffn_ln_b", "L0_ffn_w2", "L0_ffn_b2",
              "L0_ffn_b1", "L0_ffn_q_scale", "L0_ffn_k_scale", "L0_attn_b_D", "L0_attn_b_b_out", "L0_attn_b_log_dt", "L0_attn_b_log_Lam_real",
              "L0_attn_b_Lam_imag", "L1_ffn_routing_token", "L1_ffn_b1_h", "L1_ffn_b1_l", "L1_ffn_b2_h", "L1_ffn_b2_l", "L1_ffn_gamma_h", "L1_ffn_gamma_l", "L1_attn_b_norm_w"):
        host[k] = a[k]

    nc = bacc.Bacc("TRN2", target_bir_lowering=False, num_devices=1)
    arrays, aps = {}, {}
    for k, v in host.items():
        v = np.ascontiguousarray(v)
        arrays[f"in_{k}"] = v
        aps[k] = nc.dram_tensor(f"in_{k}", v.shape, mybir.dt.from_np(v.dtype), kind="ExternalInput").ap()
    out = nc.dram_tensor("out_0", (B, N, D), F32, kind="ExternalOutput").ap()
    hybrid_layers(nc, aps, out)
    result = run_bass_kernel_spmd(nc, [arrays], core_ids=[0])
    return result.results[0]["out_0"]
```

```python
from contextlib import ExitStack

import numpy as np

import concourse.bass as bass
from concourse import mybir

F32 = mybir.dt.float32
BF16 = mybir.dt.bfloat16
I32 = mybir.dt.int32
ALU = mybir.AluOpType
ACT = mybir.ActivationFunctionType
AX = mybir.AxisListType

B = 8
N = 512
T = 128
TILES = N // T
D = 128
SLOTS = 2
PAIRS = B // SLOTS
BANKS = 8 // SLOTS

DELTA_H, DELTA_D = 4, 32
WIN_H, WIN_D, WINDOW, DEPTH = 8, 64, 64, 2
HID = 341
STATES = 64
KEEP = 128
FETCH = 144
ITERS = 50
CAUSAL_H, CAUSAL_D = 16, 8
LIGHT, HEAVY = 64, 512
SCAN_H, SCAN_M = 8, 16
CELL = SCAN_M + 1
ROWS = SCAN_H * SCAN_M
GATES = ROWS * CELL
CHUNK = 16
CHUNKS = N // CHUNK
BANK_ROWS = 30

LN_EPS = 1e-5
MASKED = -1e30


RS_IN = 2.0 ** 16
RS_OUT = 2.0 ** 8


class Steps:

    def __init__(self, sem, names, turns=PAIRS * TILES, slots=SLOTS):
        self.sem, self.names, self.turns, self.slots = sem, names, turns, slots
        self.at = 0

    def value(self, run, i, name, s):
        i = i.n if isinstance(i, Turn) else i
        per = len(self.names) * self.slots
        return i * per + (run * self.turns * per + self.names.index(name) * self.slots + s + 1)

    def tick(self, name, s):
        assert (self.names[self.at // self.slots], self.at % self.slots) == (name, s), (name, s, self.names[self.at // self.slots])
        self.at = (self.at + 1) % (len(self.names) * self.slots)
        return self.sem


class Turn:

    def __init__(self, pair, j):
        self.pair, self.j, self.n = pair, j, pair * TILES + j

    def tile(self, s):
        return self.pair * (SLOTS * TILES) + self.j + s * TILES


def constants():
    p, f = np.arange(128)[:, None], np.arange(128)[None, :]
    same = lambda n: p // n == f // n
    masks = [p == f, p < f, p <= f, -(same(2) & (p < f)).astype(np.float32), -(same(2) & (p > f)).astype(np.float32)]
    for n in (2, 4, 8, 16, 32):
        masks.append(same(2 * n) & (p // n < f // n))
    masks.append(p // 64 < f // 64)
    masks.append(p + 1 == f)
    masks.append((p == 127) & (f == 0))
    masks.append(same(32))
    masks = np.stack([m.astype(np.float32) for m in masks], axis=1)
    k = np.arange(WINDOW + T)[None, :] - WINDOW
    seen = (k <= p) & (p - k <= WINDOW)
    window = np.stack([np.tile(np.where(seen & ((k >= 0) | (j > 0)), 0.0, MASKED), (1, 2)) for j in range(TILES)], axis=1)
    causal = np.where(f <= p, 0.0, MASKED)
    bf16 = mybir.dt.np(BF16)
    before = (np.arange(N + 384)[None, :] < 384 + p).astype(np.float32)
    half = np.arange(0, WIN_D, 2, dtype=np.float32)
    inv_freq = (1.0 / np.float32(10000.0) ** (half / np.float32(WIN_D))).astype(np.float32)
    t = np.arange(N, dtype=np.float32)
    freqs = (t[:, None] * inv_freq[None, :]).astype(np.float32)
    base = ((half + np.float32(0.4 * WIN_D)) / np.float32(1.4 * WIN_D)).astype(np.float32)
    power = ((t - N // 2) / np.float32(WINDOW // 2)).astype(np.float32)
    scale = (base[None, :] ** power[:, None]).astype(np.float32)
    cos, sin = np.cos(freqs), np.sin(freqs)
    both = lambda lo, hi: np.concatenate([lo, hi], axis=1)
    rope = np.stack([both(8 * cos * scale, 8 * cos * scale), both(-8 * sin * scale, 8 * sin * scale),
                     both(cos / scale, cos / scale), both(-sin / scale, sin / scale)], axis=1).astype(np.float32)
    rope = rope.reshape(TILES, T, 4, WIN_D).transpose(1, 0, 2, 3)
    pick = np.zeros((B, B, 128), np.float32)
    pick[np.arange(B), np.arange(B), :] = 1.0
    keep = np.tile((np.arange(TILES) < TILES - 1).astype(np.float32), (128, 1))
    return {"masks": masks, "window_mask": window.astype(bf16), "causal_mask": causal.astype(bf16), "eye_bf16": np.eye(128).astype(bf16),
            "before": before.astype(bf16), "rope": rope, "pick": pick, "keep": keep}


M_EYE, M_STRICT, M_UPPER, M_PAIR_U, M_PAIR_L, M_OFF, M_SHIFT, M_LAST, M_HEADS = 0, 1, 2, 3, 4, 5, 11, 12, 13


def hybrid_layers(nc, t, out):
    ctx = ExitStack()
    with ctx:
        ctx.enter_context(nc.allow_non_contiguous_dma(reason="biases and scales, a column of values each"))

        def sb(name, shape, dt=F32):
            return ctx.enter_context(nc.sbuf_tensor(name, shape, dt))

        def sem(name):
            return ctx.enter_context(nc.semaphore(name))

        x = sb("x", [128, B * TILES, D])
        hs = sb("hs", [128, B * TILES, D])
        feedT = sb("feedT", [128, B, N])
        masks = sb("masks", [128, 14, 128])
        window_mask = sb("window_mask", [128, TILES, 2 * (WINDOW + T)], BF16)
        causal_mask = sb("causal_mask", [128, 128], BF16)
        eye_bf16 = sb("eye_bf16", [128, 128], BF16)
        before = sb("before", [128, N + 384], BF16)
        pick = sb("pick", [B, B, 128])
        keep = sb("keep", [128, TILES])
        ones_row = sb("ones_row", [1, 128])
        dw = sb("dw", [128, 3 * D + DELTA_H])
        dwo = sb("dwo", [128, D])
        dg = sb("dg", [128, 1])
        wqkv = sb("wqkv", [128, DEPTH, 3 * WIN_H * WIN_D])
        wwo = sb("wwo", [128, DEPTH, 4, D])
        qk_scale = sb("qk_scale", [128, DEPTH, 4, WIN_D])
        turnt = sb("turnt", [128, DEPTH, TILES, 4, WIN_D])
        lgb = sb("lgb", [128, DEPTH, 2])
        w1 = sb("w1", [128, DEPTH, 2 * HID])
        w1b = sb("w1b", [128, DEPTH, 6])
        w2 = sb("w2", [128, DEPTH, 3, D])
        sB = sb("sB", [128, 2, 2 * STATES])
        sC = sb("sC", [128, 2, D])
        sD = sb("sD", [128, 1])
        sWo = sb("sWo", [128, D])
        sbo = sb("sbo", [1, D])
        sp_ = sb("sp_", [128, 3])
        turns = sb("turns", [128, 2, N + 1])
        cqk = sb("cqk", [128, 2, 4, 128])
        cv = sb("cv", [128, D])
        cwo = sb("cwo", [128, D])
        fw1 = sb("fw1", [128, HEAVY + 128])
        fgam = sb("fgam", [128, 2])
        fb2 = sb("fb2", [1, D])
        token = sb("token", [128, D])
        scores = sb("scores", [128, B * TILES])
        weight = sb("weight", [128, B * TILES])
        fb1 = sb("fb1", [128, 5])
        fw2 = sb("fw2", [128, 5, D])
        gwn = sb("gwn", [128, 1])
        gwv = sb("gwv", [128, D])
        gwa = sb("gwa", [128, GATES])
        gwo = sb("gwo", [128, D])
        ARENA = 8960
        delta_state = sb("delta_state", [128, SLOTS, 128])
        zero = sb("zero", [128, 1])
        arena = sb("arena", [128, SLOTS, ARENA])
        small = sb("small", [128, SLOTS, 256])
        minus_half = sb("minus_half", [128, 16])
        P = ctx.enter_context(nc.psum_tensor("P", [128, 8, 512], F32))

        def carve(sizes):
            at, views = 0, {}
            for name, size in sizes:
                views[name] = at, size
                at += size
            assert at <= ARENA, at
            return lambda s, name: arena[:, s, views[name][0]:views[name][0] + views[name][1]]

        def bank(s, k):
            return P[:, BANKS * s + k, :]

        def heads(ap, n):
            return ap.rearrange("p (h d) -> p h d", h=n)

        def over(ap, n, size):
            return ap.unsqueeze(2).broadcast_to([128, n, size])

        def each(ap, n):
            return ap.unsqueeze(1).broadcast_to([ap.shape[0], n, ap.shape[-1]])

        eye = masks[:, M_EYE, :]
        eyeb = eye_bf16[:, :]

        loaded = {k: sem(f"loaded_{k}") for k in ("x", "tables", "delta", "window", "state", "causal", "ffn", "gates")}
        prep = sem("weights_prepared")
        tables = sem("state_tables_step")
        tables_act = sem("state_tables_sine")
        theta_ready = sem("theta_ready")
        cleared = sem("carries_cleared")
        slot_free = sem("slot_free")
        y_moved = sem("scan_output_moved")
        stored = sem("stored")

        def steps(key, names, **kw):
            return Steps(sem(key), names, **kw)

        def stat(s, a, n=1):
            return small[:, s, a:a + n]

        def wait_slots(eng, base, i):
            eng.wait_ge(slot_free, (i.n if isinstance(i, Turn) else i) * SLOTS + (base + SLOTS))

        def root_pool(eng, v, p, run, i, name, get, done):
            for s in range(SLOTS):
                eng.wait_ge(v.sem, v.value(run, i, name, s))
                eng.tensor_tensor(get(s), get(s), minus_half[:, 0:get(s).shape[-1]], ALU.pow).then_inc(p.tick(done, s), 1)

        def newton(eng, v, run, i, names, get, ready):
            a, b_, c = names
            for s in range(SLOTS):
                var, guess, tmp, res = get(s)
                ready(s)
                eng.tensor_tensor(tmp, guess, guess, ALU.mult).then_inc(v.tick(a, s), 1)
            for s in range(SLOTS):
                var, guess, tmp, res = get(s)
                eng.wait_ge(v.sem, v.value(run, i, a, s))
                eng.scalar_tensor_tensor(out=tmp, in0=tmp, scalar=-0.5 * RS_IN * RS_OUT, in1=var, op0=ALU.mult,
                                         op1=ALU.mult).then_inc(v.tick(b_, s), 1)
            for s in range(SLOTS):
                var, guess, tmp, res = get(s)
                eng.wait_ge(v.sem, v.value(run, i, b_, s))
                eng.scalar_tensor_tensor(out=res, in0=tmp, scalar=1.5 * RS_OUT, in1=guess, op0=ALU.add,
                                         op1=ALU.mult).then_inc(v.tick(c, s), 1)

        def guess_scalar(eng, v, a, run, i, var_step, names, get):
            for s in range(SLOTS):
                var, guess, tmp, res = get(s)
                eng.wait_ge(v.sem, v.value(run, i, var_step, s))
                eng.activation(guess, var, ACT.Ln, scale=RS_IN).then_inc(a.tick(names[0], s), 1)
            for s in range(SLOTS):
                var, guess, tmp, res = get(s)
                eng.wait_ge(a.sem, a.value(run, i, names[0], s))
                eng.activation(guess, guess, ACT.Exp, scale=-0.5).then_inc(a.tick(names[1], s), 1)

        def tiles_of(ap, i, s):
            return ap[:, bass.ds(i * (SLOTS * TILES) + s * TILES, TILES), :]

        def xb(i, s):
            return x[:, bass.ds(i.tile(s), 1), :]

        def batch(ap, i, s):
            return ap[:, bass.ds(i * SLOTS + s, 1), :]

        def turn_loop(eng, body):
            with eng.Fori(0, PAIRS) as pair:
                with eng.Fori(0, TILES) as j:
                    body(Turn(pair, j))

        def tileT(i, s):
            return feedT[:, :, :].rearrange("p b (j t) -> p (b j) t", j=TILES)[:, bass.ds(i.tile(s), 1), :]

        def pair_loop(eng, body):
            with eng.Fori(0, PAIRS) as i:
                body(i)

        stages = []
        dv = steps("delta_vector", ["xT", "ss", "vqk", "one_e", "beta", "nd1", "nd2", "nd3", "qkn", "kb", "A", "X2", "vS",
                                           "X4", "X8", "X16", "X32", "X64", "X128", "oss", "vo", "no1", "no2", "no3", "on", "S1", "S2", "S3"])
        da = steps("delta_scalar", ["sq", "lnq", "rsq", "tT", "M2", "M4", "M8", "M16", "M32", "M64", "U", "osq", "lno", "rso", "oT"])
        LEVELS = (2, 4, 8, 16, 32, 64)
        dp = steps("delta_pool", [f"off{lvl}" for lvl in LEVELS])
        dt_ = steps("delta_tensor", ["proj", "tT", "grams", "AX2", "kS", "XAX2", "AX4", "XAX4", "AX8", "XAX8", "AX16", "XAX16", "AX32", "XAX32",
                                     "AX64", "XAX64", "U", "O", "KU", "oT", "y"])
        dcv = carve([("xT", 128), ("sq", 256), ("qk", 384), ("v", 128), ("tT", 384), ("AT", 512), ("W", 512),
                     ("X", 512), ("XT", 512), ("M", 512), ("off", 3072), ("U", 128), ("R", 128), ("osq", 128), ("on", 128), ("oT", 128)])
        Q8 = lambda s: (stat(s, 32, 8), stat(s, 40, 8), stat(s, 48, 8), stat(s, 56, 8))
        O4 = lambda s: (stat(s, 72, 4), stat(s, 76, 4), stat(s, 80, 4), stat(s, 84, 4))
        BETA = 64

        def gram(s, n):
            return P[:, BANKS * s:BANKS * s + 4, 128 * n:128 * n + 128]

        pair_made = sem("delta_pair_blocks")

        class Delta:
            def vector(self, eng, run, base):
                def body(i):
                    wait_slots(eng, base, i)
                    for s in range(SLOTS):
                        eng.tensor_scalar(dcv(s, "xT"), tileT(i, s), 1.0, None, ALU.mult).then_inc(dv.tick("xT", s), 1)
                    for s in range(SLOTS):
                        eng.wait_ge(da.sem, da.value(run, i, "sq", s))
                        eng.tensor_reduce(Q8(s)[0], heads(dcv(s, "sq"), 8), AX.X, ALU.add).then_inc(dv.tick("ss", s), 1)
                    for s in range(SLOTS):
                        eng.wait_ge(dv.sem, dv.value(run, i, "ss", s))
                        eng.tensor_scalar(Q8(s)[0], Q8(s)[0], 1e-24, None, ALU.max).then_inc(dv.tick("vqk", s), 1)
                    for s in range(SLOTS):
                        eng.tensor_scalar(stat(s, BETA, 4), stat(s, BETA, 4), 1.0, None, ALU.add).then_inc(dv.tick("one_e", s), 1)
                    for s in range(SLOTS):
                        eng.wait_ge(dv.sem, dv.value(run, i, "one_e", s))
                        eng.reciprocal(stat(s, BETA, 4), stat(s, BETA, 4)).then_inc(dv.tick("beta", s), 1)
                    newton(eng, dv, run, i, ["nd1", "nd2", "nd3"], Q8,
                           lambda s: eng.wait_ge(da.sem, da.value(run, i, "rsq", s)))
                    for s in range(SLOTS):
                        eng.wait_ge(dv.sem, dv.value(run, i, "nd3", s))
                        eng.tensor_tensor(heads(dcv(s, "qk")[:, 0:256], 8), heads(bank(s, 1)[:, 0:256], 8),
                                          over(Q8(s)[3], 8, DELTA_D), ALU.mult).then_inc(dv.tick("qkn", s), 1)
                    for s in range(SLOTS):
                        eng.wait_ge(dv.sem, dv.value(run, i, "qkn", s))
                        eng.tensor_tensor(heads(dcv(s, "v"), 4), heads(bank(s, 1)[:, 256:384], 4),
                                          over(stat(s, BETA, 4), 4, DELTA_D), ALU.mult)
                        eng.tensor_tensor(heads(dcv(s, "qk")[:, 256:384], 4), heads(dcv(s, "qk")[:, 128:256], 4),
                                          over(stat(s, BETA, 4), 4, DELTA_D), ALU.mult).then_inc(dv.tick("kb", s), 1)
                    for s in range(SLOTS):
                        eng.wait_ge(dt_.sem, dt_.value(run, i, "grams", s))
                        eng.tensor_tensor(heads(dcv(s, "AT"), 4), gram(s, 0), each(masks[:, M_STRICT, :], 4), ALU.mult)\
                            .then_inc(dv.tick("A", s), 1)
                    for s in range(SLOTS):
                        eng.wait_ge(dv.sem, dv.value(run, i, "A", s))
                        eng.tensor_tensor(heads(dcv(s, "X"), 4), gram(s, 2), each(masks[:, M_PAIR_L, :], 4), ALU.mult)
                        eng.tensor_tensor(heads(dcv(s, "XT"), 4), heads(dcv(s, "AT"), 4), each(masks[:, M_PAIR_U, :], 4), ALU.mult)
                        eng.tensor_tensor(heads(dcv(s, "W"), 4), gram(s, 1), each(masks[:, M_UPPER, :], 4), ALU.mult).then_inc(pair_made, 1)
                        eng.wait_ge(pair_made, i.n * SLOTS + (s + 1))
                        eng.tensor_tensor(heads(dcv(s, "X"), 4), heads(dcv(s, "X"), 4), each(eye, 4), ALU.add)
                        eng.tensor_tensor(heads(dcv(s, "XT"), 4), heads(dcv(s, "XT"), 4), each(eye, 4), ALU.add)\
                            .then_inc(dv.tick("X2", s), 1)
                    for s in range(SLOTS):
                        eng.wait_ge(dt_.sem, dt_.value(run, i, "kS", s))
                        eng.tensor_tensor(dcv(s, "v"), dcv(s, "v"), bank(s, 3)[:, 384:512], ALU.subtract).then_inc(dv.tick("vS", s), 1)
                    for n, nn in ((lvl, 2 * lvl) for lvl in LEVELS):
                        for s in range(SLOTS):
                            eng.wait_ge(dt_.sem, dt_.value(run, i, f"XAX{n}", s))
                            if nn < 128:
                                eng.tensor_tensor(dcv(s, "X"), dcv(s, "X"), bank(s, 1), ALU.subtract)
                            eng.tensor_tensor(dcv(s, "XT"), dcv(s, "XT"), bank(s, 2), ALU.subtract).then_inc(dv.tick(f"X{nn}", s), 1)
                    for s in range(SLOTS):
                        eng.wait_ge(da.sem, da.value(run, i, "osq", s))
                        eng.tensor_reduce(O4(s)[0], heads(dcv(s, "osq"), 4), AX.X, ALU.add).then_inc(dv.tick("oss", s), 1)
                    for s in range(SLOTS):
                        eng.wait_ge(dv.sem, dv.value(run, i, "oss", s))
                        eng.tensor_scalar(O4(s)[0], O4(s)[0], LN_EPS, None, ALU.add).then_inc(dv.tick("vo", s), 1)
                    newton(eng, dv, run, i, ["no1", "no2", "no3"], O4,
                           lambda s: eng.wait_ge(da.sem, da.value(run, i, "rso", s)))
                    for s in range(SLOTS):
                        eng.wait_ge(dv.sem, dv.value(run, i, "no3", s))
                        eng.tensor_tensor(heads(dcv(s, "on"), 4), heads(bank(s, 0)[:, 0:128], 4),
                                          over(O4(s)[3], 4, DELTA_D), ALU.mult).then_inc(dv.tick("on", s), 1)
                    for s in range(SLOTS):
                        eng.wait_ge(dt_.sem, dt_.value(run, i, "KU", s))
                        eng.tensor_tensor(dcv(s, "R"), bank(s, 3)[:, 256:384], masks[:, M_HEADS, :], ALU.mult).then_inc(dv.tick("S1", s), 1)
                    for s in range(SLOTS):
                        eng.wait_ge(dv.sem, dv.value(run, i, "S1", s))
                        eng.tensor_tensor(dcv(s, "R"), dcv(s, "R"), delta_state[:, s, :], ALU.add).then_inc(dv.tick("S2", s), 1)
                    for s in range(SLOTS):
                        eng.wait_ge(dv.sem, dv.value(run, i, "S2", s))
                        eng.tensor_scalar(delta_state[:, s, :], dcv(s, "R"), keep[:, bass.ds(i.j, 1)], None, ALU.mult).then_inc(dv.tick("S3", s), 1)
                    for s in range(SLOTS):
                        eng.wait_ge(dt_.sem, dt_.value(run, i, "y", s))
                        eng.tensor_tensor(xb(i, s), xb(i, s), bank(s, 2)[:, 0:128], ALU.add).then_inc(slot_free, 1)
                turn_loop(eng, body)

            def scalar(self, eng, run, base):
                eng.preload_act_table_set("natural_log_exp_and_others")

                def body(i):
                    wait_slots(eng, base, i)
                    for s in range(SLOTS):
                        eng.wait_ge(dt_.sem, dt_.value(run, i, "proj", s))
                        eng.activation(stat(s, BETA, 4), bank(s, 1)[:, 384:388], ACT.Exp, scale=-1.0)
                        eng.activation(dcv(s, "sq"), bank(s, 1)[:, 0:256], ACT.Square).then_inc(da.tick("sq", s), 1)
                    guess_scalar(eng, dv, da, run, i, "vqk", ["lnq", "rsq"], Q8)
                    for s in range(SLOTS):
                        eng.wait_ge(dt_.sem, dt_.value(run, i, "tT", s))
                        eng.activation(dcv(s, "tT"), bank(s, 0)[:, 0:384], ACT.Copy).then_inc(da.tick("tT", s), 1)
                    for n in LEVELS:
                        for s in range(SLOTS):
                            eng.wait_ge(dt_.sem, dt_.value(run, i, f"AX{n}", s))
                            eng.activation(dcv(s, "M"), bank(s, 0), ACT.Copy).then_inc(da.tick(f"M{n}", s), 1)
                    for s in range(SLOTS):
                        eng.wait_ge(dt_.sem, dt_.value(run, i, "U", s))
                        eng.activation(dcv(s, "U"), bank(s, 3)[:, 0:128], ACT.Copy).then_inc(da.tick("U", s), 1)
                    for s in range(SLOTS):
                        eng.wait_ge(dt_.sem, dt_.value(run, i, "O", s))
                        eng.activation(dcv(s, "osq"), bank(s, 0)[:, 0:128], ACT.Square, scale=DELTA_D ** -0.5).then_inc(da.tick("osq", s), 1)
                    guess_scalar(eng, dv, da, run, i, "vo", ["lno", "rso"], O4)
                    for s in range(SLOTS):
                        eng.wait_ge(dt_.sem, dt_.value(run, i, "oT", s))
                        eng.activation(dcv(s, "oT"), bank(s, 1)[:, 0:128], ACT.Copy).then_inc(da.tick("oT", s), 1)
                turn_loop(eng, body)

            def pool(self, eng, run, base):
                def body(i):
                    wait_slots(eng, base, i)
                    for n, lvl in enumerate(LEVELS):
                        for s in range(SLOTS):
                            if n == 0:
                                eng.wait_ge(dv.sem, dv.value(run, i, "A", s))
                            eng.tensor_tensor(heads(dcv(s, "off")[:, 512 * n:512 * n + 512], 4), heads(dcv(s, "AT"), 4),
                                              each(masks[:, M_OFF + n, :], 4), ALU.mult).then_inc(dp.tick(f"off{lvl}", s), 1)
                turn_loop(eng, body)

            def tensor(self, eng, run, base):
                def per_head(out_, lhs, rhs, n=128):
                    for h in range(4):
                        ins = eng.matmul(out_[:, n * h:n * h + n], lhs(h), rhs(h), start=True, stop=True)
                    return ins

                def body(i):
                    wait_slots(eng, base, i)
                    blk = lambda ap, n=128: (lambda h: ap[:, n * h:n * h + n])
                    for s in range(SLOTS):
                        eng.wait_ge(dv.sem, dv.value(run, i, "xT", s))
                        eng.matmul(bank(s, 1)[:, 0:388], dcv(s, "xT"), dw[:, :], start=True, stop=True).then_inc(dt_.tick("proj", s), 1)
                    for s in range(SLOTS):
                        eng.wait_ge(dv.sem, dv.value(run, i, "kb", s))
                        for n in range(3):
                            ins = eng.transpose(bank(s, 0)[:, 128 * n:128 * n + 128], dcv(s, "qk")[:, 128 * n:128 * n + 128], eye)
                        ins.then_inc(dt_.tick("tT", s), 1)
                    for s in range(SLOTS):
                        eng.wait_ge(da.sem, da.value(run, i, "tT", s))
                        row = lambda n: (lambda h: dcv(s, "tT")[32 * h:32 * h + 32, 128 * n:128 * n + 128])
                        for n, (a, b_) in enumerate(((1, 2), (1, 0), (2, 1))):
                            for h in range(4):
                                ins = eng.matmul(bank(s, h)[:, 128 * n:128 * n + 128], row(a)(h), row(b_)(h), start=True, stop=True)
                        ins.then_inc(dt_.tick("grams", s), 1)
                    for n, (lvl, x_) in enumerate((lvl, f"X{lvl}") for lvl in LEVELS):
                        for s in range(SLOTS):
                            eng.wait_ge(dp.sem, dp.value(run, i, f"off{lvl}", s))
                            eng.wait_ge(dv.sem, dv.value(run, i, x_, s))
                            per_head(bank(s, 0), blk(dcv(s, "off")[:, 512 * n:512 * n + 512]), blk(dcv(s, "X"))).then_inc(dt_.tick(f"AX{lvl}", s), 1)
                        if n == 0:
                            for s in range(SLOTS):
                                eng.matmul(bank(s, 3)[:, 384:512], dcv(s, "tT")[:, 256:384], delta_state[:, s, :], start=True, stop=True)\
                                    .then_inc(dt_.tick("kS", s), 1)
                        for s in range(SLOTS):
                            eng.wait_ge(da.sem, da.value(run, i, f"M{lvl}", s))
                            if lvl < 64:
                                per_head(bank(s, 1), blk(dcv(s, "XT")), blk(dcv(s, "M")))
                            per_head(bank(s, 2), blk(dcv(s, "M")), blk(dcv(s, "XT"))).then_inc(dt_.tick(f"XAX{lvl}", s), 1)
                    for s in range(SLOTS):
                        eng.wait_ge(dv.sem, dv.value(run, i, "X128", s))
                        per_head(bank(s, 3), blk(dcv(s, "XT")), blk(dcv(s, "v"), 32), 32).then_inc(dt_.tick("U", s), 1)
                    for s in range(SLOTS):
                        eng.wait_ge(da.sem, da.value(run, i, "U", s))
                        eng.matmul(bank(s, 0)[:, 0:128], dcv(s, "tT")[:, 0:128], delta_state[:, s, :], start=True, stop=True)
                        for h in range(4):
                            ins = eng.matmul(bank(s, 0)[:, 32 * h:32 * h + 32], dcv(s, "W")[:, 128 * h:128 * h + 128], dcv(s, "U")[:, 32 * h:32 * h + 32],
                                             start=False, stop=True, skip_group_check=True)
                        ins.then_inc(dt_.tick("O", s), 1)
                    for s in range(SLOTS):
                        eng.matmul(bank(s, 3)[:, 256:384], dcv(s, "qk")[:, 128:256], dcv(s, "U"), start=True, stop=True).then_inc(dt_.tick("KU", s), 1)
                    for s in range(SLOTS):
                        eng.wait_ge(dv.sem, dv.value(run, i, "on", s))
                        eng.transpose(bank(s, 1)[:, 0:128], dcv(s, "on"), eye).then_inc(dt_.tick("oT", s), 1)
                    for s in range(SLOTS):
                        eng.wait_ge(da.sem, da.value(run, i, "oT", s))
                        eng.matmul(bank(s, 2)[:, 0:128], dcv(s, "oT"), dwo[:, :], start=True, stop=True).then_inc(dt_.tick("y", s), 1)
                turn_loop(eng, body)

        fv_ = steps("window_front_vector", ["hT", "q1", "ss", "vqk", "q3", "nq1", "nq2", "nq3", "qn", "kn"])
        fa_ = steps("window_front_scalar", ["vh", "k", "v", "sq", "lnq", "rsq"])
        fp_ = steps("window_front_pool", ["k1", "k3"])
        ft_ = steps("window_front_tensor", ["qkv"])
        wv_ = steps("window_vector", ["qT", "max", "rz", "pT", "o", "h"])
        wa = steps("window_scalar", ["kT", "p", "pT", "oT"])
        wt = steps("window_tensor", ["qkT", "sim", "pT", "o", "oT", "y"])
        KEYS = WINDOW + T
        wcv = carve([("hT", T), ("q", 512), ("k", 512), ("v", 512), ("vh", 512), ("t", 512), ("tk", 512),
                     ("qT", 512), ("kT", 4 * KEYS), ("p", 8 * KEYS), ("pT", 1024), ("pTh", 1024), ("o", 512)])
        turned = lambda s: wcv(s, "pTh")[:, 0:512]
        wsq = lambda s: wcv(s, "p")[:, 0:1024]
        Q16 = lambda s: (stat(s, 32, 16), stat(s, 48, 16), stat(s, 64, 16), stat(s, 80, 16))
        MAX, Z, RZ = 96, 112, 128

        def head_place(h):
            return 2 * (h % 2) + h // 4, h // 2 % 2

        def window_loop(eng, base, front, attend, finish, finish_in=None):
            with eng.Fori(0, PAIRS) as pair:
                eng.wait_ge(slot_free, pair * (SLOTS * TILES) + (base + SLOTS))
                front(Turn(pair, 0))
                for j in range(TILES):
                    attend(Turn(pair, j))
                    if j == TILES - 1:
                        finish(Turn(pair, j))
                    elif finish_in:
                        finish_in(Turn(pair, j), Turn(pair, j + 1))
                    else:
                        front(Turn(pair, j + 1))
                        finish(Turn(pair, j))

        class Window:
            def __init__(self, depth):
                self.depth = depth

            def hb(self, i, s):
                return hs[:, bass.ds(i.tile(s), 1), :]

            def rope(self, i, n, a, b):
                return turnt[:, self.depth, i.j, n, a:b].unsqueeze(1).broadcast_to([128, WIN_H, b - a])

            def vector(self, eng, run, base):
                def load(i):
                    for s in range(SLOTS):
                        if i.j:
                            eng.wait_ge(ft_.sem, ft_.value(run, Turn(i.pair, i.j - 1), "qkv", s))
                        eng.tensor_scalar(wcv(s, "hT"), tileT(i, s), 1.0, None, ALU.mult).then_inc(fv_.tick("hT", s), 1)

                def rotate(i):
                    for s in range(SLOTS):
                        eng.wait_ge(ft_.sem, ft_.value(run, i, "qkv", s))
                        raw, q, t_ = heads(bank(s, 1), 8), heads(wcv(s, "q"), 8), heads(wcv(s, "t"), 8)
                        eng.tensor_tensor(t_[:, :, 0:32], raw[:, :, 32:64], self.rope(i, 1, 0, 32), ALU.mult)
                        eng.tensor_tensor(t_[:, :, 32:64], raw[:, :, 0:32], self.rope(i, 1, 32, 64), ALU.mult)
                        eng.tensor_tensor(q, raw, self.rope(i, 0, 0, 64), ALU.mult).then_inc(fv_.tick("q1", s), 1)

                def scale(i):
                    for s in range(SLOTS):
                        eng.wait_ge(fa_.sem, fa_.value(run, i, "sq", s))
                        eng.tensor_reduce(Q16(s)[0], heads(wsq(s), 16), AX.X, ALU.add).then_inc(fv_.tick("ss", s), 1)
                    for s in range(SLOTS):
                        eng.wait_ge(fv_.sem, fv_.value(run, i, "ss", s))
                        eng.tensor_scalar(Q16(s)[0], Q16(s)[0], 1e-24, None, ALU.max).then_inc(fv_.tick("vqk", s), 1)
                    for s in range(SLOTS):
                        eng.tensor_tensor(wcv(s, "q"), wcv(s, "q"), wcv(s, "t"), ALU.add).then_inc(fv_.tick("q3", s), 1)
                    newton(eng, fv_, run, i, ["nq1", "nq2", "nq3"], Q16,
                           lambda s: eng.wait_ge(fa_.sem, fa_.value(run, i, "rsq", s)))
                    for s in range(SLOTS):
                        eng.wait_ge(fv_.sem, fv_.value(run, i, "nq3", s))
                        eng.tensor_tensor(heads(wcv(s, "q"), 8), heads(wcv(s, "q"), 8), over(Q16(s)[3][:, 0:8], 8, WIN_D), ALU.mult)\
                            .then_inc(fv_.tick("qn", s), 1)
                    for s in range(SLOTS):
                        eng.wait_ge(fp_.sem, fp_.value(run, i, "k3", s))
                        eng.tensor_tensor(heads(turned(s), 8), heads(turned(s), 8), over(Q16(s)[3][:, 8:16], 8, WIN_D), ALU.mult)\
                            .then_inc(fv_.tick("kn", s), 1)

                def front(i):
                    load(i)
                    rotate(i)
                    scale(i)

                def attend(i):
                    if i.j < TILES - 1:
                        load(Turn(i.pair, i.j + 1))
                    for s in range(SLOTS):
                        eng.wait_ge(wt.sem, wt.value(run, i, "qkT", s))
                        eng.tensor_copy(wcv(s, "qT"), bank(s, 0)).then_inc(wv_.tick("qT", s), 1)
                    for s in range(SLOTS):
                        eng.wait_ge(wt.sem, wt.value(run, i, "sim", s))
                        for n in range(4):
                            ins = eng.tensor_reduce(stat(s, MAX + 2 * n, 2), heads(bank(s, n)[:, 0:2 * KEYS], 2), AX.X, ALU.max, negate=True)
                        ins.then_inc(wv_.tick("max", s), 1)
                    for s in range(SLOTS):
                        eng.wait_ge(wa.sem, wa.value(run, i, "p", s))
                        eng.reciprocal(stat(s, RZ, 8), stat(s, Z, 8)).then_inc(wv_.tick("rz", s), 1)
                    for s in range(SLOTS):
                        eng.wait_ge(wt.sem, wt.value(run, i, "pT", s))
                        eng.tensor_copy(wcv(s, "pT")[:, 0:512], bank(s, 0))
                        eng.tensor_copy(wcv(s, "pTh")[0:64, 0:512], bank(s, 2)[0:64, :]).then_inc(wv_.tick("pT", s), 1)
                    for s in range(SLOTS):
                        eng.wait_ge(wt.sem, wt.value(run, i, "o", s))
                        eng.tensor_tensor(heads(wcv(s, "o"), 8), heads(bank(s, 0), 8), over(stat(s, RZ, 8), 8, WIN_D), ALU.mult)\
                            .then_inc(wv_.tick("o", s), 1)

                def finish(i):
                    for s in range(SLOTS):
                        eng.wait_ge(wt.sem, wt.value(run, i, "y", s))
                        eng.tensor_tensor(self.hb(i, s), self.hb(i, s), bank(s, 0)[:, 0:128], ALU.add).then_inc(wv_.tick("h", s), 1)
                    for s in range(SLOTS):
                        eng.wait_ge(wv_.sem, wv_.value(run, i, "h", s))
                        eng.sem_inc(slot_free, 1)

                def finish_in(i, following):
                    rotate(following)
                    finish(i)
                    scale(following)
                window_loop(eng, base, front, attend, finish, finish_in)

            def scalar(self, eng, run, base):
                def split(i):
                    for s in range(SLOTS):
                        if i.j:
                            eng.wait_ge(wt.sem, wt.value(run, Turn(i.pair, i.j - 1), "o", s))
                        eng.activation(heads(wcv(s, "kT"), 4)[:, :, 0:WINDOW], heads(wcv(s, "kT"), 4)[:, :, T:KEYS], ACT.Copy)
                        eng.activation(wcv(s, "vh")[0:64, :], wcv(s, "v")[64:128, :], ACT.Copy).then_inc(fa_.tick("vh", s), 1)
                    for s in range(SLOTS):
                        eng.wait_ge(ft_.sem, ft_.value(run, i, "qkv", s))
                        eng.activation(wcv(s, "k"), bank(s, 2), ACT.Copy).then_inc(fa_.tick("k", s), 1)
                    for s in range(SLOTS):
                        eng.wait_ge(fa_.sem, fa_.value(run, i, "vh", s))
                        eng.activation(wcv(s, "v"), bank(s, 3), ACT.Copy).then_inc(fa_.tick("v", s), 1)

                def square(i):
                    for s in range(SLOTS):
                        eng.activation(wsq(s)[:, 512:1024], bank(s, 2), ACT.Square)
                        eng.wait_ge(fv_.sem, fv_.value(run, i, "q1", s))
                        eng.activation(wsq(s)[:, 0:512], bank(s, 1), ACT.Square).then_inc(fa_.tick("sq", s), 1)
                    guess_scalar(eng, fv_, fa_, run, i, "vqk", ["lnq", "rsq"], Q16)

                def front(i):
                    split(i)
                    square(i)

                def attend(i):
                    for s in range(SLOTS):
                        eng.wait_ge(wt.sem, wt.value(run, i, "qkT", s))
                        eng.activation(heads(wcv(s, "kT"), 4)[:, :, WINDOW:KEYS], heads(bank(s, 1), 4), ACT.Copy).then_inc(wa.tick("kT", s), 1)
                    for s in range(SLOTS):
                        eng.wait_ge(wv_.sem, wv_.value(run, i, "max", s))
                        for h in range(WIN_H):
                            n, c = head_place(h)
                            ins = eng.activation(wcv(s, "p")[:, KEYS * h:KEYS * h + KEYS], bank(s, n)[:, KEYS * c:KEYS * c + KEYS],
                                                 ACT.Exp, bias=stat(s, MAX + 2 * n + c), accum_out=stat(s, Z + h))
                        ins.then_inc(wa.tick("p", s), 1)
                    for s in range(SLOTS):
                        eng.wait_ge(wt.sem, wt.value(run, i, "pT", s))
                        eng.activation(wcv(s, "pT")[:, 512:1024], bank(s, 1), ACT.Copy)
                        eng.activation(wcv(s, "pTh")[0:64, 512:1024], bank(s, 3)[0:64, :], ACT.Copy).then_inc(wa.tick("pT", s), 1)

                def finish(i):
                    for s in range(SLOTS):
                        eng.wait_ge(wt.sem, wt.value(run, i, "oT", s))
                        eng.activation(wcv(s, "pT")[:, 0:512], bank(s, 0), ACT.Copy).then_inc(wa.tick("oT", s), 1)

                def finish_in(i, following):
                    split(following)
                    finish(i)
                    square(following)
                eng.preload_act_table_set("natural_log_exp_and_others")
                window_loop(eng, base, front, attend, finish, finish_in)

            def pool(self, eng, run, base):
                def front(i):
                    for s in range(SLOTS):
                        eng.wait_ge(fa_.sem, fa_.value(run, i, "k", s))
                        k, t_ = heads(wcv(s, "k"), 8), heads(wcv(s, "tk"), 8)
                        eng.tensor_tensor(t_[:, :, 0:32], k[:, :, 32:64], self.rope(i, 3, 0, 32), ALU.mult)
                        eng.tensor_tensor(t_[:, :, 32:64], k[:, :, 0:32], self.rope(i, 3, 32, 64), ALU.mult)
                        eng.tensor_tensor(heads(turned(s), 8), k, self.rope(i, 2, 0, 64), ALU.mult).then_inc(fp_.tick("k1", s), 1)
                    for s in range(SLOTS):
                        eng.wait_ge(fp_.sem, fp_.value(run, i, "k1", s))
                        eng.tensor_tensor(turned(s), turned(s), wcv(s, "tk"), ALU.add).then_inc(fp_.tick("k3", s), 1)
                nothing = lambda i: None
                window_loop(eng, base, front, nothing, nothing)

            def tensor(self, eng, run, base):
                def front(i):
                    for s in range(SLOTS):
                        eng.wait_ge(fv_.sem, fv_.value(run, i, "hT", s))
                        for n in range(3):
                            ins = eng.matmul(bank(s, 1 + n), wcv(s, "hT"), wqkv[:, self.depth, 512 * n:512 * n + 512], start=True, stop=True)
                        ins.then_inc(ft_.tick("qkv", s), 1)

                def attend(i):
                    for s in range(SLOTS):
                        if i.j:
                            eng.wait_ge(wv_.sem, wv_.value(run, Turn(i.pair, i.j - 1), "h", s))
                        eng.wait_ge(fv_.sem, fv_.value(run, i, "qn", s))
                        for n in range(4):
                            eng.transpose(bank(s, 0)[:, 128 * n:128 * n + 128], wcv(s, "q")[:, 128 * n:128 * n + 128], eye)
                        eng.wait_ge(fv_.sem, fv_.value(run, i, "kn", s))
                        for n in range(4):
                            ins = eng.transpose(bank(s, 1)[:, 128 * n:128 * n + 128], turned(s)[:, 128 * n:128 * n + 128], eye)
                        ins.then_inc(wt.tick("qkT", s), 1)
                    for s in range(SLOTS):
                        eng.wait_ge(wa.sem, wa.value(run, i, "kT", s))
                        eng.wait_ge(wv_.sem, wv_.value(run, i, "qT", s))
                        for n in range(4):
                            eng.matmul(bank(s, n)[:, 0:2 * KEYS], eyeb, window_mask[:, i.j, :], start=True, stop=True)
                        for h in range(WIN_H):
                            (n, c), r, at = head_place(h), 64 * (h % 2), h // 2
                            ins = eng.matmul(bank(s, n)[:, KEYS * c:KEYS * c + KEYS], wcv(s, "qT")[r:r + 64, 128 * at:128 * at + 128],
                                             wcv(s, "kT")[r:r + 64, KEYS * at:KEYS * at + KEYS], start=False, stop=True, skip_group_check=True)
                        ins.then_inc(wt.tick("sim", s), 1)
                    for s in range(SLOTS):
                        eng.wait_ge(wa.sem, wa.value(run, i, "p", s))
                        for h in range(8):
                            c = 128 * (h % 4)
                            eng.transpose(bank(s, h // 4)[:, c:c + 128], wcv(s, "p")[:, KEYS * h + WINDOW:KEYS * h + KEYS], eye)
                            ins = eng.transpose(bank(s, 2 + h // 4)[0:64, c:c + 128], wcv(s, "p")[:, KEYS * h:KEYS * h + WINDOW], eye)
                        ins.then_inc(wt.tick("pT", s), 1)
                    for s in range(SLOTS):
                        eng.wait_ge(wv_.sem, wv_.value(run, i, "pT", s))
                        eng.wait_ge(wa.sem, wa.value(run, i, "pT", s))
                        for h in range(8):
                            o = bank(s, 0)[:, 64 * h:64 * h + 64]
                            eng.matmul(o, wcv(s, "pT")[:, 128 * h:128 * h + 128], wcv(s, "v")[:, 64 * h:64 * h + 64], start=True, stop=False)
                            ins = eng.matmul(o, wcv(s, "pTh")[0:64, 128 * h:128 * h + 128], wcv(s, "vh")[0:64, 64 * h:64 * h + 64], start=False, stop=True)
                        ins.then_inc(wt.tick("o", s), 1)

                def finish(i):
                    for s in range(SLOTS):
                        eng.wait_ge(wv_.sem, wv_.value(run, i, "o", s))
                        for n in range(4):
                            ins = eng.transpose(bank(s, 0)[:, 128 * n:128 * n + 128], wcv(s, "o")[:, 128 * n:128 * n + 128], eye)
                        ins.then_inc(wt.tick("oT", s), 1)
                    for s in range(SLOTS):
                        eng.wait_ge(wa.sem, wa.value(run, i, "oT", s))
                        for n in range(4):
                            ins = eng.matmul(bank(s, 0)[:, 0:128], wcv(s, "pT")[:, 128 * n:128 * n + 128], wwo[:, self.depth, n, :],
                                             start=n == 0, stop=n == 3)
                        ins.then_inc(wt.tick("y", s), 1)
                window_loop(eng, base, front, attend, finish)

        GPART = [(0, 128), (128, 128), (256, HID - 256)]
        glu = {last: (steps(f"glu{int(last)}_vector", ["u0", "u1", "u2"] + ["h"] * last, turns=PAIRS),
                      steps(f"glu{int(last)}_scalar", ["gelu0", "gelu1", "gelu2"], turns=PAIRS),
                      steps(f"glu{int(last)}_tensor", ["ag0", "ag1", "ag2", "y"], turns=PAIRS)) for last in (False, True)}
        glu_ones = sem("glu_ones")
        gcv = carve([("u", 3 * 512), ("g", 2 * 512)])

        class Glu:
            def __init__(self, depth, last):
                self.depth, self.last = depth, last

            def vector(self, eng, run, base):
                gv, ga, gt = glu[self.last]
                eng.wait_ge(slot_free, base + SLOTS)
                for s in range(SLOTS):
                    ins = eng.memset(gcv(s, "u")[:, 1024:1536], 1.0)
                ins.then_inc(glu_ones, 1)
                eng.wait_ge(glu_ones, 2 * run + self.last + 1)

                def body(i):
                    for c, (lo, n) in enumerate(GPART):
                        for s in range(SLOTS):
                            eng.wait_ge(ga.sem, ga.value(run, i, f"gelu{c}", s))
                            eng.scalar_tensor_tensor(out=gcv(s, "u")[0:n, 512 * c:512 * c + 512], in0=bank(s, 2 * (c % 2))[0:n, :],
                                                     scalar=w1b[0:n, self.depth, c:c + 1], in1=gcv(s, "g")[0:n, 512 * (c % 2):512 * (c % 2) + 512],
                                                     op0=ALU.add, op1=ALU.mult).then_inc(gv.tick(f"u{c}", s), 1)
                    for s in range(SLOTS):
                        eng.wait_ge(gt.sem, gt.value(run, i, "y", s))
                        eng.tensor_tensor(tiles_of(hs, i, s), tiles_of(hs, i, s), heads(bank(s, 2), TILES), ALU.add)\
                            .then_inc(gv.tick("h", s) if self.last else slot_free, 1 if self.last else TILES)
                    if self.last:
                        for s in range(SLOTS):
                            eng.wait_ge(gv.sem, gv.value(run, i, "h", s))
                            eng.tensor_tensor(tiles_of(x, i, s), tiles_of(x, i, s), tiles_of(hs, i, s), ALU.add).then_inc(slot_free, TILES)
                pair_loop(eng, body)

            def scalar(self, eng, run, base):
                gv, ga, gt = glu[self.last]

                def body(i):
                    for c, (lo, n) in enumerate(GPART):
                        for s in range(SLOTS):
                            if c == 2:
                                eng.wait_ge(gv.sem, gv.value(run, i, "u0", s))
                            eng.wait_ge(gt.sem, gt.value(run, i, f"ag{c}", s))
                            eng.activation(gcv(s, "g")[0:n, 512 * (c % 2):512 * (c % 2) + 512], bank(s, 2 * (c % 2) + 1)[0:n, :], ACT.Gelu,
                                           bias=w1b[0:n, self.depth, 3 + c:4 + c]).then_inc(ga.tick(f"gelu{c}", s), 1)
                pair_loop(eng, body)

            def pool(self, eng, run, base):
                pass

            def tensor(self, eng, run, base):
                gv, ga, gt = glu[self.last]
                eng.wait_ge(slot_free, base + SLOTS)

                def body(i):
                    eng.wait_ge(slot_free, i * (SLOTS * TILES) + (base + SLOTS))
                    for c, (lo, n) in enumerate(GPART):
                        for s in range(SLOTS):
                            if c == 2:
                                eng.wait_ge(gv.sem, gv.value(run, i, "u0", s))
                            for half in range(2):
                                ins = eng.matmul(bank(s, 2 * (c % 2) + half)[0:n, :], w1[:, self.depth, HID * half + lo:HID * half + lo + n],
                                                 batch(feedT, i, s), start=True, stop=True)
                            ins.then_inc(gt.tick(f"ag{c}", s), 1)
                    for s in range(SLOTS):
                        eng.wait_ge(gv.sem, gv.value(run, i, "u2", s))
                        for b in range(TILES):
                            for c, (lo, n) in enumerate(GPART):
                                n += c == 2
                                ins = eng.matmul(bank(s, 2)[:, 128 * b:128 * b + 128], gcv(s, "u")[0:n, 512 * c + 128 * b:512 * c + 128 * b + 128],
                                                 w2[0:n, self.depth, c, :], start=c == 0, stop=c == 2)
                        ins.then_inc(gt.tick("y", s), 1)
                pair_loop(eng, body)

        NORMED = ("plain", "window", "glu", "gates", "routed")
        SQUARED = ("gates", "routed")
        feed = {kind: (steps(f"feed_{kind}_vector", ["stats", "mean", "var"] * (kind in NORMED) + ["xn"] + ["tok"] * (kind == "routed")
                             + ["vms", "xr"] * (kind in SQUARED) + ["kept"] * (kind == "window"), turns=PAIRS),
                       steps(f"feed_{kind}_scalar", ["ss"], turns=PAIRS),
                       steps(f"feed_{kind}_pool", ["rstd"] * (kind in NORMED) + ["rms"] * (kind in SQUARED), turns=PAIRS),
                       steps(f"feed_{kind}_tensor", ["shift"] * (kind == "glu") + ["T"], turns=PAIRS))
                for kind in ("plain", "window", "again", "glu", "gates", "routed")}
        fcv = carve([("xn", 512), ("sq", 512), ("xr", 512), ("tk", 512)])
        FSTATS, FMEAN, FVAR, FSQ, FTOK = 160, 208, 216, 220, 224
        feed_var = lambda s: stat(s, FVAR, TILES)
        feed_sq = lambda s: stat(s, FSQ, TILES)

        class Feed:
            def __init__(self, kind, depth=0):
                self.kind, self.depth = kind, depth
                self.result = "xr" if kind in SQUARED else "xn"

            def tile(self, ap, i, s, k, lo=0, n=D):
                return ap[:, bass.ds(i * (SLOTS * TILES) + (s * TILES + k), 1), lo:lo + n]

            def parts(self, i, s, k):
                if self.kind == "glu":
                    return [(self.tile(hs, i, s, k, 0, 64), 0, 64), (bank(s, 0)[:, 64 * k:64 * k + 64], 64, 64)]
                return [(self.tile(x, i, s, k), 0, D)]

            def vector(self, eng, run, base):
                fv, fa, fp, ft = feed[self.kind]

                def normed(i):
                    for s in range(SLOTS):
                        if self.kind == "glu":
                            eng.wait_ge(ft.sem, ft.value(run, i, "shift", s))
                        for k in range(TILES):
                            for n, (part, _, _) in enumerate(self.parts(i, s, k)):
                                ins = eng.bn_stats(stat(s, FSTATS + 12 * k + 6 * n, 6), part)
                        ins.then_inc(fv.tick("stats", s), 1)
                    for s in range(SLOTS):
                        eng.wait_ge(fv.sem, fv.value(run, i, "stats", s))
                        eng.memset(stat(s, 22), 0.0)
                        for k in range(TILES):
                            ins = eng.bn_aggr(stat(s, FMEAN + 2 * k, 2), stat(s, FSTATS + 12 * k, 12 if self.kind == "glu" else 6))
                        ins.then_inc(fv.tick("mean", s), 1)
                    for s in range(SLOTS):
                        eng.wait_ge(fv.sem, fv.value(run, i, "mean", s))
                        eng.tensor_scalar(feed_var(s), stat(s, FMEAN, 2 * TILES).rearrange("p (k a) -> p k a", a=2)[:, :, 1], LN_EPS, None, ALU.add)\
                            .then_inc(fv.tick("var", s), 1)
                    for s in range(SLOTS):
                        eng.wait_ge(fp.sem, fp.value(run, i, "rstd", s))
                        for k in range(TILES):
                            for part, lo, n in self.parts(i, s, k):
                                ins = eng.tensor_scalar(fcv(s, "xn")[:, D * k + lo:D * k + lo + n], part, stat(s, FMEAN + 2 * k), stat(s, FVAR + k),
                                                        ALU.subtract, ALU.mult)
                        ins.then_inc(fv.tick("xn", s), 1)

                def body(i):
                    eng.wait_ge(slot_free, i * (SLOTS * TILES) + (base + SLOTS))
                    if self.kind in NORMED:
                        normed(i)
                    else:
                        for s in range(SLOTS):
                            eng.tensor_scalar(heads(fcv(s, "xn"), TILES), tiles_of(hs, i, s), 1.0, None, ALU.mult).then_inc(fv.tick("xn", s), 1)
                    if self.kind == "routed":
                        for s in range(SLOTS):
                            eng.wait_ge(fv.sem, fv.value(run, i, "xn", s))
                            for k in range(TILES):
                                at = slice(D * k, D * k + D)
                                ins = eng.tensor_tensor_reduce(out=fcv(s, "tk")[:, at], in0=fcv(s, "xn")[:, at], in1=token[:, :], scale=1.0, scalar=0.0,
                                                               op0=ALU.mult, op1=ALU.add, accum_out=stat(s, FTOK + k))
                            ins.then_inc(fv.tick("tok", s), 1)
                    if self.kind in SQUARED:
                        for s in range(SLOTS):
                            eng.wait_ge(fa.sem, fa.value(run, i, "ss", s))
                            if self.kind == "routed":
                                ins = eng.tensor_scalar(feed_sq(s), feed_sq(s), 1e-24, None, ALU.max)
                            else:
                                ins = eng.tensor_scalar(feed_sq(s), feed_sq(s), LN_EPS, None, ALU.add)
                            ins.then_inc(fv.tick("vms", s), 1)
                        for s in range(SLOTS):
                            eng.wait_ge(fp.sem, fp.value(run, i, "rms", s))
                            eng.tensor_tensor(heads(fcv(s, "xr"), TILES), heads(fcv(s, "xn"), TILES), over(feed_sq(s), TILES, D), ALU.mult)\
                                .then_inc(fv.tick("xr", s), 1)
                    if self.kind == "window":
                        for s in range(SLOTS):
                            eng.wait_ge(fv.sem, fv.value(run, i, "xn", s))
                            eng.tensor_scalar(tiles_of(hs, i, s), heads(fcv(s, "xn"), TILES), 1.0, None, ALU.mult).then_inc(fv.tick("kept", s), 1)
                    for s in range(SLOTS):
                        eng.wait_ge(ft.sem, ft.value(run, i, "T", s))
                        if self.kind == "routed":
                            eng.tensor_scalar(scores[:, bass.ds(i * (SLOTS * TILES) + s * TILES, TILES)], stat(s, FTOK, TILES), 1.0, None, ALU.mult)
                        if self.kind == "gates":
                            eng.tensor_tensor(tiles_of(x, i, s), tiles_of(x, i, s), heads(fcv(s, "xn"), TILES), ALU.add)
                        b = bass.ds(i * SLOTS + s, 1)
                        if self.kind in ("window", "again"):
                            eng.tensor_scalar(feedT[0:64, b, :], bank(s, 1)[0:64, :], 1.0, None, ALU.mult)
                            eng.tensor_scalar(feedT[64:128, b, 0:1], zero[64:128, :], 1.0, None, ALU.mult)
                            ins = eng.tensor_scalar(feedT[64:128, b, 1:N], bank(s, 1)[64:128, 0:N - 1], 1.0, None, ALU.mult)
                        elif self.kind == "glu":
                            ins = eng.tensor_scalar(batch(feedT, i, s), bank(s, 1), lgb[:, self.depth, 0:1], lgb[:, self.depth, 1:2], ALU.mult, ALU.add)
                        else:
                            ins = eng.tensor_scalar(batch(feedT, i, s), bank(s, 1), 1.0, None, ALU.mult)
                        ins.then_inc(slot_free, TILES)
                pair_loop(eng, body)

            def scalar(self, eng, run, base):
                fv, fa, fp, ft = feed[self.kind]

                def body(i):
                    for s in range(SLOTS):
                        eng.wait_ge(fv.sem, fv.value(run, i, "xn", s))
                        for k in range(TILES):
                            at = slice(D * k, D * k + D)
                            ins = eng.activation(fcv(s, "sq")[:, at], fcv(s, "xn")[:, at], ACT.Square, scale=D ** -0.5 if self.kind == "gates" else 1.0,
                                                 accum_out=stat(s, FSQ + k))
                        ins.then_inc(fa.tick("ss", s), 1)
                if self.kind in SQUARED:
                    pair_loop(eng, body)

            def pool(self, eng, run, base):
                fv, fa, fp, ft = feed[self.kind]

                def body(i):
                    root_pool(eng, fv, fp, run, i, "var", feed_var, "rstd")
                    if self.kind in SQUARED:
                        root_pool(eng, fv, fp, run, i, "vms", feed_sq, "rms")
                if self.kind in NORMED:
                    pair_loop(eng, body)

            def tensor(self, eng, run, base):
                fv, fa, fp, ft = feed[self.kind]

                def body(i):
                    eng.wait_ge(slot_free, i * (SLOTS * TILES) + (base + SLOTS))
                    if self.kind == "glu":
                        for s in range(SLOTS):
                            for k in range(TILES):
                                o = bank(s, 0)[:, 64 * k:64 * k + 64]
                                if k:
                                    eng.matmul(o, masks[:, M_LAST, :], self.tile(hs, i, s, k - 1, 64, 64), start=True, stop=False)
                                ins = eng.matmul(o, masks[:, M_SHIFT, :], self.tile(hs, i, s, k, 64, 64), start=k == 0, stop=True)
                            ins.then_inc(ft.tick("shift", s), 1)
                    for s in range(SLOTS):
                        eng.wait_ge(fv.sem, fv.value(run, i, self.result, s))
                        for k in range(TILES):
                            ins = eng.transpose(bank(s, 1)[:, D * k:D * k + D], fcv(s, self.result)[:, D * k:D * k + D], eye)
                        ins.then_inc(ft.tick("T", s), 1)
                pair_loop(eng, body)

        sv = steps("state_vector", ["cu", "su", "u", "scan", "p", "y"], turns=PAIRS)
        spl = steps("state_pool", ["q"], turns=PAIRS)
        st = steps("state_tensor", ["u", "y", "out"], turns=PAIRS)
        scv = carve([("a", 512), ("b", 512), ("g", 512), ("p", 512), ("q", 512), ("y", 512)])
        sm = sb("sm", [128, 24])
        smi = sb("smi", [128, 2], I32)
        decay = sb("decay", [128, N])

        class State:
            def vector(self, eng, run, base):
                eng.wait_ge(slot_free, base + SLOTS)
                cos, sin = turns[:, 0, 1:N + 1], turns[:, 1, 1:N + 1]

                def body(i):
                    for s in range(SLOTS):
                        eng.wait_ge(st.sem, st.value(run, i, "u", s))
                        eng.tensor_tensor(scv(s, "a"), bank(s, 0), cos, ALU.mult).then_inc(sv.tick("cu", s), 1)
                    for s in range(SLOTS):
                        eng.tensor_tensor(scv(s, "b"), bank(s, 1), sin, ALU.mult).then_inc(sv.tick("su", s), 1)
                    for s in range(SLOTS):
                        eng.wait_ge(sv.sem, sv.value(run, i, "su", s))
                        eng.tensor_tensor(scv(s, "a"), scv(s, "a"), scv(s, "b"), ALU.add).then_inc(sv.tick("u", s), 1)
                    for s in range(SLOTS):
                        eng.wait_ge(sv.sem, sv.value(run, i, "u", s))
                        eng.tensor_tensor_scan(scv(s, "g"), decay[:, :], scv(s, "a"), 0.0, ALU.mult, ALU.add).then_inc(sv.tick("scan", s), 1)
                    for s in range(SLOTS):
                        eng.wait_ge(sv.sem, sv.value(run, i, "scan", s))
                        eng.tensor_tensor(scv(s, "p"), scv(s, "g"), cos, ALU.mult).then_inc(sv.tick("p", s), 1)
                    for s in range(SLOTS):
                        eng.wait_ge(st.sem, st.value(run, i, "y", s))
                        eng.scalar_tensor_tensor(out=scv(s, "y"), in0=batch(feedT, i, s), scalar=sD[:, 0:1], in1=bank(s, 2),
                                                 op0=ALU.mult, op1=ALU.add).then_inc(sv.tick("y", s), 1)
                    for s in range(SLOTS):
                        eng.wait_ge(st.sem, st.value(run, i, "out", s))
                        eng.tensor_tensor(tiles_of(x, i, s), tiles_of(x, i, s), heads(bank(s, 3), TILES), ALU.add).then_inc(slot_free, TILES)
                pair_loop(eng, body)

            def scalar(self, eng, run, base):
                pass

            def pool(self, eng, run, base):
                def body(i):
                    for s in range(SLOTS):
                        eng.wait_ge(sv.sem, sv.value(run, i, "scan", s))
                        eng.tensor_tensor(scv(s, "q"), scv(s, "g"), turns[:, 1, 1:N + 1], ALU.mult).then_inc(spl.tick("q", s), 1)
                pair_loop(eng, body)

            def tensor(self, eng, run, base):
                def body(i):
                    eng.wait_ge(slot_free, i * (SLOTS * TILES) + (base + SLOTS))
                    for s in range(SLOTS):
                        eng.matmul(bank(s, 0), sB[:, 0, :], batch(feedT, i, s), start=True, stop=True)
                        eng.matmul(bank(s, 1), sB[:, 1, :], batch(feedT, i, s), start=True, stop=True).then_inc(st.tick("u", s), 1)
                    for s in range(SLOTS):
                        eng.wait_ge(sv.sem, sv.value(run, i, "p", s))
                        eng.matmul(bank(s, 2), sC[:, 0, :], scv(s, "p"), start=True, stop=False)
                        eng.wait_ge(spl.sem, spl.value(run, i, "q", s))
                        eng.matmul(bank(s, 2), sC[:, 1, :], scv(s, "q"), start=False, stop=True).then_inc(st.tick("y", s), 1)
                    for s in range(SLOTS):
                        eng.wait_ge(sv.sem, sv.value(run, i, "y", s))
                        for b in range(TILES):
                            eng.matmul(bank(s, 3)[:, 128 * b:128 * b + 128], scv(s, "y")[:, 128 * b:128 * b + 128], sWo[:, :], start=True, stop=False)
                            ins = eng.matmul(bank(s, 3)[:, 128 * b:128 * b + 128], ones_row[:, :], sbo[:, :], start=False, stop=True)
                        ins.then_inc(st.tick("out", s), 1)
                pair_loop(eng, body)

        QUADS = 4
        cvv = steps("causal_vector", ["xT", "qT"])
        ca = steps("causal_scalar", ["kT", "v"])
        ct = steps("causal_tensor", ["q", "kv"])
        ccv = carve([("o", 128), ("xT", 128), ("qT", 512 * TILES), ("kT", 512 * TILES), ("v", 128 * TILES), ("p", 4 * N), ("pT", 4 * N)])
        cvv2 = steps("attend_vector", [x_ for j in range(TILES) for q in range(QUADS) for x_ in (f"max{j}{q}", f"pT{j}{q}", f"rz{j}{q}", f"o{j}{q}")], turns=PAIRS)
        ca2 = steps("attend_scalar", [x_ for j in range(TILES) for x_ in [y_ for q in range(QUADS) for y_ in (f"p{j}{q}", f"pT{j}{q}")] + [f"oT{j}"]], turns=PAIRS)
        ct2 = steps("attend_tensor", [x_ for j in range(TILES) for x_ in [y_ for q in range(QUADS) for y_ in (f"sim{j}{q}", f"pT{j}{q}", f"o{j}{q}")] + [f"oT{j}", f"y{j}"]], turns=PAIRS)
        CMAX, CZ, CRZ = 96, 112, 128
        c_scale = CAUSAL_D ** -0.5

        class Causal:
            def vector(self, eng, run, base):
                with eng.Fori(0, PAIRS) as pair:
                    for j in range(TILES):
                        i = Turn(pair, j)
                        if j == 0:
                            eng.wait_ge(slot_free, pair * (SLOTS * TILES) + (base + SLOTS))
                        for s in range(SLOTS):
                            if j:
                                eng.wait_ge(ct.sem, ct.value(run, Turn(pair, j - 1), "kv", s))
                            eng.tensor_scalar(ccv(s, "xT"), tileT(i, s), 1.0, None, ALU.mult).then_inc(cvv.tick("xT", s), 1)
                        for s in range(SLOTS):
                            eng.wait_ge(ct.sem, ct.value(run, i, "q", s))
                            eng.tensor_scalar(ccv(s, "qT")[:, 512 * j:512 * j + 512], bank(s, 1), c_scale, None, ALU.mult).then_inc(cvv.tick("qT", s), 1)
                    for j in range(TILES):
                        keys = T * (j + 1)
                        for q in range(QUADS):
                            for s in range(SLOTS):
                                eng.wait_ge(ct2.sem, ct2.value(run, pair, f"sim{j}{q}", s))
                                for h in range(4):
                                    ins = eng.tensor_reduce(stat(s, CMAX + h), bank(s, h)[:, 0:keys], AX.X, ALU.max, negate=True)
                                ins.then_inc(cvv2.tick(f"max{j}{q}", s), 1)
                            for s in range(SLOTS):
                                eng.wait_ge(ct2.sem, ct2.value(run, pair, f"pT{j}{q}", s))
                                for h in range(2):
                                    ins = eng.tensor_copy(ccv(s, "pT")[:, N * h:N * h + keys], bank(s, h)[:, 0:keys])
                                ins.then_inc(cvv2.tick(f"pT{j}{q}", s), 1)
                            for s in range(SLOTS):
                                eng.wait_ge(ca2.sem, ca2.value(run, pair, f"p{j}{q}", s))
                                eng.reciprocal(stat(s, CRZ, 4), stat(s, CZ, 4)).then_inc(cvv2.tick(f"rz{j}{q}", s), 1)
                            for s in range(SLOTS):
                                eng.wait_ge(ct2.sem, ct2.value(run, pair, f"o{j}{q}", s))
                                eng.wait_ge(cvv2.sem, cvv2.value(run, pair, f"rz{j}{q}", s))
                                eng.tensor_tensor(heads(ccv(s, "o")[:, 32 * q:32 * q + 32], 4), heads(bank(s, 0)[:, 0:32], 4),
                                                  over(stat(s, CRZ, 4), 4, CAUSAL_D), ALU.mult).then_inc(cvv2.tick(f"o{j}{q}", s), 1)
                        for s in range(SLOTS):
                            eng.wait_ge(ct2.sem, ct2.value(run, pair, f"y{j}", s))
                            eng.tensor_tensor(xb(Turn(pair, j), s), xb(Turn(pair, j), s), bank(s, 2)[:, 0:128], ALU.add).then_inc(slot_free, 1)

            def scalar(self, eng, run, base):
                with eng.Fori(0, PAIRS) as pair:
                    for j in range(TILES):
                        i = Turn(pair, j)
                        for s in range(SLOTS):
                            eng.wait_ge(ct.sem, ct.value(run, i, "kv", s))
                            eng.activation(ccv(s, "kT")[:, 512 * j:512 * j + 512], bank(s, 2), ACT.Copy).then_inc(ca.tick("kT", s), 1)
                        for s in range(SLOTS):
                            eng.activation(ccv(s, "v")[:, 128 * j:128 * j + 128], bank(s, 3)[:, 0:128], ACT.Copy).then_inc(ca.tick("v", s), 1)
                    for j in range(TILES):
                        keys = T * (j + 1)
                        for q in range(QUADS):
                            for s in range(SLOTS):
                                eng.wait_ge(cvv2.sem, cvv2.value(run, pair, f"max{j}{q}", s))
                                for h in range(4):
                                    ins = eng.activation(ccv(s, "p")[:, N * h:N * h + keys], bank(s, h)[:, 0:keys], ACT.Exp, bias=stat(s, CMAX + h),
                                                         accum_out=stat(s, CZ + h))
                                ins.then_inc(ca2.tick(f"p{j}{q}", s), 1)
                            for s in range(SLOTS):
                                eng.wait_ge(ct2.sem, ct2.value(run, pair, f"pT{j}{q}", s))
                                for h in range(2, 4):
                                    ins = eng.activation(ccv(s, "pT")[:, N * h:N * h + keys], bank(s, h)[:, 0:keys], ACT.Copy)
                                ins.then_inc(ca2.tick(f"pT{j}{q}", s), 1)
                        for s in range(SLOTS):
                            eng.wait_ge(ct2.sem, ct2.value(run, pair, f"oT{j}", s))
                            eng.activation(ccv(s, "xT"), bank(s, 1)[:, 0:128], ACT.Copy).then_inc(ca2.tick(f"oT{j}", s), 1)

            def pool(self, eng, run, base):
                pass

            def tensor(self, eng, run, base):
                with eng.Fori(0, PAIRS) as pair:
                    for j in range(TILES):
                        i = Turn(pair, j)
                        if j == 0:
                            eng.wait_ge(slot_free, pair * (SLOTS * TILES) + (base + SLOTS))
                        for s in range(SLOTS):
                            eng.wait_ge(cvv.sem, cvv.value(run, i, "xT", s))
                            if j:
                                eng.wait_ge(cvv.sem, cvv.value(run, Turn(pair, j - 1), "qT", s))
                            for n in range(4):
                                ins = eng.matmul(bank(s, 1)[:, 128 * n:128 * n + 128], cqk[:, 0, n, :], ccv(s, "xT"), start=True, stop=True)
                            ins.then_inc(ct.tick("q", s), 1)
                        for s in range(SLOTS):
                            if j:
                                eng.wait_ge(ca.sem, ca.value(run, Turn(pair, j - 1), "v", s))
                            for n in range(4):
                                eng.matmul(bank(s, 2)[:, 128 * n:128 * n + 128], cqk[:, 1, n, :], ccv(s, "xT"), start=True, stop=True)
                            eng.matmul(bank(s, 3)[:, 0:128], ccv(s, "xT"), cv[:, :], start=True, stop=True).then_inc(ct.tick("kv", s), 1)
                    for j in range(TILES):
                        for q in range(QUADS):
                            for s in range(SLOTS):
                                if j == 0 and q == 0:
                                    eng.wait_ge(cvv.sem, cvv.value(run, Turn(pair, TILES - 1), "qT", s))
                                    eng.wait_ge(ca.sem, ca.value(run, Turn(pair, TILES - 1), "v", s))
                                elif q:
                                    eng.wait_ge(cvv2.sem, cvv2.value(run, pair, f"o{j}{q - 1}", s))
                                else:
                                    eng.wait_ge(slot_free, pair * (SLOTS * TILES) + (base + SLOTS * j + s + 1))
                                for k in range(j + 1):
                                    for h in range(4):
                                        o = bank(s, h)[:, 128 * k:128 * k + 128]
                                        ins = eng.matmul(o, ccv(s, "qT")[32 * h:32 * h + 32, 512 * j + 128 * q:512 * j + 128 * q + 128],
                                                         ccv(s, "kT")[32 * h:32 * h + 32, 512 * k + 128 * q:512 * k + 128 * q + 128], start=True, stop=k < j)
                                for h in range(4):
                                    ins = eng.matmul(bank(s, h)[:, T * j:T * j + T], eyeb, causal_mask[:, :], start=False, stop=True)
                                ins.then_inc(ct2.tick(f"sim{j}{q}", s), 1)
                            for s in range(SLOTS):
                                eng.wait_ge(ca2.sem, ca2.value(run, pair, f"p{j}{q}", s))
                                for h in range(4):
                                    for k in range(j + 1):
                                        ins = eng.transpose(bank(s, h)[:, 128 * k:128 * k + 128], ccv(s, "p")[:, N * h + 128 * k:N * h + 128 * k + 128], eye)
                                ins.then_inc(ct2.tick(f"pT{j}{q}", s), 1)
                            for s in range(SLOTS):
                                eng.wait_ge(cvv2.sem, cvv2.value(run, pair, f"pT{j}{q}", s))
                                eng.wait_ge(ca2.sem, ca2.value(run, pair, f"pT{j}{q}", s))
                                for h in range(4):
                                    for k in range(j + 1):
                                        at = 128 * k + 32 * q + 8 * h
                                        ins = eng.matmul(bank(s, 0)[:, 8 * h:8 * h + 8], ccv(s, "pT")[:, N * h + 128 * k:N * h + 128 * k + 128],
                                                         ccv(s, "v")[:, at:at + 8], start=k == 0, stop=k == j)
                                ins.then_inc(ct2.tick(f"o{j}{q}", s), 1)
                        for s in range(SLOTS):
                            eng.wait_ge(cvv2.sem, cvv2.value(run, pair, f"o{j}{QUADS - 1}", s))
                            eng.transpose(bank(s, 1)[:, 0:128], ccv(s, "o"), eye).then_inc(ct2.tick(f"oT{j}", s), 1)
                        for s in range(SLOTS):
                            eng.wait_ge(ca2.sem, ca2.value(run, pair, f"oT{j}", s))
                            eng.matmul(bank(s, 2)[:, 0:128], ccv(s, "xT"), cwo[:, :], start=True, stop=True).then_inc(ct2.tick(f"y{j}", s), 1)

        RPART = [128, 128, 128, 128, LIGHT]
        rv = steps("routed_vector", ["light"], turns=PAIRS)
        ra = steps("routed_scalar", [f"gelu{c}" for c in range(5)], turns=PAIRS)
        rt = steps("routed_tensor", [f"h{c}" for c in range(5)] + ["y"], turns=PAIRS)
        rcv = carve([("u", 5 * 512)])
        rset = sem("routed_ones")
        descent_in = sem("descent_scores")
        dd = sem("descent_vector")
        dac = sem("descent_scalar")
        key_T = sem("descent_back")
        key_cols = sem("descent_columns")
        row_out = sem("rank_row")
        rank_done = sem("rank_step")
        route = sb("route", [B, 12])
        LMAX, NA, MX, ZS, LZ, NMX = 0, 1, 2, 3, 4, 5
        picked = sb("picked", [128, 2, TILES, B])
        rank = sb("rank", [128, 2, 2])
        S_ = lambda: arena[0:B, 0, 0:N]
        T_ = lambda: arena[0:B, 0, N:2 * N]
        E_ = lambda: arena[0:B, 0, 2 * N:3 * N]
        K_ = lambda: arena[0:B, 0, 3 * N:4 * N]
        W_ = lambda: arena[0:B, 0, 4 * N:5 * N]
        CMP = lambda g: arena[:, 0, (5 + g) * N:(6 + g) * N]
        LOGK = float(np.log(np.float32(FETCH)))
        RANKS = B * TILES

        class Routed:
            def vector(self, eng, run, base):
                n = [run * DESCENT]

                def link(ins):
                    n[0] += 1
                    ins.then_inc(dd, 1)
                    eng.wait_ge(dd, n[0])

                eng.wait_ge(slot_free, base + SLOTS)
                for s in range(SLOTS):
                    ins = eng.memset(rcv(s, "u")[64:128, 2048:2560], 1.0)
                ins.then_inc(rset, 1)
                eng.wait_ge(rset, run + 1)
                eng.wait_ge(descent_in, run + 1)
                eng.tensor_copy(S_(), P[0:B, 0, :]).then_inc(dd, 1)
                n[0] += 1
                eng.wait_ge(dd, n[0])
                link(eng.tensor_reduce(route[:, LMAX:LMAX + 1], S_(), AX.X, ALU.max))
                eng.memset(route[:, NA:NA + 1], float(np.log(np.float32(N))) - LOGK)
                eng.memset(route[:, MX:MX + 1], 0.0).then_inc(dd, 1)
                n[0] += 1
                eng.wait_ge(dd, n[0])
                link(eng.tensor_tensor(route[:, MX:MX + 1], route[:, LMAX:LMAX + 1], route[:, NA:NA + 1], ALU.min))
                start = n[0]
                with eng.Fori(0, ITERS - 1) as it:
                    eng.tensor_scalar(T_(), S_(), route[:, NA:NA + 1], route[:, MX:MX + 1], ALU.min, ALU.subtract).then_inc(dd, 1)
                    eng.wait_ge(dac, it * 2 + (run * 2 * (ITERS - 1) + 2))
                    eng.scalar_tensor_tensor(out=route[:, NA:NA + 1], in0=route[:, LZ:LZ + 1], scalar=-LOGK, in1=route[:, MX:MX + 1],
                                             op0=ALU.add, op1=ALU.add).then_inc(dd, 1)
                    eng.wait_ge(dd, it * 3 + (start + 2))
                    eng.tensor_tensor(route[:, MX:MX + 1], route[:, LMAX:LMAX + 1], route[:, NA:NA + 1], ALU.min).then_inc(dd, 1)
                    eng.wait_ge(dd, it * 3 + (start + 3))
                n[0] = start + 3 * (ITERS - 1)
                link(eng.tensor_scalar(T_(), S_(), route[:, NA:NA + 1], 0.0, ALU.subtract, ALU.min))
                link(eng.scalar_tensor_tensor(out=K_(), in0=T_(), scalar=-2.0 ** -25, in1=T_(), op0=ALU.is_lt, op1=ALU.mult))
                eng.wait_ge(exp_key, run + 1)
                link(eng.tensor_scalar(T_(), E_(), -1.0, 1.0, ALU.mult, ALU.add))
                link(eng.tensor_tensor(W_(), T_(), E_(), ALU.add))
                assert n[0] == run * DESCENT + DESCENT, (n[0], DESCENT)
                eng.wait_ge(key_T, run + 1)
                eng.tensor_copy(picked[:, :, :, :].rearrange("p a j b -> p (a j b)"), P[:, 1, 0:2 * TILES * B]).then_inc(key_cols, 1)
                eng.wait_ge(key_cols, run + 1)
                for b in range(B):
                    for j in range(TILES):
                        m = b * TILES + j
                        if j == 0:
                            eng.wait_ge(row_out, run * B + b + 1)
                        row = P[:, 2 + b % 2, :]
                        key = picked[:, 0, j, b:b + 1]
                        g = m % 2
                        eng.tensor_scalar(CMP(0), row, key, 0.0, ALU.is_gt, ALU.add, accum_out=rank[:, g, 0:1])
                        eng.scalar_tensor_tensor(out=CMP(1), in0=row, scalar=key, in1=before[:, 384 - 128 * j:384 - 128 * j + N],
                                                 op0=ALU.is_equal, op1=ALU.mult, accum_out=rank[:, g, 1:2]).then_inc(rank_done, 1)
                        eng.wait_ge(rank_done, (run * RANKS + m) * 3 + 1)
                        eng.tensor_tensor(rank[:, g, 0:1], rank[:, g, 0:1], rank[:, g, 1:2], ALU.add).then_inc(rank_done, 1)
                        eng.wait_ge(rank_done, (run * RANKS + m) * 3 + 2)
                        eng.scalar_tensor_tensor(out=weight[:, m:m + 1], in0=rank[:, g, 0:1], scalar=float(KEEP), in1=picked[:, 1, j, b:b + 1],
                                                 op0=ALU.is_lt, op1=ALU.mult).then_inc(rank_done, 1)
                eng.wait_ge(rank_done, (run + 1) * RANKS * 3)

                def body(i):
                    for s in range(SLOTS):
                        eng.wait_ge(rt.sem, rt.value(run, i, "y", s))
                        eng.tensor_tensor(tiles_of(x, i, s), tiles_of(x, i, s), heads(bank(s, 3), TILES), ALU.add).then_inc(rv.tick("light", s), 1)
                    for s in range(SLOTS):
                        eng.wait_ge(rv.sem, rv.value(run, i, "light", s))
                        for k in range(TILES):
                            at = i * (SLOTS * TILES) + (s * TILES + k)
                            ins = eng.scalar_tensor_tensor(out=x[:, bass.ds(at, 1), :], in0=bank(s, 0)[:, 128 * k:128 * k + 128],
                                                           scalar=weight[:, bass.ds(at, 1)], in1=x[:, bass.ds(at, 1), :], op0=ALU.mult, op1=ALU.add)
                        ins.then_inc(slot_free, TILES)
                pair_loop(eng, body)

            def scalar(self, eng, run, base):
                first = run * DESCENT + 4
                eng.preload_act_table_set("natural_log_exp_and_others")
                with eng.Fori(0, ITERS - 1) as it:
                    eng.wait_ge(dd, it * 3 + (first + 1))
                    eng.activation(E_(), T_(), ACT.Exp, accum_out=route[:, ZS:ZS + 1]).then_inc(dac, 1)
                    eng.wait_ge(dac, it * 2 + (run * 2 * (ITERS - 1) + 1))
                    eng.activation(route[:, LZ:LZ + 1], route[:, ZS:ZS + 1], ACT.Ln).then_inc(dac, 1)
                eng.wait_ge(dd, first + 3 * (ITERS - 1) + 2)
                eng.activation(E_(), K_(), ACT.Exp).then_inc(exp_key, 1)
                eng.wait_ge(rank_done, (run + 1) * RANKS * 3)

                def body(i):
                    for c, n in enumerate(RPART):
                        for s in range(SLOTS):
                            eng.wait_ge(rt.sem, rt.value(run, i, f"h{c}", s))
                            eng.activation(rcv(s, "u")[0:n, 512 * c:512 * c + 512], bank(s, c % 3)[0:n, :], ACT.Gelu,
                                           bias=fb1[0:n, c:c + 1]).then_inc(ra.tick(f"gelu{c}", s), 1)
                pair_loop(eng, body)

            def pool(self, eng, run, base):
                pass

            def tensor(self, eng, run, base):
                eng.wait_ge(slot_free, base + SLOTS)
                for j in range(TILES):
                    ins = eng.transpose(P[0:B, 0, 128 * j:128 * j + 128], scores[:, :].rearrange("p (b j) -> p j b", j=TILES)[:, j, :], eye)
                ins.then_inc(descent_in, 1)
                eng.wait_ge(dd, run * DESCENT + DESCENT)
                for a, src in enumerate((K_(), W_())):
                    for j in range(TILES):
                        at = (a * TILES + j) * B
                        ins = eng.transpose(P[:, 1, at:at + B], src[:, 128 * j:128 * j + 128], masks[0:B, M_EYE, 0:B])
                ins.then_inc(key_T, 1)
                for b in range(B):
                    if b >= 2:
                        eng.wait_ge(rank_done, (run * RANKS + (b - 1) * TILES) * 3)
                    eng.matmul(P[:, 2 + b % 2, :], pick[:, b, :], K_(), start=True, stop=True).then_inc(row_out, 1)
                eng.wait_ge(rank_done, (run + 1) * RANKS * 3)

                def body(i):
                    eng.wait_ge(slot_free, i * (SLOTS * TILES) + (base + SLOTS))
                    for c, n in enumerate(RPART):
                        for s in range(SLOTS):
                            if c >= 3:
                                eng.wait_ge(ra.sem, ra.value(run, i, f"gelu{c - 3}", s))
                            eng.matmul(bank(s, c % 3), fw1[:, 128 * c:128 * c + 128], batch(feedT, i, s), start=True, stop=True)\
                                .then_inc(rt.tick(f"h{c}", s), 1)
                    for s in range(SLOTS):
                        eng.wait_ge(ra.sem, ra.value(run, i, "gelu4", s))
                        for b in range(TILES):
                            u = lambda c, n: rcv(s, "u")[0:n, 512 * c + 128 * b:512 * c + 128 * b + 128]
                            eng.matmul(bank(s, 3)[:, 128 * b:128 * b + 128], u(4, LIGHT + 1), fw2[0:LIGHT + 1, 4, :], start=True, stop=True)
                            heavy = bank(s, 0)[:, 128 * b:128 * b + 128]
                            for c in range(4):
                                eng.matmul(heavy, u(c, 128), fw2[:, c, :], start=c == 0, stop=False)
                            ins = eng.matmul(heavy, ones_row[:, :], fb2[:, :], start=False, stop=True)
                        ins.then_inc(rt.tick("y", s), 1)
                pair_loop(eng, body)

        DESCENT = 8 + 3 * (ITERS - 1)
        exp_key = sem("descent_exponential")

        SCAN_TURNS = CHUNKS // SLOTS
        gates_vector = sem("gates_vector")
        gates_scalar = sem("gates_scalar")
        gates_pool = sem("gates_pool")
        gates_tensor = sem("gates_tensor")
        GATE_STEPS = {"max": (gates_vector, 4, 1), "less": (gates_vector, 4, 2), "z": (gates_vector, 4, 3), "rz": (gates_vector, 4, 4),
                      "in": (gates_scalar, 3, 1), "v": (gates_scalar, 3, 2), "e": (gates_scalar, 3, 3),
                      "g": (gates_pool, 2, 1), "gv": (gates_pool, 2, 2), "logits": (gates_tensor, 1, 1)}

        def gates_wait(eng, i, name, s, turns_back=0):
            sem_, per, at = GATE_STEPS[name]
            eng.wait_ge(sem_, i * (SLOTS * per) + (SLOTS * per * (1 - turns_back) + per * s + at))

        mcv = carve([("e", GATES), ("in", 128), ("v", 128), ("mx", 128), ("z", 128), ("rz", 128), ("ring", CHUNK * SCAN_M * CELL)])
        chains = B * SCAN_H
        states = sb("states", [chains, SLOTS, CHUNK + 1, SCAN_M])
        chunk_done = sem("chunk_scanned")
        moved_out = [sem(f"gates_out_{s}") for s in range(SLOTS)]
        moved = [sem(f"gates_moved_{s}") for s in range(SLOTS)]
        saved = [sem(f"states_saved_{s}") for s in range(SLOTS)]
        step_done = sem("scan_step")
        saving = sem("states_being_saved")
        BANKED = [(n * BANK_ROWS, min(BANK_ROWS, ROWS - n * BANK_ROWS)) for n in range(-(-ROWS // BANK_ROWS))]
        gates_dram = nc.dram_tensor("gates_by_chain", [SLOTS, B, SCAN_H, CHUNK, SCAN_M * CELL], F32).ap()
        mixed = nc.dram_tensor("scan_by_token", [B, N, SCAN_H, SCAN_M], F32).ap()
        STEPS = 2 * CHUNK + 1

        MOVES = 16 * B

        class Scan:

            def vector(self, eng, run, base):
                eng.wait_ge(slot_free, base + SLOTS)
                eng.memset(states[:, :, :, :], 0.0).then_inc(chunk_done, 1)
                eng.wait_ge(chunk_done, 1)
                eng.sem_inc(chunk_done, 1)
                eng.sem_inc(step_done, 1)
                for sem_, per in ((gates_vector, 4), (gates_scalar, 3), (gates_pool, 2), (gates_tensor, 1)):
                    eng.sem_inc(sem_, SLOTS * per)
                view = lambda n, k: P[:, n, 0:CELL * k].rearrange("p (r c) -> p r c", c=CELL)

                def less_max(i, s):
                    gates_wait(eng, i, "logits", s)
                    for n, (lo, k) in enumerate(BANKED):
                        ins = eng.tensor_reduce(mcv(s, "mx")[:, lo:lo + k], view(n, k), AX.X, ALU.max)
                    ins.then_inc(gates_vector, 1)
                    gates_wait(eng, i, "max", s)
                    eng.wait_ge(moved_out[s], i * MOVES + MOVES)
                    for n, (lo, k) in enumerate(BANKED):
                        ins = eng.tensor_tensor(mcv(s, "e")[:, CELL * lo:CELL * (lo + k)].rearrange("p (r c) -> p r c", c=CELL), view(n, k),
                                                over(mcv(s, "mx")[:, lo:lo + k], k, CELL), ALU.subtract)
                    ins.then_inc(gates_vector, 1)

                def sums(i, s):
                    gates_wait(eng, i, "e", s)
                    eng.tensor_reduce(mcv(s, "z"), heads(mcv(s, "e"), ROWS), AX.X, ALU.add).then_inc(gates_vector, 1)
                    gates_wait(eng, i, "z", s)
                    eng.reciprocal(mcv(s, "rz"), mcv(s, "z")).then_inc(gates_vector, 1)

                def scan(i, s):
                    eng.wait_ge(moved[s], i * MOVES + 2 * MOVES)
                    eng.wait_ge(saved[s], i * MOVES + MOVES)
                    ring = mcv(s, "ring").rearrange("p (t r c) -> p t r c", t=CHUNK, c=CELL)
                    at = (i * SLOTS + s) * STEPS
                    eng.wait_ge(step_done, at + 1)
                    eng.tensor_copy(states[:, s, 0, :], states[:, 1 - s, CHUNK, :]).then_inc(step_done, 1)
                    for k in range(CHUNK):
                        eng.wait_ge(step_done, at + (2 * k + 2))
                        eng.tensor_tensor(ring[0:chains, k, :, 1:CELL], ring[0:chains, k, :, 1:CELL],
                                          each(states[:, s, k, :], SCAN_M), ALU.mult).then_inc(step_done, 1)
                        eng.wait_ge(step_done, at + (2 * k + 3))
                        eng.tensor_reduce(states[:, s, k + 1, :], ring[0:chains, k, :, :], AX.X, ALU.add).then_inc(step_done, 1)
                    eng.wait_ge(step_done, at + STEPS + 1)
                    eng.sem_inc(chunk_done, 1)

                for s in range(SLOTS):
                    less_max(0, s)
                    sums(0, s)
                with eng.Fori(0, SCAN_TURNS - 1) as i:
                    for s in range(SLOTS):
                        less_max(i + 1, s)
                        scan(i, s)
                        sums(i + 1, s)
                for s in range(SLOTS):
                    scan(SCAN_TURNS - 1, s)
                eng.wait_ge(y_moved, 16 * B)
                eng.sem_inc(slot_free, B * TILES)

            def scalar(self, eng, run, base):
                eng.wait_ge(slot_free, base + SLOTS)
                with eng.Fori(0, SCAN_TURNS) as i:
                    for s in range(SLOTS):
                        gates_wait(eng, i, "logits", s, 1)
                        eng.activation(mcv(s, "in").rearrange("p (b t) -> p b t", b=B), feedT[:, :, bass.ds((i * SLOTS + s) * CHUNK, CHUNK)],
                                       ACT.Copy).then_inc(gates_scalar, 1)
                        gates_wait(eng, i, "logits", s)
                        gates_wait(eng, i, "gv", s, 1)
                        eng.activation(mcv(s, "v"), P[:, 5, 0:128], ACT.Copy).then_inc(gates_scalar, 1)
                        gates_wait(eng, i, "less", s)
                        eng.activation(mcv(s, "e"), mcv(s, "e"), ACT.Exp).then_inc(gates_scalar, 1)

            def pool(self, eng, run, base):
                with eng.Fori(0, SCAN_TURNS) as i:
                    for s in range(SLOTS):
                        gates_wait(eng, i, "rz", s)
                        eng.tensor_tensor(heads(mcv(s, "e"), ROWS), heads(mcv(s, "e"), ROWS), over(mcv(s, "rz"), ROWS, CELL), ALU.mult)\
                            .then_inc(gates_pool, 1)
                        gates_wait(eng, i, "g", s)
                        first = heads(mcv(s, "e"), ROWS)[:, :, 0:1]
                        eng.tensor_tensor(first, first, mcv(s, "v").unsqueeze(2), ALU.mult).then_inc(gates_pool, 1)

            def sync(self, eng, run, base):
                eng.wait_ge(slot_free, base + SLOTS)
                for s in range(SLOTS):
                    eng.sem_inc(saved[s], MOVES)
                    eng.sem_inc(moved[s], MOVES)
                    eng.sem_inc(moved_out[s], MOVES)

                def save(c, s):
                    for b in range(B):
                        eng.dma_start(mixed[b, bass.ds(c * CHUNK, CHUNK), :, :].rearrange("t h m -> h t m"),
                                      states[SCAN_H * b:SCAN_H * b + SCAN_H, s, 1:CHUNK + 1, :]).then_inc(saved[s], 16)

                def body(i, first):
                    for s in range(SLOTS):
                        gates_wait(eng, i, "gv", s)
                        eng.sem_inc(saving, 1)
                        eng.wait_ge(moved[s], i * MOVES + MOVES)
                        for b in range(B):
                            eng.dma_start(gates_dram[s, b].rearrange("h t e -> t h e"),
                                          mcv(s, "e")[CHUNK * b:CHUNK * b + CHUNK, :].rearrange("t (h e) -> t h e", h=SCAN_H)).then_inc(moved_out[s], 16)
                        eng.wait_ge(chunk_done, i * SLOTS + (s + 1))
                        eng.sem_inc(saving, 1)
                        if not first:
                            save(i * SLOTS + (s - SLOTS), s)
                        eng.wait_ge(moved_out[s], i * MOVES + 2 * MOVES)
                        for b in range(B):
                            eng.dma_start(mcv(s, "ring")[SCAN_H * b:SCAN_H * b + SCAN_H, :].rearrange("h (t e) -> h t e", t=CHUNK),
                                          gates_dram[s, b]).then_inc(moved[s], 16)

                body(0, True)
                with eng.Fori(1, SCAN_TURNS) as i:
                    body(i, False)
                for s in range(SLOTS):
                    eng.wait_ge(chunk_done, CHUNKS + s + 1)
                    save(CHUNKS - SLOTS + s, s)

            def tensor(self, eng, run, base):
                eng.wait_ge(slot_free, base + SLOTS)
                with eng.Fori(0, SCAN_TURNS) as i:
                    for s in range(SLOTS):
                        gates_wait(eng, i, "in", s)
                        gates_wait(eng, i, "less", 1 - s, 1 - s)
                        gates_wait(eng, i, "v", 1 - s, 1 - s)
                        for n, (lo, k) in enumerate(BANKED):
                            eng.matmul(P[:, n, 0:CELL * k], mcv(s, "in"), gwa[:, CELL * lo:CELL * (lo + k)], start=True, stop=True)
                        eng.matmul(P[:, 5, 0:128], mcv(s, "in"), gwv[:, :], start=True, stop=True).then_inc(gates_tensor, 1)

        ov = steps("mix_vector", ["in"])
        oa = steps("mix_scalar", ["T"])
        ot = steps("mix_tensor", ["T", "y"])
        ocv = carve([("in", 128), ("T", 128)])

        class Mix:
            def vector(self, eng, run, base):
                def body(i):
                    wait_slots(eng, base, i)
                    for s in range(SLOTS):
                        eng.tensor_scalar(ocv(s, "in"), hs[:, bass.ds(i.tile(s), 1), :], 1.0, None, ALU.mult).then_inc(ov.tick("in", s), 1)
                    for s in range(SLOTS):
                        eng.wait_ge(ot.sem, ot.value(run, i, "y", s))
                        eng.tensor_tensor(xb(i, s), xb(i, s), bank(s, 1)[:, 0:128], ALU.add).then_inc(slot_free, 1)
                turn_loop(eng, body)

            def scalar(self, eng, run, base):
                def body(i):
                    for s in range(SLOTS):
                        eng.wait_ge(ot.sem, ot.value(run, i, "T", s))
                        eng.activation(ocv(s, "T"), bank(s, 0)[:, 0:128], ACT.Copy).then_inc(oa.tick("T", s), 1)
                turn_loop(eng, body)

            def pool(self, eng, run, base):
                pass

            def tensor(self, eng, run, base):
                def body(i):
                    wait_slots(eng, base, i)
                    for s in range(SLOTS):
                        eng.wait_ge(ov.sem, ov.value(run, i, "in", s))
                        eng.transpose(bank(s, 0)[:, 0:128], ocv(s, "in"), eye).then_inc(ot.tick("T", s), 1)
                    for s in range(SLOTS):
                        eng.wait_ge(oa.sem, oa.value(run, i, "T", s))
                        eng.matmul(bank(s, 1)[:, 0:128], ocv(s, "T"), gwo[:, :], start=True, stop=True).then_inc(ot.tick("y", s), 1)
                turn_loop(eng, body)

        ffn0 = lambda n: [(Feed("window"), n), (Window(0), 2 * n), (Feed("glu", 0), 2 * n), (Glu(0, False), n),
                          (Feed("again"), n), (Window(1), 2 * n + 1), (Feed("glu", 1), 2 * n + 1), (Glu(1, True), n)]
        program = [
            (Feed("plain"), 0), (Delta(), 0),
            *ffn0(0),
            (Feed("plain"), 1), (State(), 0),
            *ffn0(1),
            (Feed("plain"), 2), (Causal(), 0),
            (Feed("routed"), 0), (Routed(), 0),
            (Feed("gates"), 0), (Scan(), 0), (Mix(), 0),
            (Feed("routed"), 1), (Routed(), 1),
        ]

        loads = {
            "x": [(x[:, TILES * b:TILES * b + TILES, :], t["x"][b].rearrange("(j t) d -> t j d", t=T)) for b in range(B)],
            "tables": [(masks[:, :, :], t["masks"]), (window_mask[:, :, :], t["window_mask"]), (causal_mask[:, :], t["causal_mask"]), (eye_bf16[:, :], t["eye_bf16"]),
                       (before[:, :], t["before"]), (turnt[:, 0, :, :, :], t["rope"]), (turnt[:, 1, :, :, :], t["rope"]), (pick[:, :, :], t["pick"]),
                       (keep[:, :], t["keep"])],
            "delta": [(dw[:, :], t["delta_w"]), (dwo[:, :], t["L0_attn_a_Wo"])]
            + [(dg[32 * h:32 * h + 32, :], t["L0_attn_a_g_norm"].unsqueeze(1)) for h in range(4)],
            "window": [(wqkv[:, :, :], t["L0_ffn_wqkv"].rearrange("l d n -> d l n")),
                       (wwo[:, :, :, :], t["L0_ffn_wo"].rearrange("l (c p) n -> p l c n", c=4)),
                       (w1[:, :, :], t["L0_ffn_w1"].rearrange("l d n -> d l n")),
                       (lgb[:, :, 0], t["L0_ffn_ln_g"].rearrange("l d -> d l")), (lgb[:, :, 1], t["L0_ffn_ln_b"].rearrange("l d -> d l"))]
            + [(w2[0:n, l, c, :], t["L0_ffn_w2"][l, lo:lo + n, :]) for l in range(DEPTH) for c, (lo, n) in enumerate(GPART)]
            + [(w2[HID - 256:HID - 255, l, 2, :], t["L0_ffn_b2"][l:l + 1, :]) for l in range(DEPTH)]
            + [(w1b[0:n, l, 3 * half + c:3 * half + c + 1], t["L0_ffn_b1"][l, HID * half + lo:HID * half + lo + n].unsqueeze(1))
               for l in range(DEPTH) for half in range(2) for c, (lo, n) in enumerate(GPART)]
            + [(qk_scale[:, l, 2 * w, :], t[nm][l, :].partition_broadcast(128)) for l in range(DEPTH) for w, nm in enumerate(("L0_ffn_q_scale", "L0_ffn_k_scale"))]
            + [(qk_scale[:, l, 2 * w + 1, 32 * h:32 * h + 32], t[nm][l, 32 - 32 * h:64 - 32 * h].partition_broadcast(128))
               for l in range(DEPTH) for w, nm in enumerate(("L0_ffn_q_scale", "L0_ffn_k_scale")) for h in range(2)],
            "state": [(sB[:, :, :], t["state_b"]), (sC[:, :, :], t["state_c"]), (sD[:, :], t["L0_attn_b_D"].unsqueeze(1)), (sWo[:, :], t["state_wo"]),
                      (sbo[:, :], t["L0_attn_b_b_out"].unsqueeze(0)), (sp_[:, 1:2], t["L0_attn_b_log_dt"].partition_broadcast(128))]
            + [(sp_[64 * h:64 * h + 64, c:c + 1], t[nm].unsqueeze(1)) for h in range(2) for c, nm in ((0, "L0_attn_b_log_Lam_real"), (2, "L0_attn_b_Lam_imag"))],
            "causal": [(cqk[:, :, :, :], t["causal_qk"]), (cv[:, :], t["causal_v"]), (cwo[:, :], t["causal_wo"])],
            "ffn": [(fw1[:, :], t["routed_w1"]), (fb1[:, 0:4], t["L1_ffn_b1_h"].rearrange("(c p) -> p c", c=4)), (fb1[0:64, 4:5], t["L1_ffn_b1_l"].unsqueeze(1)),
                    (fw2[:, 0:4, :], t["routed_w2h"].rearrange("(c p) n -> p c n", c=4)), (fw2[0:64, 4, :], t["routed_w2l"]),
                    (fb2[:, :], t["L1_ffn_b2_h"].unsqueeze(0)), (fw2[64:65, 4, :], t["L1_ffn_b2_l"].unsqueeze(0)),
                    (token[:, :], t["L1_ffn_routing_token"].partition_broadcast(128)),
                    (fgam[:, 0:1], t["L1_ffn_gamma_h"].unsqueeze(1)), (fgam[:, 1:2], t["L1_ffn_gamma_l"].unsqueeze(1))],
            "gates": [(gwn[:, :], t["L1_attn_b_norm_w"].unsqueeze(1)), (gwv[:, :], t["gates_v"]), (gwa[:, :], t["gates_a"]), (gwo[:, :], t["gates_wo"])],
        }
        total = {k: 16 * len(v) for k, v in loads.items()}

        block = ctx.enter_context(nc.Block())

        FIRST = ("x", "tables", "delta")
        FIRST_STAGES = 2

        def bases():
            base = 0
            for stage, run in program:
                yield stage, run, base
                base += B * TILES

        @block.sync
        def _(eng):
            for key in ("x", "tables", "delta", "window", "state"):
                for dst, src in loads[key]:
                    eng.dma_start(dst, src).then_inc(loaded[key], 16)
            for stage, run, base in bases():
                if isinstance(stage, Scan):
                    stage.sync(eng, run, base)
                    for s in range(SLOTS):
                        eng.wait_ge(saved[s], MOVES * (SCAN_TURNS + 1))
                    for b in range(B):
                        eng.dma_start(hs[:, TILES * b:TILES * b + TILES, :], mixed[b].rearrange("(j t) h m -> t j (h m)", t=T)).then_inc(y_moved, 16)
            eng.wait_ge(slot_free, B * TILES * len(program) + SLOTS)
            for b in range(B):
                eng.dma_start(out[b].rearrange("(j t) d -> t j d", t=T), x[:, TILES * b:TILES * b + TILES, :]).then_inc(stored, 16)
            eng.wait_ge(stored, 16 * B)

        @block.gpsimd
        def _(eng):
            for key in ("causal", "ffn", "gates"):
                for dst, src in loads[key]:
                    eng.dma_start(dst, src).then_inc(loaded[key], 16)
            for s in range(SLOTS):
                for name in ("kT", "v"):
                    eng.memset(wcv(s, name), 0.0)
            eng.memset(zero[:, :], 0.0)
            eng.memset(minus_half[:, :], -0.5)
            for s in range(SLOTS):
                eng.memset(stat(s, 25), 0.0)
            eng.memset(delta_state[:, :, :], 0.0).then_inc(cleared, 1)
            eng.wait_ge(cleared, 1)
            for stage, run, base in bases():
                stage.pool(eng, run, base)

        @block.scalar
        def _(eng):
            for n, (stage, run, base) in enumerate(bases()):
                if n == FIRST_STAGES:
                    eng.wait_ge(theta_ready, 1)
                    eng.activation(turns[:, 1, 1:2], sm[:, 12:13], ACT.Sin)
                    eng.activation(turns[:, 0, 1:2], sm[:, 13:14], ACT.Sin).then_inc(tables_act, 1)
                stage.scalar(eng, run, base)

        @block.tensor
        def _(eng):
            for k in FIRST:
                eng.wait_ge(loaded[k], total[k])
            eng.wait_ge(prep, 1)
            for n, (stage, run, base) in enumerate(bases()):
                if n == FIRST_STAGES:
                    for k in loads:
                        eng.wait_ge(loaded[k], total[k])
                    eng.wait_ge(prep, 2)
                stage.tensor(eng, run, base)

        @block.vector
        def _(eng):
            eng.memset(ones_row[:, :], 1.0)
            for k in FIRST:
                eng.wait_ge(loaded[k], total[k])
            eng.tensor_scalar(dwo[:, :], dwo[:, :], dg[:, 0:1], None, ALU.mult).then_inc(prep, 1)
            eng.wait_ge(cleared, 1)
            for _ in range(SLOTS):
                eng.sem_inc(slot_free, 1)
            order = list(bases())
            for stage, run, base in order[:FIRST_STAGES]:
                stage.vector(eng, run, base)
            for k in loads:
                eng.wait_ge(loaded[k], total[k])
            for l in range(DEPTH):
                for j in range(TILES):
                    eng.tensor_tensor(turnt[:, l, j, :, :], turnt[:, l, j, :, :], qk_scale[:, l, :, :], ALU.mult)
            eng.tensor_scalar(fw1[:, 0:HEAVY], fw1[:, 0:HEAVY], fgam[:, 0:1], float(D) ** 0.5, ALU.mult, ALU.mult)
            eng.tensor_scalar(fw1[:, HEAVY:], fw1[:, HEAVY:], fgam[:, 1:2], float(D) ** 0.5, ALU.mult, ALU.mult)
            eng.tensor_scalar(gwa[:, :], gwa[:, :], gwn[:, 0:1], None, ALU.mult)
            eng.tensor_scalar(gwv[:, :], gwv[:, :], gwn[:, 0:1], None, ALU.mult)
            eng.tensor_scalar(sB[:, 1, STATES:], sB[:, 1, STATES:], -1.0, None, ALU.mult)
            eng.tensor_scalar(sC[64:128, 0, :], sC[64:128, 0, :], -1.0, None, ALU.mult)
            eng.tensor_scalar(sC[:, 1, :], sC[:, 1, :], -1.0, None, ALU.mult)
            n = [0]

            def chain(ins):
                n[0] += 1
                ins.then_inc(tables, 1)
                eng.wait_ge(tables, n[0])

            def exp(dst, src, a, b, c, w):
                chain(eng.tensor_scalar(b, src, 87.0, -87.0, ALU.min, ALU.max))
                chain(eng.tensor_scalar(a, b, 1.4426950408889634, 12582912.0, ALU.mult, ALU.add))
                chain(eng.tensor_scalar(a, a, 12582912.0, None, ALU.subtract))
                chain(eng.scalar_tensor_tensor(out=b, in0=a, scalar=-0.693359375, in1=b, op0=ALU.mult, op1=ALU.add))
                chain(eng.scalar_tensor_tensor(out=b, in0=a, scalar=2.12194440e-4, in1=b, op0=ALU.mult, op1=ALU.add))
                chain(eng.tensor_scalar(c, b, 1.0 / 5040, 1.0 / 720, ALU.mult, ALU.add))
                for f in (120.0, 24.0, 6.0, 2.0, 1.0, 1.0):
                    chain(eng.tensor_tensor(c, c, b, ALU.mult))
                    chain(eng.tensor_scalar(c, c, 1.0 / f, None, ALU.add))
                chain(eng.tensor_scalar(a, a, 127.0, 8388608.0, ALU.add, ALU.mult))
                chain(eng.tensor_copy(smi[:, 0:w], a))
                chain(eng.tensor_tensor(dst, c, smi[:, 0:w].bitcast(F32), ALU.mult))

            exp(sm[:, 0:2], sp_[:, 0:2], sm[:, 2:4], sm[:, 4:6], sm[:, 6:8], 2)
            chain(eng.scalar_tensor_tensor(out=sm[:, 8:9], in0=sm[:, 0:1], scalar=-1.0, in1=sm[:, 1:2], op0=ALU.mult, op1=ALU.mult))
            exp(sm[:, 9:10], sm[:, 8:9], sm[:, 2:3], sm[:, 4:5], sm[:, 6:7], 1)
            eng.tensor_scalar(sB[:, :, :], sB[:, :, :], sm[:, 1:2], None, ALU.mult)
            chain(eng.memset(decay[:, :], 1.0))
            chain(eng.tensor_scalar(decay[:, :], decay[:, :], sm[:, 9:10], None, ALU.mult))
            chain(eng.memset(decay[:, 0:1], 0.0))
            chain(eng.tensor_tensor(sm[:, 10:11], sp_[:, 2:3], sm[:, 1:2], ALU.mult))
            chain(eng.tensor_scalar(sm[:, 11:12], sm[:, 10:11], float(1 / (2 * np.pi)), 12582912.0, ALU.mult, ALU.add))
            chain(eng.tensor_scalar(sm[:, 11:12], sm[:, 11:12], 12582912.0, None, ALU.subtract))
            two_pi = 2 * np.pi
            c1 = np.floor(two_pi * 2 ** 8) / 2 ** 8
            c2 = np.floor((two_pi - c1) * 2 ** 20) / 2 ** 20
            for part in (c1, c2, two_pi - c1 - c2):
                chain(eng.scalar_tensor_tensor(out=sm[:, 10:11], in0=sm[:, 11:12], scalar=float(-part), in1=sm[:, 10:11], op0=ALU.mult, op1=ALU.add))
            chain(eng.tensor_scalar(sm[:, 12:13], sm[:, 10:11], 3.1415925, -3.1415925, ALU.min, ALU.max))
            chain(eng.tensor_scalar(sm[:, 14:15], sm[:, 12:13], -1.0, None, ALU.mult))
            chain(eng.tensor_tensor(sm[:, 13:14], sm[:, 14:15], sm[:, 12:13], ALU.min))
            eng.tensor_scalar(sm[:, 13:14], sm[:, 13:14], float(np.pi / 2), None, ALU.add).then_inc(theta_ready, 1)
            eng.wait_ge(tables_act, 1)
            scr = lambda n, w: arena[:, 0, 8192 + 256 * n:8192 + 256 * n + w]
            L = 1
            while L < N:
                m_ = min(L, N - L)
                cL, sL = turns[:, 0, L:L + 1], turns[:, 1, L:L + 1]
                lo = lambda w: turns[:, w, 1:1 + m_]
                chain(eng.tensor_scalar(scr(0, m_), lo(1), sL, None, ALU.mult))
                chain(eng.tensor_scalar(scr(1, m_), lo(1), cL, None, ALU.mult))
                chain(eng.scalar_tensor_tensor(out=turns[:, 0, L + 1:L + 1 + m_], in0=lo(0), scalar=cL, in1=scr(0, m_), op0=ALU.mult, op1=ALU.subtract))
                chain(eng.scalar_tensor_tensor(out=turns[:, 1, L + 1:L + 1 + m_], in0=lo(0), scalar=sL, in1=scr(1, m_), op0=ALU.mult, op1=ALU.add))
                L += m_
            eng.memset(stat(0, 250), 0.0).then_inc(prep, 1)
            eng.wait_ge(prep, 2)
            for stage, run, base in order[FIRST_STAGES:]:
                stage.vector(eng, run, base)


def kernel(**inputs):
    import concourse.bacc as bacc
    from concourse.bass_utils import run_bass_kernel_spmd

    a = {k: np.ascontiguousarray(v) for k, v in inputs.items()}
    host = dict(constants())
    host["x"] = a["L0_attn_a_x"]
    host["delta_w"] = np.concatenate([a["L0_attn_a_Wq"], a["L0_attn_a_Wk"], a["L0_attn_a_Wv"], a["L0_attn_a_Wbeta"]], axis=1)
    br, bi, cr, ci = (a[f"L0_attn_b_{k}"].T for k in ("B_real", "B_imag", "C_real", "C_imag"))
    host["state_b"] = np.stack([np.concatenate([br, bi], 1), np.concatenate([bi, br], 1)], axis=1)
    host["state_c"] = np.stack([np.concatenate([cr, ci], 0), np.concatenate([ci, cr], 0)], axis=1)
    host["state_wo"] = a["L0_attn_b_W_out"].T
    spread = np.zeros((D, 2, CAUSAL_H, 32), np.float32)
    for n, w in enumerate((a["L1_attn_a_Wq"], a["L1_attn_a_Wk"])):
        spread[:, n, :, :CAUSAL_D] = w.T.reshape(D, CAUSAL_H, CAUSAL_D)
    host["causal_qk"] = spread.reshape(D, 2, 4, 128)
    host["causal_v"], host["causal_wo"] = a["L1_attn_a_Wv"].T, a["L1_attn_a_Wo"].T
    host["routed_w1"] = np.concatenate([a["L1_ffn_w1_h"].T, a["L1_ffn_w1_l"].T, np.zeros((D, 128 - LIGHT), np.float32)], axis=1)
    host["routed_w2h"], host["routed_w2l"] = a["L1_ffn_w2_h"].T, a["L1_ffn_w2_l"].T
    host["gates_v"], host["gates_a"], host["gates_wo"] = a["L1_attn_b_W_v"].T, a["L1_attn_b_W_a"].T, a["L1_attn_b_W_out"].T
    for k in ("L0_attn_a_Wo", "L0_attn_a_g_norm", "L0_ffn_wqkv", "L0_ffn_wo", "L0_ffn_w1", "L0_ffn_ln_g", "L0_ffn_ln_b", "L0_ffn_w2", "L0_ffn_b2",
              "L0_ffn_b1", "L0_ffn_q_scale", "L0_ffn_k_scale", "L0_attn_b_D", "L0_attn_b_b_out", "L0_attn_b_log_dt", "L0_attn_b_log_Lam_real",
              "L0_attn_b_Lam_imag", "L1_ffn_routing_token", "L1_ffn_b1_h", "L1_ffn_b1_l", "L1_ffn_b2_h", "L1_ffn_b2_l", "L1_ffn_gamma_h", "L1_ffn_gamma_l", "L1_attn_b_norm_w"):
        host[k] = a[k]

    nc = bacc.Bacc("TRN2", target_bir_lowering=False, num_devices=1)
    arrays, aps = {}, {}
    for k, v in host.items():
        v = np.ascontiguousarray(v)
        arrays[f"in_{k}"] = v
        aps[k] = nc.dram_tensor(f"in_{k}", v.shape, mybir.dt.from_np(v.dtype), kind="ExternalInput").ap()
    out = nc.dram_tensor("out_0", (B, N, D), F32, kind="ExternalOutput").ap()
    hybrid_layers(nc, aps, out)
    result = run_bass_kernel_spmd(nc, [arrays], core_ids=[0])
    return result.results[0]["out_0"]
```
